# Optimizing a Trainium2 kernel written in Bass

```python
import numpy as np
import jax
import jax.numpy as jnp

def _softmax(x, axis=-1):
    return jax.nn.softmax(x, axis=axis)

def _gelu(x):
    return jax.nn.gelu(x, approximate=True)

def _silu(x):
    return jax.nn.silu(x)

def _sigmoid(x):
    return jax.nn.sigmoid(x)

def _layernorm(x, axis=-1, eps=1e-05):
    m = jnp.mean(x, axis=axis, keepdims=True)
    v = jnp.var(x, axis=axis, keepdims=True)
    return (x - m) / jnp.sqrt(v + eps)

def _scatter_add(tgt, idx, src, axis=0):
    return tgt.at[idx].add(src)

def _segment_sum(src, seg, n):
    return jax.ops.segment_sum(src, seg, n)
kernel_name = 'mk_macaron_d1_jaxref_r8_9079c4'

def setup_inputs(seed: int=0):
    np.random.seed(seed)
    _w = jnp.asarray

    def _L0_attn_setup():
        import jax, jax.numpy as jnp
        import numpy as np
        D_MODEL = 128
        N_HEADS = 16
        HEAD_DIM = D_MODEL // N_HEADS
        ROPE_BASE = 10000.0

        def rotate_half(x):
            d = x.shape[-1]
            x1, x2 = (x[..., :d // 2], x[..., d // 2:])
            return jnp.concatenate((-x2, x1), axis=-1)

        def rope_cos_sin(T, dim, dtype):
            inv_freq = 1.0 / ROPE_BASE ** (jnp.arange(0, dim, 2, dtype=jnp.float32) / dim)
            t = jnp.arange(T, dtype=jnp.float32)
            freqs = jnp.einsum('i,j->ij', t, inv_freq)
            emb = jnp.concatenate((freqs, freqs), axis=-1)
            return (jnp.cos(emb).astype(dtype), jnp.sin(emb).astype(dtype))
        key = jax.random.key(seed)
        ks = jax.random.split(key, 9)
        s = 0.02
        return {'x': jax.random.normal(ks[0], (4, 256, D_MODEL), dtype=jnp.float32), 'Wq': jax.random.normal(ks[1], (D_MODEL, D_MODEL), dtype=jnp.float32) * s, 'bq': jax.random.normal(ks[2], (D_MODEL,), dtype=jnp.float32) * s, 'Wk': jax.random.normal(ks[3], (D_MODEL, D_MODEL), dtype=jnp.float32) * s, 'bk': jax.random.normal(ks[4], (D_MODEL,), dtype=jnp.float32) * s, 'Wv': jax.random.normal(ks[5], (D_MODEL, D_MODEL), dtype=jnp.float32) * s, 'bv': jax.random.normal(ks[6], (D_MODEL,), dtype=jnp.float32) * s, 'Wo': jax.random.normal(ks[7], (D_MODEL, D_MODEL), dtype=jnp.float32) * s, 'bo': jax.random.normal(ks[8], (D_MODEL,), dtype=jnp.float32) * s}
    _L0_attn_in = _L0_attn_setup()

    def _L0_ffn_setup():
        import jax, jax.numpy as jnp
        import numpy as np
        B, S, D, H, F = (4, 512, 128, 16, 512)
        CAP = 0.125
        ROPE_BASE = 10000.0

        def rmsnorm(x, g):
            return x * jax.lax.rsqrt(jnp.mean(x * x, -1, keepdims=True) + 1e-06) * g

        def rope(t, pos):
            hd = t.shape[-1]
            inv = 1.0 / ROPE_BASE ** (jnp.arange(0, hd, 2, dtype=jnp.float32) / hd)
            f = pos[:, None, :, None].astype(jnp.float32) * inv
            emb = jnp.concatenate([f, f], axis=-1)
            cos, sin = (jnp.cos(emb), jnp.sin(emb))
            rot = jnp.concatenate([-t[..., hd // 2:], t[..., :hd // 2]], axis=-1)
            return t * cos + rot * sin
        key = jax.random.key(seed)
        ks = jax.random.split(key, 9)
        scale = 0.02
        x = jax.random.normal(ks[0], (B, S, D), jnp.float32)
        causal = jnp.where(jnp.tril(jnp.ones((S, S), bool)), 0.0, -1000000000.0).astype(jnp.float32)
        attention_mask = jnp.broadcast_to(causal[None, None], (B, 1, S, S))
        position_ids = jnp.broadcast_to(jnp.arange(S, dtype=jnp.int32), (B, S))
        return {'x': x, 'attention_mask': attention_mask, 'position_ids': position_ids, 'router_w': jax.random.normal(ks[1], (D, 1), jnp.float32) * scale, 'router_b': jnp.zeros((1,), jnp.float32), 'wq': jax.random.normal(ks[2], (D, D), jnp.float32) * scale, 'wk': jax.random.normal(ks[3], (D, D), jnp.float32) * scale, 'wv': jax.random.normal(ks[4], (D, D), jnp.float32) * scale, 'wo': jax.random.normal(ks[5], (D, D), jnp.float32) * scale, 'w1': jax.random.normal(ks[6], (D, F), jnp.float32) * scale, 'w2': jax.random.normal(ks[7], (F, D), jnp.float32) * scale, 'ln1': jnp.ones((D,), jnp.float32), 'ln2': jnp.ones((D,), jnp.float32)}
    _L0_ffn_in = _L0_ffn_setup()
    _d = {'L0_attn_x': _L0_attn_in['x'], 'L0_attn_Wq': _L0_attn_in['Wq'], 'L0_attn_bq': _L0_attn_in['bq'], 'L0_attn_Wk': _L0_attn_in['Wk'], 'L0_attn_bk': _L0_attn_in['bk'], 'L0_attn_Wv': _L0_attn_in['Wv'], 'L0_attn_bv': _L0_attn_in['bv'], 'L0_attn_Wo': _L0_attn_in['Wo'], 'L0_attn_bo': _L0_attn_in['bo'], 'L0_ffn_attention_mask': _L0_ffn_in['attention_mask'], 'L0_ffn_position_ids': _L0_ffn_in['position_ids'], 'L0_ffn_router_w': _L0_ffn_in['router_w'], 'L0_ffn_router_b': _L0_ffn_in['router_b'], 'L0_ffn_wq': _L0_ffn_in['wq'], 'L0_ffn_wk': _L0_ffn_in['wk'], 'L0_ffn_wv': _L0_ffn_in['wv'], 'L0_ffn_wo': _L0_ffn_in['wo'], 'L0_ffn_w1': _L0_ffn_in['w1'], 'L0_ffn_w2': _L0_ffn_in['w2'], 'L0_ffn_ln1': _L0_ffn_in['ln1'], 'L0_ffn_ln2': _L0_ffn_in['ln2']}
    _x0 = _d['L0_attn_x']
    _d['L0_attn_x'] = jax.random.normal(jax.random.fold_in(jax.random.key(seed), 1), (2, 1024, 128), dtype=_x0.dtype)
    del _x0
    return _d

def reference(L0_attn_x, L0_attn_Wq, L0_attn_bq, L0_attn_Wk, L0_attn_bk, L0_attn_Wv, L0_attn_bv, L0_attn_Wo, L0_attn_bo, L0_ffn_attention_mask, L0_ffn_position_ids, L0_ffn_router_w, L0_ffn_router_b, L0_ffn_wq, L0_ffn_wk, L0_ffn_wv, L0_ffn_wo, L0_ffn_w1, L0_ffn_w2, L0_ffn_ln1, L0_ffn_ln2):

    def _L0_attn_ref(x, Wq, bq, Wk, bk, Wv, bv, Wo, bo):
        import jax, jax.numpy as jnp
        import numpy as np
        D_MODEL = 128
        N_HEADS = 16
        HEAD_DIM = D_MODEL // N_HEADS
        ROPE_BASE = 10000.0

        def rotate_half(x):
            d = x.shape[-1]
            x1, x2 = (x[..., :d // 2], x[..., d // 2:])
            return jnp.concatenate((-x2, x1), axis=-1)

        def rope_cos_sin(T, dim, dtype):
            inv_freq = 1.0 / ROPE_BASE ** (jnp.arange(0, dim, 2, dtype=jnp.float32) / dim)
            t = jnp.arange(T, dtype=jnp.float32)
            freqs = jnp.einsum('i,j->ij', t, inv_freq)
            emb = jnp.concatenate((freqs, freqs), axis=-1)
            return (jnp.cos(emb).astype(dtype), jnp.sin(emb).astype(dtype))
        B, T, D = x.shape
        H, hd = (N_HEADS, HEAD_DIM)

        def proj(W, b):
            y = jnp.einsum('btd,ed->bte', x, W) + b
            return y.reshape(B, T, H, hd).transpose(0, 2, 1, 3)
        q = proj(Wq, bq)
        k = proj(Wk, bk)
        v = proj(Wv, bv)
        cos, sin = rope_cos_sin(T, hd, x.dtype)
        q = q * cos + rotate_half(q) * sin
        k = k * cos + rotate_half(k) * sin
        scores = jnp.einsum('bhqd,bhkd->bhqk', q, k) / jnp.sqrt(jnp.asarray(hd, x.dtype))
        causal = jnp.tril(jnp.ones((T, T), dtype=bool))
        scores = jnp.where(causal, scores, jnp.asarray(-jnp.inf, x.dtype))
        attn = jax.nn.softmax(scores, axis=-1)
        out = jnp.einsum('bhqk,bhkd->bhqd', attn, v)
        out = out.transpose(0, 2, 1, 3).reshape(B, T, D)
        return jnp.einsum('btd,ed->bte', out, Wo) + bo

    def _L0_ffn_ref(x, attention_mask, position_ids, router_w, router_b, wq, wk, wv, wo, w1, w2, ln1, ln2):
        import jax, jax.numpy as jnp
        import numpy as np
        B, S, D, H, F = (4, 512, 128, 16, 512)
        CAP = 0.125
        ROPE_BASE = 10000.0

        def rmsnorm(x, g):
            return x * jax.lax.rsqrt(jnp.mean(x * x, -1, keepdims=True) + 1e-06) * g

        def rope(t, pos):
            hd = t.shape[-1]
            inv = 1.0 / ROPE_BASE ** (jnp.arange(0, hd, 2, dtype=jnp.float32) / hd)
            f = pos[:, None, :, None].astype(jnp.float32) * inv
            emb = jnp.concatenate([f, f], axis=-1)
            cos, sin = (jnp.cos(emb), jnp.sin(emb))
            rot = jnp.concatenate([-t[..., hd // 2:], t[..., :hd // 2]], axis=-1)
            return t * cos + rot * sin
        b, s, d = x.shape
        hd = d // H
        weights = (x @ router_w)[..., 0] + router_b[0]
        k = int(CAP * s)
        topv, topi = jax.lax.top_k(weights, k)
        thr = topv[:, -1]
        sel_mask = (weights > thr[:, None]).astype(x.dtype)
        kc = k - 1
        sel_idx = jnp.sort(topi[:, :kc], axis=1)
        bidx = jnp.arange(b)[:, None]
        x_sel = x[bidx, sel_idx]
        pos_sel = position_ids[bidx, sel_idx]
        w_sel = weights[bidx, sel_idx]
        m = attention_mask[:, 0]
        m_sel = m[bidx[:, :, None], sel_idx[:, :, None], sel_idx[:, None, :]]
        hn = rmsnorm(x_sel, ln1)

        def heads(t):
            return t.reshape(b, kc, H, hd).transpose(0, 2, 1, 3)
        q = rope(heads(hn @ wq), pos_sel)
        kk = rope(heads(hn @ wk), pos_sel)
        v = heads(hn @ wv)
        sc = jnp.einsum('bhqd,bhkd->bhqk', q, kk) / np.sqrt(hd).astype(np.float32)
        sc = sc + m_sel[:, None]
        a = jax.nn.softmax(sc, axis=-1)
        o = jnp.einsum('bhqk,bhkd->bhqd', a, v).transpose(0, 2, 1, 3).reshape(b, kc, d) @ wo
        x1 = x_sel + o
        x2 = x1 + jax.nn.gelu(rmsnorm(x1, ln2) @ w1) @ w2
        proc = x2 * w_sel[..., None]
        out = jnp.zeros_like(x).at[bidx, sel_idx].set(proc)
        return out + x * (1.0 - sel_mask)[..., None]
    x = L0_attn_x
    x = x + 0.5 * _L0_ffn_ref(_layernorm(x, axis=-1), L0_ffn_attention_mask, L0_ffn_position_ids, L0_ffn_router_w, L0_ffn_router_b, L0_ffn_wq, L0_ffn_wk, L0_ffn_wv, L0_ffn_wo, L0_ffn_w1, L0_ffn_w2, L0_ffn_ln1, L0_ffn_ln2)
    x = x + _L0_attn_ref(_layernorm(x, axis=-1), L0_attn_Wq, L0_attn_bq, L0_attn_Wk, L0_attn_bk, L0_attn_Wv, L0_attn_bv, L0_attn_Wo, L0_attn_bo)
    x = x + 0.5 * _L0_ffn_ref(_layernorm(x, axis=-1), L0_ffn_attention_mask, L0_ffn_position_ids, L0_ffn_router_w, L0_ffn_router_b, L0_ffn_wq, L0_ffn_wk, L0_ffn_wv, L0_ffn_wo, L0_ffn_w1, L0_ffn_w2, L0_ffn_ln1, L0_ffn_ln2)
    return x

_drawn_inputs = setup_inputs


def setup_inputs(seed=0):
    import zlib

    import numpy as np

    out = dict(_drawn_inputs(seed))
    spreads = {'L0_ffn_ln1': (1.0, 0.6), 'L0_ffn_ln2': (1.0, 0.6)}
    factors = {'L0_attn_Wq': 8.0,
     'L0_attn_bq': 8.0,
     'L0_attn_Wk': 8.0,
     'L0_attn_bk': 8.0,
     'L0_attn_Wv': 8.0,
     'L0_attn_bv': 8.0,
     'L0_attn_Wo': 8.0,
     'L0_attn_bo': 3.815,
     'L0_ffn_wq': 8.0,
     'L0_ffn_wk': 8.0,
     'L0_ffn_wv': 8.0,
     'L0_ffn_wo': 8.0,
     'L0_ffn_w1': 8.0,
     'L0_ffn_w2': 7.532}
    for name, (base, spread) in spreads.items():
        noise = np.random.default_rng([zlib.crc32(name.encode()), seed]).standard_normal(out[name].shape)
        drawn = base * np.exp(spread * noise) if base else spread * noise
        out[name] = jnp.asarray(drawn.astype(out[name].dtype))
    for name, factor in factors.items():
        out[name] = (out[name] * factor).astype(out[name].dtype)
    return out
```

```python
from contextlib import ExitStack

import numpy as np

import concourse.bass as bass
from concourse import mybir

B, T, D, H = 2, 1024, 128, 16
HD = D // H
NB = T // 128
S_MASK = 512
MB = S_MASK // 128
F = 512
FB = F // 128
KEEP = int(0.125 * T) - 1
HALF = HD // 2
SCALE = float(1.0 / np.sqrt(HD))
LN_EPS, RMS_EPS = 1e-5, 1e-6

AUX_COS, AUX_NSIN, AUX_SIN, AUX_W = D, D + HALF, D + 2 * HALF, D + 3 * HALF
XW = AUX_W + 1

HG = 4
GB = H // HG
G = B * GB
PARTS = 3
STACK = PARTS * PARTS * HD
SHIFT = 128 - PARTS
SETS = 3
VW = 32
NEG = -1.0e30

CHUNKS = [[(0, 0, 512)], [(0, 512, 512)], [(1, 128, 384), (3, 384, 128)], [(2, 256, 256), (6, 768, 256)],
          [(1, 512, 512)], [(2, 512, 512)], [(3, 512, 512)], [(4, 512, 512)], [(5, 640, 384), (7, 896, 128)]]
NC = len(CHUNKS)
DIAG = []
for _pieces in CHUNKS:
    _at, _starts = 0, []
    for _kb, _q0, _w in _pieces:
        if _kb * 128 == _q0:
            _starts.append(_at)
        _at += _w
    DIAG.append(_starts)
DIAG_CHUNKS = [c for c in range(NC) if DIAG[c]]
HALF_END = [3, 8]
QORDER = [7, 0, 6, 1, 5, 2, 4, 3]
TILES = HG * NB
USES = TILES + 1
FIRST = TILES // 2


def body_plan(has_next, has_second, has_first):
    tiles = []
    if has_second:
        tiles += [("tile", 1, a) for a in range(FIRST, TILES)] + [("maxt", 1, 0)]
    if has_first:
        tiles += [("tile", 2, a) for a in range(FIRST)]
    plan, done = [], 0
    n_pos = NC * HG if has_first else NC * HG // 2
    for p in range(NC):
        if p < NC - 1 or has_next:
            chunk = (0, p + 1) if p < NC - 1 else (1, 0)
            for j in range(HG):
                if p == NC - 1 and j == 2:
                    plan += [("pv", 0, p), ("evac", 0, 1)]
                plan.append(("st", *chunk, j))
                if p == 4 and j == 0:
                    plan.append(("evac", 0, 0))
                upto = min(len(tiles), (p * HG + j + 1) * len(tiles) // n_pos)
                plan += tiles[done:upto]
                done = upto
        else:
            plan += [("pv", 0, p), ("evac", 0, 1)]
        if p < NC - 1:
            plan.append(("pv", 0, p))
        if p == 5:
            plan.append(("zt", 0, 0))
    plan.append(("zt", 0, 1))
    return plan


def build(nc, x_d, masks_d, pos_d, rw_d, rb_d, fwq_d, fwk_d, fwv_d, fwo_d, fw1_d, fw2_d, ln1_d, ln2_d,
          wqk_d, bqk_d, wv_d, bv_d, wo_d, bo_d, rope_d, invf_d, out_d):
    f32, bf16, i32 = mybir.dt.float32, mybir.dt.bfloat16, mybir.dt.int32
    ACT, ALU, AX = mybir.ActivationFunctionType, mybir.AluOpType, mybir.AxisListType

    ctx = ExitStack()
    with ctx:
        def sb(name, shape, dt=f32):
            return ctx.enter_context(nc.sbuf_tensor(name, shape, dt))

        def sem(name):
            return ctx.enter_context(nc.semaphore(name))

        psum = ctx.enter_context(nc.psum_tensor("psum", [128, 8, 512], f32))

        def bank(n, lo=0, hi=512):
            return psum[:, n, lo:hi]

        ident = sb("ident", [128, 128])
        lower = sb("lower", [128, 128])
        iota_row = sb("iota_row", [128, 128])
        iota_col = sb("iota_col", [128, 1])
        headmask = sb("headmask", [128, H])
        ones_bf = sb("ones_bf", [128, 128], bf16)
        neghalf = sb("neghalf", [128, NB])
        diagmask = sb("diagmask", [128, T], bf16)
        rope_c = sb("rope_c", [128, 2, T])
        invf = sb("invf", [128, HALF])
        rw = sb("rw", [128, D])
        rb = sb("rb", [128, 1])
        fqkv = sb("fqkv", [128, 3 * D])
        fwo = sb("fwo", [128, D])
        fw1 = sb("fw1", [128, F])
        fw2 = sb("fw2", [128, FB, D])
        ln1 = sb("ln1", [128, 1])
        ln2 = sb("ln2", [128, 1])
        wqk = sb("wqk", [128, 4, D])
        bqk = sb("bqk", [128, 4])
        wv = sb("wv", [128, D])
        bv = sb("bv", [128, D])
        wo = sb("wo", [128, D])
        bo = sb("bo", [128, D])
        masks = sb("masks", [128, B, MB + 1, S_MASK + 128])
        pos_i = sb("pos_i", [128, B, MB + 1], i32)
        xa = sb("xa", [128, B * NB, D])
        xb = sb("xb", [128, B * NB, D])
        xn = sb("xn", [128, B * NB, XW])
        base = sb("base", [128, B * NB, D])
        stats = sb("stats", [128, B * NB, 6])
        mv = sb("mv", [128, B * NB, 2])
        veps = sb("veps", [128, B, NB])
        rstd = sb("rstd", [128, B, NB])
        wcol = sb("wcol", [128, B, NB])
        thr = sb("thr", [128, B])
        drop = sb("drop", [128, B, NB])
        rcol = sb("rcol", [128, B, NB])
        scr = sb("scr", [128, T])
        xs = sb("xs", [128, B, XW])
        ssq = sb("ssq", [128, B, 2])
        ms = sb("ms", [128, B, 2])
        rs = sb("rs", [128, B, 2])
        junk_a = sb("junk_a", [128, 2 * B, D])
        nmx = sb("nmx", [128, B, H])
        rsum = sb("rsum", [128, B, H])
        rrec = sb("rrec", [128, B, H])

        NA = B * (MB + 1) * HALF
        posf, ang, turns, red = (sb(n, [128, NA]) for n in ("posf", "ang", "turns", "red"))
        trig = sb("trig", [128, 3, NA])
        red2 = sb("red2", [128, 2, NA])

        ARENA = 28672
        arena = sb("arena", [128, ARENA])
        taken = {"ffn": 0, "att": 0}

        def part(who, shape, dt=f32):
            n = int(np.prod(shape))
            words = n if dt == f32 else n // 2
            at = taken[who]
            taken[who] = at + words
            assert taken[who] <= ARENA, (who, taken)
            ap = arena[:, at:at + words]
            if dt != f32:
                ap = ap.bitcast(dt)
            if len(shape) == 2:
                ap = ap.rearrange("p (a b) -> p a b", a=shape[0])
            if len(shape) == 3:
                ap = ap.rearrange("p (a b c) -> p a b c", a=shape[0], b=shape[1])
            if len(shape) == 4:
                ap = ap.rearrange("p (a b c d) -> p a b c d", a=shape[0], b=shape[1], c=shape[2])
            return ap

        wrow = part("ffn", [B, T])
        rrow = part("ffn", [B, T])
        slots = part("ffn", [B, T])
        slots_t = part("ffn", [B, NB + 1, 128])
        cmp_gt = part("ffn", [NB, T], bf16)
        cmp_eq = part("ffn", [NB, 128], bf16)
        umask = part("ffn", [B, MB + 1, 128])
        ktm = part("ffn", [H, 128])
        sc = part("ffn", [H, 128])
        prob = part("ffn", [H, 128])
        prob_t = part("ffn", [H, 128])
        ra = part("ffn", [2 * H, 2, HALF])
        rbuf = part("ffn", [2 * H, 2, HALF])
        qk = part("ffn", [B, 2 * D])
        vs = part("ffn", [B, D])
        qt = part("ffn", [B, D])
        msel = part("ffn", [B, D])
        osel = part("ffn", [B, D])
        ot = part("ffn", [B, D])
        x1 = part("ffn", [B, D])
        x2 = part("ffn", [B, D])
        proc = part("ffn", [B, D])
        usq = part("ffn", [1, F])[:, 0]
        th = part("ffn", [1, F])[:, 0]
        gel = part("ffn", [B, F])
        hn = part("ffn", [B, D])
        ht = part("ffn", [B, D])

        q_set = part("att", [SETS, HG, T], bf16)
        k_set = part("att", [SETS, HG, T], bf16)
        v_all = part("att", [G, NB * HG * HD])
        v_set = part("att", [SETS, NB, HG, VW])
        p_at = taken["att"]
        p_buf = part("att", [3, HG, 512])
        p_end = taken["att"]
        taken["att"] = p_at
        xnt = part("att", [B, T])
        parts = part("att", [PARTS, T], bf16)
        rq = part("att", [1, T])[:, 0]
        rt = part("att", [1, T])[:, 0]
        assert taken["att"] <= p_end
        taken["att"] = p_at + B * T
        o_tok = part("att", [B, NB, D])
        taken["att"] = p_end
        o_all = part("att", [G, NB * HG * HD])
        z_buf = part("att", [2, 512])
        zrec = part("att", [2, 16])
        mx = part("att", [1, TILES])[:, 0]
        shift = part("att", [PARTS, 128], bf16)
        srem = part("att", [1, 128])[:, 0]
        junk_v = part("att", [2, T], bf16)

        qk_scr = [nc.dram_tensor(f"{n}_parts", (G, PARTS * HD, HG * T), bf16, kind="Internal").ap() for n in ("q", "k")]

        loaded_x, loaded_w = sem("loaded_x"), sem("loaded_w")
        pool_step, vec_step, act_step = sem("pool_step"), sem("vec_step"), sem("act_step")
        consts_ready = sem("consts_ready")
        angles_ready, trig_ready, aux_trig = sem("angles_ready"), sem("trig_ready"), sem("aux_trig")
        mask_wide = sem("mask_wide")
        veps_ready, rstd_ready, xn_ready = sem("veps_ready"), sem("rstd_ready"), sem("xn_ready")
        wcol_ready, aux_w, wrow_ps = sem("wcol_ready"), sem("aux_w"), sem("wrow_ps")
        cmp_ready, rank_ps, rrow_ready = sem("cmp_ready"), sem("rank_ps"), sem("rrow_ready")
        rcol_ps, drop_ready, slots_ready = sem("rcol_ps"), sem("drop_ready"), sem("slots_ready")
        slots_t_ready, clamp_ready, gather_ps = sem("slots_t_ready"), sem("clamp_ready"), sem("gather_ps")
        xs_ready, ssq_ready, ms_ready, rs_ready = sem("xs_ready"), sem("ssq_ready"), sem("ms_ready"), sem("rs_ready")
        hn_ready, ht_ps, ht_ready = sem("hn_ready"), sem("ht_ps"), sem("ht_ready")
        u_ps, u_ready, msel_ps, msel_ready = sem("u_ps"), sem("u_ready"), sem("msel_ps"), sem("msel_ready")
        qkv_ps, qk_ready, vs_ready = sem("qkv_ps"), sem("qk_ready"), sem("vs_ready")
        qkt_ps, qkt_ready = sem("qkt_ps"), sem("qkt_ready")
        sc_ps, sc_taken, mx_ready, exp_ready = sem("sc_ps"), sem("sc_taken"), sem("mx_ready"), sem("exp_ready")
        pt_ps, pt_ready_v, pt_ready_a = sem("pt_ps"), sem("pt_ready_v"), sem("pt_ready_a")
        o_ps, o_ready, ot_ps, ot_ready = sem("o_ps"), sem("o_ready"), sem("ot_ps"), sem("ot_ready")
        x1_ps, x1_ready, hid_ps = sem("x1_ps"), sem("x1_ready"), sem("hid_ps")
        usq_ready, arg_ready, tanh_ready, gel_ready = sem("usq_ready"), sem("arg_ready"), sem("tanh_ready"), sem("gel_ready")
        x2_ps, proc_ready, base_ready = sem("x2_ps"), sem("proc_ready"), sem("base_ready")
        y_ps, y_ready, stored = sem("y_ps"), sem("y_ready"), sem("stored")
        sets_clear, ones_v = sem("sets_clear"), sem("ones_v")
        xnt_ps, xnt_ready = sem("xnt_ps"), sem("xnt_ready")
        proj_ps, rot_ready, hi_ready, rem_ready, mid_ready = (
            sem("proj_ps"), sem("rot_ready"), sem("hi_ready"), sem("rem_ready"), sem("mid_ready"))
        low_ready, parts_stored, v_ps, v_ready = sem("low_ready"), sem("parts_stored"), sem("v_ps"), sem("v_ready")
        set_loaded = [sem(f"set_loaded{i}") for i in range(SETS)]
        shift_loaded = [sem(f"shift_loaded{i}") for i in range(SETS)]
        v_set_ready = sem("v_set_ready")
        tile_ps, tile_taken = sem("tile_ps"), sem("tile_taken")
        tiles_seen, diags_seen = sem("tiles_seen"), sem("diags_seen")
        shift_step, shift_ready = sem("shift_step"), sem("shift_ready")
        st_ps, exp_done, diag_done = sem("st_ps"), sem("exp_done"), sem("diag_done")
        prob_free = sem("prob_free")
        z_ready, zt_ps, zrec_ready = sem("z_ready"), sem("zt_ps"), sem("zrec_ready")
        pv_free = [sem("pv_free0"), sem("pv_free1")]
        o_tok_ready, att_t_ps, att_t_ready, att_ps, att_base = sem("o_tok_ready"), sem("att_t_ps"), sem("att_t_ready"), sem("att_ps"), sem("att_base")

        class Step:

            def __init__(self, eng, s):
                self.eng, self.s, self.n = eng, s, 0

            def __call__(self, ins):
                self.n += 1
                ins.then_inc(self.s, 1)
                self.eng.wait_ge(self.s, self.n)

        def blocks(t, b):
            return t[:, b * NB:(b + 1) * NB]

        W_LOADS = 0
        ffn_tokens = {0: (xa, xb), 1: (xa, xb)}
        block = ctx.enter_context(nc.Block())

        @block.sync
        def _(sp):
            for b in range(B):
                sp.dma_start(blocks(xa, b), x_d[b].rearrange("(n p) d -> p n d", p=128)).then_inc(loaded_x, 16)
            small = [
                (rw[:], rw_d.rearrange("d o -> o d").partition_broadcast(128).rearrange("p o d -> p (o d)")),
                (rb[:], rb_d.partition_broadcast(128)), (invf[:], invf_d.partition_broadcast(128)),
                (bv[:], bv_d.partition_broadcast(128)), (bo[:], bo_d.partition_broadcast(128)),
                (ln1[:], ln1_d.rearrange("(p o) -> p o", o=1)), (ln2[:], ln2_d.rearrange("(p o) -> p o", o=1)),
                (fqkv[:, 0:D], fwq_d), (fqkv[:, D:2 * D], fwk_d), (fqkv[:, 2 * D:], fwv_d), (fwo[:], fwo_d),
                (fw1[:], fw1_d), (fw2[:], fw2_d.rearrange("(n p) d -> p n d", p=128)),
                (wqk[:], wqk_d), (bqk[:], bqk_d), (wv[:], wv_d), (wo[:], wo_d), (rope_c[:], rope_d), (pos_i[:], pos_d),
            ]
            for b in range(B):
                small += [
                    (masks[:, b, 0:MB, 0:S_MASK], masks_d[b, 0].rearrange("(n p) c -> p n c", p=128)),
                    (masks[:, b, MB, 0:S_MASK], masks_d[b, 0, S_MASK - 1].partition_broadcast(128)),
                ]
            assert len(small) == W_COUNT
            for dst, src in small:
                sp.dma_start(dst, src).then_inc(loaded_w, 16)

            def load_set(g):
                s = g % SETS
                for p in range(PARTS):
                    rows = slice(p * PARTS * HD, (p + 1) * PARTS * HD)
                    src = qk_scr[0][g, p * HD:(p + 1) * HD, :]
                    for r in range(PARTS):
                        lo = (p * PARTS + r) * HD
                        sp.dma_start(q_set[lo:lo + HD, s].rearrange("p a b -> p (a b)"), src).then_inc(set_loaded[s], 16)
                    sp.dma_start(k_set[rows, s].rearrange("p a b -> p (a b)"), qk_scr[1][g]).then_inc(set_loaded[s], 16)

            for n in range(2 * B):
                b, which = divmod(n, 2)
                for p in range(PARTS):
                    sp.wait_ge((hi_ready, mid_ready, low_ready)[p], n + 1)
                    sp.dma_start(
                        qk_scr[which][b * GB:(b + 1) * GB, p * HD:(p + 1) * HD, :].rearrange("g d (j t) -> g (d j) t", j=HG),
                        parts[:, p, :]).then_inc(parts_stored, 16)
            sp.wait_ge(parts_stored, 16 * PARTS * 2)
            sp.wait_ge(sets_clear, 2)
            for g in range(SETS):
                load_set(g)
            sp.wait_ge(parts_stored, 16 * PARTS * 2 * B)
            for g in range(G):
                sp.wait_ge(shift_ready, g + 1)
                for r in range(PARTS):
                    sp.dma_start(q_set[SHIFT + r:SHIFT + r + 1, g % SETS].rearrange("p j (i c) -> p (j i) c", c=128),
                                 shift[0:TILES, r, :]).then_inc(shift_loaded[g % SETS], 16)
                if 1 <= g <= G - SETS:
                    sp.wait_ge(st_ps, NC * HG * g)
                    load_set(g - 1 + SETS)
            for b in range(B):
                sp.wait_ge(y_ready, B * 2 + b + 1)
                sp.dma_start(out_d[b].rearrange("(n p) d -> p n d", p=128), blocks(xb, b)).then_inc(stored, 16)
            sp.wait_ge(stored, 16 * B)

        @block.gpsimd
        def _(gp):
            step = Step(gp, pool_step)
            step(nc.gpsimd.memset(lower[:], 1.0))
            step(nc.gpsimd.affine_select(out=lower[:], in_=lower[:], compare_op=ALU.is_gt, fill=0.0, base=0,
                                         pattern=[[1, 128]], channel_multiplier=-1))
            step(nc.gpsimd.memset(ident[:], 0.0))
            step(nc.gpsimd.affine_select(out=ident[:], in_=ident[:], compare_op=ALU.not_equal, fill=1.0, base=0,
                                         pattern=[[1, 128]], channel_multiplier=-1))
            step(nc.gpsimd.memset(diagmask[:], 0.0))
            dm = diagmask[:, T - 128:T]
            step(nc.gpsimd.affine_select(out=dm, in_=dm, compare_op=ALU.is_ge, fill=NEG, base=0,
                                         pattern=[[-1, 128]], channel_multiplier=1))
            step(nc.gpsimd.memset(headmask[:], 1.0))
            step(nc.gpsimd.affine_select(out=headmask[:], in_=headmask[:], compare_op=ALU.is_ge, fill=0.0, base=0,
                                         pattern=[[-HD, H]], channel_multiplier=1))
            step(nc.gpsimd.affine_select(out=headmask[:], in_=headmask[:], compare_op=ALU.is_ge, fill=0.0, base=HD - 1,
                                         pattern=[[HD, H]], channel_multiplier=-1))
            step(nc.gpsimd.iota(iota_row[:], pattern=[[1, 128]], base=0, channel_multiplier=0,
                                allow_small_or_imprecise_dtypes=True))
            step(nc.gpsimd.iota(iota_col[:], pattern=[[0, 1]], base=0, channel_multiplier=1,
                                allow_small_or_imprecise_dtypes=True))
            step(nc.gpsimd.memset(neghalf[:], -0.5))
            nc.gpsimd.memset(ones_bf[:], 1.0).then_inc(consts_ready, 1)

            def root(f, b):
                gp.wait_ge(veps_ready, B * f + b + 1)
                if f == 0 and b == 0:
                    gp.wait_ge(pool_step, step.n)
                nc.gpsimd.tensor_tensor(rstd[:, b], veps[:, b], neghalf[:], ALU.pow).then_inc(rstd_ready, 1)

            def ffn(f):
                xi, _ = ffn_tokens[f]
                for b in range(B):
                    root(2 * f, b)
                if f == 0:
                    gp.wait_ge(loaded_w, 16 * W_COUNT)
                    for b in range(B):
                        nc.gpsimd.tensor_copy(masks[:, b, :, S_MASK:], masks[:, b, :, S_MASK - 1:S_MASK]
                                              .to_broadcast([128, MB + 1, 128])).then_inc(mask_wide, 1)
                for b in range(B):
                    gp.wait_ge(wcol_ready, B * f + b + 1)
                    gp.wait_ge(xn_ready, 2 * B * f + b + 1)
                    nc.gpsimd.tensor_copy(blocks(xn, b)[:, :, AUX_W], wcol[:, b]).then_inc(aux_w, 1)
                for b in range(B):
                    gp.wait_ge(ms_ready, 2 * B * f + b + 1)
                    nc.gpsimd.tensor_tensor(rs[:, b, 0:1], ms[:, b, 0:1], neghalf[:, 0:1], ALU.pow).then_inc(rs_ready, 1)
                for b in range(B):
                    gp.wait_ge(drop_ready, B * f + b + 1)
                    step(nc.gpsimd.tensor_tensor(blocks(base, b), blocks(xn, b)[:, :, 0:D],
                                                 drop[:, b].unsqueeze(2).to_broadcast([128, NB, D]), ALU.mult))
                    nc.gpsimd.tensor_tensor(blocks(base, b), blocks(base, b), blocks(xi, b), ALU.add).then_inc(base_ready, 1)
                for b in range(B):
                    gp.wait_ge(ms_ready, 2 * B * f + B + b + 1)
                    nc.gpsimd.tensor_tensor(rs[:, b, 1:2], ms[:, b, 1:2], neghalf[:, 0:1], ALU.pow).then_inc(rs_ready, 1)

            ffn(0)

            gp.wait_ge(y_ready, B)
            step(nc.gpsimd.memset(v_set[:].rearrange("p s n j w -> p (s n j w)"), 0.0))
            nc.gpsimd.memset(v_set[:, :, :, :, HD].rearrange("p s n j -> p s (n j)"), 1.0).then_inc(ones_v, 1)
            nc.gpsimd.memset(q_set[:].rearrange("p s j t -> p (s j t)"), 0.0).then_inc(sets_clear, 1)
            nc.gpsimd.memset(k_set[:].rearrange("p s j t -> p (s j t)"), 1.0).then_inc(sets_clear, 1)
            for b in range(B):
                root(1, b)
            for b in range(B):
                gp.wait_ge(y_ready, b + 1)
                nc.gpsimd.tensor_tensor(blocks(base, b), blocks(xb, b),
                                        bo[:].unsqueeze(1).to_broadcast([128, NB, D]), ALU.add).then_inc(att_base, 1)

            def v_to_set(g, s):
                nc.gpsimd.tensor_copy(v_set[:, s, :, :, 0:HD].rearrange("p n j w -> p (n j) w"), v_all[:, g].rearrange("p (a w) -> p a w", w=HD)
                                      if isinstance(g, int) else
                                      v_all[:, bass.ds(g, 1)].rearrange("p o (a w) -> p (o a) w", w=HD)).then_inc(v_set_ready, 1)

            gp.wait_ge(ones_v, 1)
            gp.wait_ge(v_ready, B)
            v_to_set(0, 0)
            v_to_set(1, 1)

            def diagonal(g, c):
                gp.wait_ge(exp_done, g * (NC * HG) + HG * (c + 1))
                gp.sem_inc(diags_seen, 1)
                for at in DIAG[c]:
                    v = p_buf[:, c % 3, :, at:at + 128]
                    last = nc.gpsimd.affine_select(out=v, in_=v, compare_op=ALU.is_ge, fill=0.0, base=0,
                                                   pattern=[[0, HG], [1, 128]], channel_multiplier=-1)
                last.then_inc(diag_done, 1)

            diagonal(0, 0)

            def body(g, s, has_next, copies_v):
                for c in DIAG_CHUNKS[1:]:
                    diagonal(g, c)
                    if c == 3 and copies_v:
                        gp.wait_ge(prob_free, g * NC + 3)
                        v_to_set(g + 2, (s + 2) % SETS)
                if has_next:
                    diagonal(g + 1, 0)

            with gp.Fori(0, (G - 2) // SETS) as i:
                for s in range(SETS):
                    body(i * SETS + s, s, True, True)
            body(G - 2, (G - 2) % SETS, True, False)
            body(G - 1, (G - 1) % SETS, False, False)

            ffn(1)

        @block.vector
        def _(ve):
            V = nc.vector
            step = Step(ve, vec_step)

            ve.wait_ge(loaded_w, 16 * W_COUNT)
            TWO_PI = 2.0 * np.pi
            C1 = 6.28125
            C2 = float(np.float32(np.round((TWO_PI - C1) * 2.0 ** 21) / 2.0 ** 21))
            C3 = float(np.float32(TWO_PI - C1 - C2))
            MAGIC = 1.5 * 2.0 ** 23
            PI_IN = 3.1415925
            step(V.tensor_copy(posf[:, 0:B * (MB + 1)], pos_i[:].rearrange("p b n -> p (b n)")))
            step(V.tensor_tensor(ang[:].rearrange("p (a f) -> p a f", f=HALF),
                                 posf[:, 0:B * (MB + 1)].unsqueeze(2).to_broadcast([128, B * (MB + 1), HALF]),
                                 invf[:].unsqueeze(1).to_broadcast([128, B * (MB + 1), HALF]), ALU.mult))
            for k, (turn, add) in enumerate(((0.25, np.pi / 2), (0.0, 0.0))):
                step(V.tensor_scalar(turns[:], ang[:], float(1.0 / TWO_PI), turn, ALU.mult, ALU.add))
                step(V.tensor_scalar(turns[:], turns[:], MAGIC, MAGIC, ALU.add, ALU.subtract))
                step(V.scalar_tensor_tensor(red[:], turns[:], -C1, ang[:], ALU.mult, ALU.add))
                step(V.scalar_tensor_tensor(red[:], turns[:], -C2, red[:], ALU.mult, ALU.add))
                step(V.scalar_tensor_tensor(red[:], turns[:], -C3, red[:], ALU.mult, ALU.add))
                step(V.tensor_scalar(red[:], red[:], float(add), PI_IN, ALU.add, ALU.min))
                V.tensor_scalar(red2[:, k], red[:], -PI_IN, None, ALU.max).then_inc(angles_ready, 1)
                ve.wait_ge(angles_ready, k + 1)
            ve.wait_ge(trig_ready, 2)
            step(V.tensor_scalar(trig[:, 1], trig[:, 2], -1.0, None, ALU.mult))
            for b in range(B):
                for k in range(3):
                    src = trig[:, k].rearrange("p (b n f) -> p b n f", b=B, n=MB + 1)[:, b]
                    at = AUX_COS + k * HALF
                    V.tensor_copy(blocks(xn, b)[:, 0:MB, at:at + HALF], src[:, 0:MB]).then_inc(aux_trig, 1)
                    V.tensor_copy(blocks(xn, b)[:, MB:NB, at:at + HALF],
                                  src[:, MB:MB + 1].to_broadcast([128, NB - MB, HALF])).then_inc(aux_trig, 1)

            def layernorm(n, xi):
                for b in range(B):
                    for k in range(b * NB, (b + 1) * NB):
                        V.bn_stats(stats[:, k], xi[:, k]).then_inc(vec_step, 1)
                    step.n += NB
                    ve.wait_ge(vec_step, step.n)
                    for k in range(b * NB, (b + 1) * NB):
                        V.bn_aggr(mv[:, k], stats[:, k]).then_inc(vec_step, 1)
                    step.n += NB
                    ve.wait_ge(vec_step, step.n)
                    V.tensor_scalar(veps[:, b], blocks(mv, b)[:, :, 1], LN_EPS, None, ALU.add).then_inc(veps_ready, 1)
                for b in range(B):
                    ve.wait_ge(rstd_ready, B * n + b + 1)
                    for k in range(NB):
                        last = V.tensor_scalar(xn[:, b * NB + k, 0:D], xi[:, b * NB + k], mv[:, b * NB + k, 0:1],
                                               rstd[:, b, k:k + 1], ALU.subtract, ALU.mult)
                    last.then_inc(xn_ready, 1)

            def ffn(f):
                xi, xo = ffn_tokens[f]
                layernorm(2 * f, xi)
                prod = scr[:].rearrange("p (n d) -> p n d", n=NB)
                for b in range(B):
                    n = B * f + b + 1
                    ve.wait_ge(xn_ready, 2 * B * f + b + 1)
                    step(V.tensor_tensor(prod, blocks(xn, b)[:, :, 0:D], rw[:].unsqueeze(1).to_broadcast([128, NB, D]), ALU.mult))
                    step(V.tensor_reduce(wcol[:, b], prod, AX.X, ALU.add))
                    V.tensor_scalar(wcol[:, b], wcol[:, b], rb[:, 0:1], None, ALU.add).then_inc(wcol_ready, 1)
                for b in range(B):
                    n = B * f + b + 1
                    ve.wait_ge(wrow_ps, n)
                    step(V.tensor_copy(wrow[:, b], psum[:, 4 * b:4 * b + 2].rearrange("p a c -> p (a c)")))
                    if b or f:
                        ve.wait_ge(rank_ps, n - 1)
                    for k in range(NB):
                        w = wcol[:, b, k:k + 1]
                        e = 128 * (k + 1)
                        V.tensor_scalar(cmp_gt[:, k, 0:e], wrow[:, b, 0:e], w, None, ALU.is_lt)
                        if e < T:
                            V.tensor_scalar(cmp_gt[:, k, e:T], wrow[:, b, e:T], w, None, ALU.is_le)
                        V.scalar_tensor_tensor(cmp_eq[:, k], wrow[:, b, e - 128:e], w, lower[:], ALU.is_equal,
                                               ALU.mult).then_inc(cmp_ready, 1)
                for b in range(B):
                    n = B * f + b + 1
                    ve.wait_ge(rank_ps, n)
                    V.tensor_copy(rrow[:, b], psum[:, 4 * b:4 * b + 2].rearrange("p a c -> p (a c)")).then_inc(rrow_ready, 1)
                    ve.wait_ge(rrow_ready, n)
                    step(V.scalar_tensor_tensor(scr[:], rrow[:, b], float(KEEP), wrow[:, b], ALU.is_equal, ALU.mult,
                                                accum_out=thr[:, b:b + 1]))
                    V.tensor_scalar(drop[:, b], wcol[:, b], thr[:, b:b + 1], 0.5, ALU.is_le, ALU.mult).then_inc(drop_ready, 1)
                    ve.wait_ge(rcol_ps, n)
                    step(V.tensor_copy(rcol[:, b], bank(4 * b + 2, 0, NB)))
                    V.tensor_tensor(slots_t[:, b, 0:NB], iota_row[:].unsqueeze(1).to_broadcast([128, NB, 128]),
                                    rcol[:, b].unsqueeze(2).to_broadcast([128, NB, 128]), ALU.is_equal).then_inc(slots_t_ready, 1)
                    ve.wait_ge(slots_t_ready, n)
                    V.tensor_reduce(slots_t[:, b, NB], slots_t[:, b, MB:NB].rearrange("p n s -> p s n"), AX.X,
                                    ALU.add).then_inc(clamp_ready, 1)
                    V.tensor_scalar(slots[:, b], rrow[:, b], iota_col[:, 0:1], None, ALU.is_equal).then_inc(slots_ready, 1)

                def rms(b, k, src):
                    n = 2 * B * f + B * k + b + 1
                    ve.wait_ge(ssq_ready, n)
                    V.tensor_scalar(ms[:, b, k:k + 1], ssq[:, b, k:k + 1], 1.0 / D, RMS_EPS, ALU.mult, ALU.add).then_inc(ms_ready, 1)
                    ve.wait_ge(rs_ready, n)
                    V.tensor_scalar(hn[:, b], src, rs[:, b, k:k + 1], None, ALU.mult).then_inc(hn_ready, 1)

                for b in range(B):
                    ve.wait_ge(gather_ps, B * f + b + 1)
                    V.tensor_copy(xs[:, b], bank(4 * b + 3, 0, XW)).then_inc(xs_ready, 1)
                for b in range(B):
                    rms(b, 0, xs[:, b, 0:D])
                for b in range(B):
                    ve.wait_ge(ht_ps, 2 * B * f + b + 1)
                    V.tensor_scalar(ht[:, b], bank(4 * b + 2, 0, D), ln1[:, 0:1], None, ALU.mult).then_inc(ht_ready, 1)
                for b in range(B):
                    ve.wait_ge(qkv_ps, B * f + b + 1)
                    src = bank(4 * b + 2, 0, 2 * D).rearrange("p (h a c) -> p h a c", h=2 * H, a=2)

                    def row(at, shape, view):
                        return xs[:, b, at:at + HALF].unsqueeze(1).to_broadcast([128, 2 * H, HALF])
                    step(V.tensor_tensor(ra[:, :, 0], src[:, :, 0], row(AUX_COS, 0, 0), ALU.mult))
                    step(V.tensor_tensor(ra[:, :, 1], src[:, :, 1], row(AUX_COS, 0, 0), ALU.mult))
                    step(V.tensor_tensor(rbuf[:, :, 0], src[:, :, 1], row(AUX_NSIN, 0, 0), ALU.mult))
                    step(V.tensor_tensor(rbuf[:, :, 1], src[:, :, 0], row(AUX_SIN, 0, 0), ALU.mult))
                    V.tensor_tensor(qk[:, b], ra[:].rearrange("p h a c -> p (h a c)"),
                                    rbuf[:].rearrange("p h a c -> p (h a c)"), ALU.add).then_inc(qk_ready, 1)
                    ve.wait_ge(qk_ready, B * f + b + 1)
                for b in range(B):
                    n = B * f + b + 1
                    ve.wait_ge(qkt_ps, n)
                    if b or f:
                        ve.wait_ge(sc_ps, 2 * (n - 1))
                    V.tensor_copy(qt[:, b], bank(4 * b + 3, 0, D))
                    V.tensor_tensor(ktm[:], bank(4 * b + 3, D, 2 * D).unsqueeze(1).to_broadcast([128, H, 128]),
                                    headmask[:].unsqueeze(2).to_broadcast([128, H, 128]), ALU.mult).then_inc(qkt_ready, 1)
                    for half in range(2):
                        m = 2 * (B * f + b) + half + 1
                        hs = slice(8 * half, 8 * half + 8)
                        ve.wait_ge(sc_ps, m)
                        if half == 0:
                            ve.wait_ge(msel_ready, n)
                            if b or f:
                                ve.wait_ge(exp_ready, m - 1)
                        V.scalar_tensor_tensor(sc[:, hs], psum[:, 4 * b:4 * b + 2].rearrange("p a (h k) -> p (a h) k", k=128),
                                               SCALE, msel[:, b].unsqueeze(1).to_broadcast([128, 8, 128]), ALU.mult,
                                               ALU.add).then_inc(sc_taken, 1)
                        ve.wait_ge(sc_taken, m)
                        V.tensor_reduce(nmx[:, b, hs], sc[:, hs, 0:KEEP], AX.X, ALU.max, negate=True).then_inc(mx_ready, 1)
                    ve.wait_ge(pt_ps, m - 1)
                    if b or f:
                        ve.wait_ge(o_ps, n - 1)
                    V.tensor_copy(prob_t[0:KEEP, 0:8], psum[0:KEEP, 4 * b:4 * b + 2].rearrange("p a (h k) -> p (a h) k", k=128)
                                  ).then_inc(pt_ready_v, 1)
                    ve.wait_ge(exp_ready, m)
                    step(V.reciprocal(rrec[:, b], rsum[:, b]))
                    ve.wait_ge(o_ps, n)
                    V.tensor_tensor(osel[:, b].rearrange("p (h c) -> p h c", h=H),
                                    bank(4 * b + 2, 0, D).rearrange("p (h c) -> p h c", h=H),
                                    rrec[:, b].unsqueeze(2).to_broadcast([128, H, HD]), ALU.mult).then_inc(o_ready, 1)
                for b in range(B):
                    ve.wait_ge(ot_ps, B * f + b + 1)
                    V.tensor_copy(ot[:, b], bank(4 * b + 3, 0, D)).then_inc(ot_ready, 1)
                for b in range(B):
                    ve.wait_ge(x1_ps, B * f + b + 1)
                    V.tensor_tensor(x1[:, b], bank(4 * b + 2, 0, D), xs[:, b, 0:D], ALU.add).then_inc(x1_ready, 1)
                for b in range(B):
                    ve.wait_ge(x1_ready, B * f + b + 1)
                    rms(b, 1, x1[:, b])
                for b in range(B):
                    ve.wait_ge(ht_ps, 2 * B * f + B + b + 1)
                    V.tensor_scalar(ht[:, b], bank(4 * b + 3, 0, D), ln2[:, 0:1], None, ALU.mult).then_inc(ht_ready, 1)
                for b in range(B):
                    n = B * f + b + 1
                    ve.wait_ge(usq_ready, n)
                    step(V.tensor_scalar(usq[:], usq[:], 0.044715, 1.0, ALU.mult, ALU.add))
                    V.tensor_tensor(usq[:], usq[:], bank(4 * b), ALU.mult).then_inc(arg_ready, 1)
                    ve.wait_ge(tanh_ready, n)
                    V.scalar_tensor_tensor(gel[:, b], th[:], 1.0, bank(4 * b), ALU.add, ALU.mult).then_inc(gel_ready, 1)
                for b in range(B):
                    ve.wait_ge(x2_ps, B * f + b + 1)
                    step(V.scalar_tensor_tensor(x2[:, b], bank(4 * b + 2, 0, D), 0.5, x1[:, b], ALU.mult, ALU.add))
                    V.tensor_scalar(proc[:, b], x2[:, b], xs[:, b, AUX_W:AUX_W + 1], 0.5, ALU.mult, ALU.mult).then_inc(proc_ready, 1)
                for b in range(B):
                    ve.wait_ge(y_ps, B * f + b + 1)
                    ve.wait_ge(base_ready, B * f + b + 1)
                    V.tensor_tensor(blocks(xo, b), psum[:, 4 * b:4 * b + 2].rearrange("p a (n d) -> p (a n) d", d=D),
                                    blocks(base, b), ALU.add).then_inc(y_ready, 1)

            ve.wait_ge(loaded_x, 16 * B)
            ve.wait_ge(consts_ready, 1)
            ffn(0)

            ve.wait_ge(y_ready, B)
            layernorm(1, xb)
            for b in range(B):
                ve.wait_ge(xnt_ps, b + 1)
                V.tensor_copy(xnt[:, b], psum[:, 2 * b:2 * b + 2].rearrange("p a c -> p (a c)")).then_inc(xnt_ready, 1)
            for n in range(2 * B):
                b, which = divmod(n, 2)
                two = psum[:, 4 * which:4 * which + 2].rearrange("p a c -> p (a c)")
                rot = psum[:, 4 * which + 2:4 * which + 4].rearrange("p a c -> p (a c)")
                ve.wait_ge(proj_ps, n + 1)
                if n:
                    ve.wait_ge(mid_ready, n)
                    ve.wait_ge(low_ready, n)
                V.scalar_tensor_tensor(rq[:], two, bqk[:, 2 * which:2 * which + 1], rope_c[:, 0], ALU.add, ALU.mult).then_inc(vec_step, 1)
                V.scalar_tensor_tensor(rt[:], rot, bqk[:, 2 * which + 1:2 * which + 2], rope_c[:, 1], ALU.add, ALU.mult).then_inc(vec_step, 1)
                step.n += 2
                ve.wait_ge(vec_step, step.n)
                V.tensor_tensor(rq[:], rq[:], rt[:], ALU.add).then_inc(rot_ready, 1)
                ve.wait_ge(hi_ready, n + 1)
                V.tensor_tensor(rt[:], rq[:], parts[:, 0], ALU.subtract).then_inc(rem_ready, 1)
                ve.wait_ge(mid_ready, n + 1)
                V.tensor_tensor(parts[:, 2], rt[:], parts[:, 1], ALU.subtract).then_inc(low_ready, 1)
                if which == 1:
                    ve.wait_ge(v_ps, b + 1)
                    for g in range(GB):
                        last = V.tensor_tensor(
                            v_all[:, b * GB + g].rearrange("p (n e) -> p n e", n=NB),
                            psum[:, 0:2].rearrange("p a (n e) -> p (a n) e", e=D)[:, :, g * 32:g * 32 + 32],
                            bv[:, g * 32:g * 32 + 32].unsqueeze(1).to_broadcast([128, NB, 32]), ALU.add)
                    last.then_inc(v_ready, 1)

            def slot(a, n):
                return psum[:, 2 * (a % 2):2 * (a % 2) + 2].rearrange("p a c -> p (a c)")[:, 0:n]

            def tile_max(g, a):
                j, i = a // NB, QORDER[a % NB]
                n = 128 * (i + 1)
                ve.wait_ge(tile_ps, g * USES + a + 1)
                ve.sem_inc(tiles_seen, 1)
                V.tensor_tensor_reduce(out=junk_v[:, a % 2, 0:n], in0=slot(a, n), in1=diagmask[:, T - n:T], scale=1.0, scalar=-3.0e38,
                                       op0=ALU.add, op1=ALU.max, accum_out=mx[:, j * NB + i:j * NB + i + 1]).then_inc(tile_taken, 1)

            def max_parts(g):
                ps = psum[0:TILES, 0, 0:128]
                ve.wait_ge(tile_ps, g * USES + USES)
                V.tensor_scalar(shift[0:TILES, 0], ps, -1.0, None, ALU.mult).then_inc(shift_step, 1)
                ve.wait_ge(shift_step, g * 2 + 1)
                V.scalar_tensor_tensor(srem[0:TILES], ps, -1.0, shift[0:TILES, 0], ALU.mult, ALU.subtract).then_inc(tile_taken, 1)
                ve.wait_ge(tile_taken, g * USES + USES)
                V.tensor_copy(shift[0:TILES, 1], srem[0:TILES]).then_inc(shift_step, 1)
                ve.wait_ge(shift_step, g * 2 + 2)
                V.tensor_tensor(shift[0:TILES, 2], srem[0:TILES], shift[0:TILES, 1], ALU.subtract).then_inc(shift_ready, 1)

            def normalise(g, h):
                z = psum[:, 6 + h].rearrange("p (n j w) -> p n j w", n=4, j=HG)
                ve.wait_ge(zt_ps, g * 2 + h + 1)
                V.reciprocal(zrec[:, h].rearrange("p (n j) -> p n j", n=4), z[:, :, :, HD]).then_inc(zrec_ready, 1)
                ve.wait_ge(zrec_ready, g * 2 + h + 1)
                dst = o_all[:, g, h * 128:(h + 1) * 128] if isinstance(g, int) else \
                    o_all[:, bass.ds(g, 1), h * 128:(h + 1) * 128].rearrange("p o e -> p (o e)")
                V.tensor_tensor(dst.rearrange("p (n j w) -> p n j w", n=4, j=HG), z[:, :, :, 0:HD],
                                zrec[:, h].rearrange("p (n j) -> p n j", n=4).unsqueeze(3).to_broadcast([128, 4, HG, HD]),
                                ALU.mult).then_inc(pv_free[h], 1)

            for a in range(TILES):
                tile_max(0, a)
            max_parts(0)
            for a in range(FIRST):
                tile_max(1, a)
            V.memset(zrec[:, 0], 0.0).then_inc(pv_free[0], 1)
            V.memset(zrec[:, 1], 0.0).then_inc(pv_free[1], 1)

            def body(g, has_next, has_second, has_first):
                for what, dg, n, *_ in body_plan(has_next, has_second, has_first):
                    if what == "tile":
                        tile_max(g + dg, n)
                    elif what == "maxt":
                        max_parts(g + dg)
                    elif what == "zt":
                        normalise(g, n)

            with ve.Fori(0, (G - 2) // SETS) as i:
                for s in range(SETS):
                    body(i * SETS + s, True, True, True)
            body(G - 2, True, True, False)
            body(G - 1, False, False, False)

            for b in range(B):
                ve.wait_ge(pv_free[0], G + 1)
                ve.wait_ge(pv_free[1], G + 1)
                V.tensor_copy(o_tok[:, b].rearrange("p n (g e) -> p n g e", g=GB),
                              o_all[:, b * GB:(b + 1) * GB].rearrange("p g (n e) -> p n g e", n=NB)).then_inc(o_tok_ready, 1)
            for b in range(B):
                ve.wait_ge(att_t_ps, b + 1)
                V.tensor_copy(xnt[:, b], psum[:, 4 * b:4 * b + 2].rearrange("p a c -> p (a c)")).then_inc(att_t_ready, 1)
            for b in range(B):
                ve.wait_ge(att_ps, b + 1)
                ve.wait_ge(att_base, b + 1)
                V.tensor_tensor(blocks(xa, b), psum[:, 4 * b + 2:4 * b + 4].rearrange("p a (n d) -> p (a n) d", d=D),
                                blocks(base, b), ALU.add).then_inc(y_ready, 1)
            ve.wait_ge(y_ready, 2 * B)
            ffn(1)

        @block.scalar
        def _(ac):
            A = nc.scalar
            for k in range(2):
                ac.wait_ge(angles_ready, k + 1)
                A.activation(trig[:, 2 * k], red2[:, k], ACT.Sin).then_inc(trig_ready, 1)

            def ffn(f):
                for b in range(B):
                    ac.wait_ge(xs_ready, B * f + b + 1)
                    A.activation(junk_a[:, b], xs[:, b, 0:D], ACT.Square, accum_out=ssq[:, b, 0:1]).then_inc(ssq_ready, 1)
                for b in range(B):
                    ac.wait_ge(u_ps, B * f + b + 1)
                    A.activation(umask[:, b].rearrange("p n s -> p (n s)"),
                                 psum[:, 4 * b:4 * b + 2].rearrange("p a c -> p (a c)")[:, 0:(MB + 1) * 128], ACT.Copy).then_inc(u_ready, 1)
                for b in range(B):
                    ac.wait_ge(msel_ps, B * f + b + 1)
                    A.activation(msel[:, b], bank(4 * b + 3, 0, D), ACT.Copy).then_inc(msel_ready, 1)
                for b in range(B):
                    ac.wait_ge(qk_ready, B * f + b + 1)
                    A.activation(vs[:, b], bank(4 * b + 2, 2 * D, 3 * D), ACT.Copy).then_inc(vs_ready, 1)
                for b in range(B):
                    for half in range(2):
                        m = 2 * (B * f + b) + half + 1
                        ac.wait_ge(mx_ready, m)
                        if half == 0 and (b or f):
                            ac.wait_ge(pt_ps, m - 1)
                        for h in range(8 * half, 8 * half + 8):
                            last = A.activation(prob[:, h, 0:KEEP], sc[:, h, 0:KEEP], ACT.Exp, bias=nmx[:, b, h:h + 1],
                                                accum_out=rsum[:, b, h:h + 1])
                        last.then_inc(exp_ready, 1)
                    ac.wait_ge(pt_ps, m)
                    A.activation(prob_t[0:KEEP, 8:16], psum[0:KEEP, 4 * b:4 * b + 2].rearrange("p a (h k) -> p (a h) k", k=128),
                                 ACT.Copy).then_inc(pt_ready_a, 1)
                for b in range(B):
                    ac.wait_ge(x1_ready, B * f + b + 1)
                    A.activation(junk_a[:, B + b], x1[:, b], ACT.Square, accum_out=ssq[:, b, 1:2]).then_inc(ssq_ready, 1)
                for b in range(B):
                    n = B * f + b + 1
                    ac.wait_ge(hid_ps, n)
                    if n > 1:
                        ac.wait_ge(tanh_ready, n - 1)
                    A.activation(usq[:], bank(4 * b), ACT.Square).then_inc(usq_ready, 1)
                    ac.wait_ge(arg_ready, n)
                    if n > 1:
                        ac.wait_ge(gel_ready, n - 1)
                    A.activation(th[:], usq[:], ACT.Tanh, scale=float(np.sqrt(2.0 / np.pi))).then_inc(tanh_ready, 1)

            ffn(0)

            for n in range(2 * B):
                ac.wait_ge(rot_ready, n + 1)
                if n:
                    ac.wait_ge(parts_stored, 16 * PARTS * n)
                A.activation(parts[:, 0], rq[:], ACT.Copy).then_inc(hi_ready, 1)
                ac.wait_ge(rem_ready, n + 1)
                A.activation(parts[:, 1], rt[:], ACT.Copy).then_inc(mid_ready, 1)

            def exps(g, c, j):
                e = g * (NC * HG) + (HG * c + j)
                ac.wait_ge(st_ps, e + 1)
                if j == 0:
                    ac.wait_ge(prob_free, g * NC + (c + 1))
                A.activation(p_buf[:, c % 3, j], bank(4 + j % 2), ACT.Exp, scale=SCALE).then_inc(exp_done, 1)

            def evacuate(g, h):
                ac.wait_ge(prob_free, g * NC + (HALF_END[h] + 1 + 3))
                A.activation(z_buf[:, h], bank(6 + h), ACT.Copy).then_inc(z_ready, 1)

            ac.wait_ge(parts_stored, 16 * PARTS * 2 * B)
            for j in range(HG):
                exps(0, 0, j)

            def body(g, has_next, has_second, has_first):
                for what, dg, n, *j in body_plan(has_next, has_second, has_first):
                    if what == "st":
                        exps(g + dg, n, j[0])
                    elif what == "evac":
                        evacuate(g, n)

            with ac.Fori(0, (G - 2) // SETS) as i:
                for s in range(SETS):
                    body(i * SETS + s, True, True, True)
            body(G - 2, True, True, False)
            body(G - 1, False, False, False)

            ffn(1)

        @block.tensor
        def _(pe):
            M = nc.tensor

            def mm(out, w, m, start=True, stop=True):
                return M.matmul(out, w, m, start=start, stop=stop)

            def ffn(f):
                for b in range(B):
                    pe.wait_ge(wcol_ready, B * f + b + 1)
                    for k in range(NB):
                        last = M.transpose(bank(4 * b + k // 4, 128 * (k % 4), 128 * (k % 4) + 128),
                                           wcol[:, b, k:k + 1].to_broadcast([128, 128]), ident[:])
                    last.then_inc(wrow_ps, 1)
                for b in range(B):
                    for k in range(NB):
                        pe.wait_ge(cmp_ready, NB * (B * f + b) + k + 1)
                        for h in range(2):
                            mm(bank(4 * b + h), ones_bf[:], cmp_gt[:, k, 512 * h:512 * h + 512], start=(k == 0), stop=False)
                    for k in range(NB):
                        last = mm(bank(4 * b + k // 4, 128 * (k % 4), 128 * (k % 4) + 128), ones_bf[:], cmp_eq[:, k],
                                  start=False, stop=(k % 4 == 3))
                    last.then_inc(rank_ps, 1)
                for b in range(B):
                    n = B * f + b + 1
                    pe.wait_ge(rrow_ready, n)
                    for k in range(NB):
                        last = mm(bank(4 * b + 2, k, k + 1), rrow[0:1, b, 128 * k:128 * k + 128], ident[0:1, 0:1])
                    last.then_inc(rcol_ps, 1)
                for b in range(B):
                    n = B * f + b + 1
                    pe.wait_ge(slots_t_ready, n)
                    pe.wait_ge(aux_w, n)
                    if f == 0:
                        pe.wait_ge(aux_trig, 6 * B)
                    for k in range(NB):
                        last = mm(bank(4 * b + 3, 0, XW), slots_t[:, b, k], xn[:, b * NB + k, :], start=(k == 0), stop=(k == NB - 1))
                    last.then_inc(gather_ps, 1)
                for b in range(B):
                    n = B * f + b + 1
                    pe.wait_ge(clamp_ready, n)
                    if f == 0:
                        pe.wait_ge(mask_wide, B)
                    for c in range(MB + 1):
                        for k in range(MB + 1):
                            last = mm(bank(4 * b + c // 4, 128 * (c % 4), 128 * (c % 4) + 128),
                                      masks[:, b, k, 128 * c:128 * c + 128], slots_t[:, b, k if k < MB else NB],
                                      start=(k == 0), stop=(k == MB))
                    last.then_inc(u_ps, 1)
                for b in range(B):
                    pe.wait_ge(hn_ready, 2 * B * f + b + 1)
                    M.transpose(bank(4 * b + 2, 0, D), hn[:, b], ident[:]).then_inc(ht_ps, 1)
                for b in range(B):
                    pe.wait_ge(u_ready, B * f + b + 1)
                    for k in range(MB + 1):
                        last = mm(bank(4 * b + 3, 0, D), umask[:, b, k], slots_t[:, b, k if k < MB else NB],
                                  start=(k == 0), stop=(k == MB))
                    last.then_inc(msel_ps, 1)
                for b in range(B):
                    pe.wait_ge(ht_ready, 2 * B * f + b + 1)
                    mm(bank(4 * b + 2, 0, 3 * D), ht[:, b], fqkv[:]).then_inc(qkv_ps, 1)
                for b in range(B):
                    n = B * f + b + 1
                    pe.wait_ge(qk_ready, n)
                    pe.wait_ge(msel_ready, n)
                    M.transpose(bank(4 * b + 3, 0, D), qk[:, b, 0:D], ident[:])
                    M.transpose(bank(4 * b + 3, D, 2 * D), qk[:, b, D:2 * D], ident[:]).then_inc(qkt_ps, 1)
                for b in range(B):
                    n = B * f + b + 1
                    pe.wait_ge(qkt_ready, n)
                    for half in range(2):
                        m = 2 * (B * f + b) + half + 1
                        if half:
                            pe.wait_ge(sc_taken, m - 1)
                        for q in range(2):
                            h = 8 * half + 4 * q
                            last = mm(bank(4 * b + q), qt[:, b], ktm[:, h:h + 4].rearrange("p h k -> p (h k)"))
                        last.then_inc(sc_ps, 1)
                    for half in range(2):
                        m = 2 * (B * f + b) + half + 1
                        pe.wait_ge(exp_ready, m)
                        if half == 0:
                            pe.wait_ge(sc_taken, m + 1)
                        else:
                            pe.wait_ge(pt_ready_v, n)
                        for q in range(8):
                            last = M.transpose(psum[0:KEEP, 4 * b + q // 4, 128 * (q % 4):128 * (q % 4) + 128],
                                               prob[:, 8 * half + q, 0:KEEP], ident[:])
                        last.then_inc(pt_ps, 1)
                    pe.wait_ge(pt_ready_a, n)
                    pe.wait_ge(vs_ready, n)
                    for h in range(H):
                        last = mm(bank(4 * b + 2, HD * h, HD * h + HD), prob_t[0:KEEP, h], vs[0:KEEP, b, HD * h:HD * h + HD])
                    last.then_inc(o_ps, 1)
                for b in range(B):
                    pe.wait_ge(o_ready, B * f + b + 1)
                    M.transpose(bank(4 * b + 3, 0, D), osel[:, b], ident[:]).then_inc(ot_ps, 1)
                for b in range(B):
                    pe.wait_ge(ot_ready, B * f + b + 1)
                    mm(bank(4 * b + 2, 0, D), ot[:, b], fwo[:]).then_inc(x1_ps, 1)
                for b in range(B):
                    pe.wait_ge(hn_ready, 2 * B * f + B + b + 1)
                    M.transpose(bank(4 * b + 3, 0, D), hn[:, b], ident[:]).then_inc(ht_ps, 1)
                for b in range(B):
                    pe.wait_ge(ht_ready, 2 * B * f + B + b + 1)
                    for k in range(FB):
                        last = mm(bank(4 * b, 128 * k, 128 * k + 128), fw1[:, 128 * k:128 * k + 128], ht[:, b])
                    last.then_inc(hid_ps, 1)
                for b in range(B):
                    pe.wait_ge(gel_ready, B * f + b + 1)
                    for k in range(FB):
                        last = mm(bank(4 * b + 2, 0, D), gel[:, b, 128 * k:128 * k + 128], fw2[:, k], start=(k == 0), stop=(k == FB - 1))
                    last.then_inc(x2_ps, 1)
                for b in range(B):
                    n = B * f + b + 1
                    pe.wait_ge(proc_ready, n)
                    pe.wait_ge(slots_ready, n)
                    for k in range(NB):
                        last = mm(bank(4 * b + k // 4, 128 * (k % 4), 128 * (k % 4) + 128),
                                  slots[0:KEEP, b, 128 * k:128 * k + 128], proc[0:KEEP, b])
                    last.then_inc(y_ps, 1)

            pe.wait_ge(consts_ready, 1)
            pe.wait_ge(loaded_w, 16 * W_COUNT)
            ffn(0)

            for b in range(B):
                pe.wait_ge(xn_ready, B + b + 1)
                if b == 0:
                    pe.wait_ge(y_ready, B)
                for k in range(NB):
                    last = M.transpose(bank(2 * b + k // 4, 128 * (k % 4), 128 * (k % 4) + 128), xn[:, b * NB + k, 0:D], ident[:])
                last.then_inc(xnt_ps, 1)
            for b in range(B):
                pe.wait_ge(xnt_ready, B)
                for which in range(2):
                    n = 2 * b + which
                    if n >= 2:
                        if which == 0:
                            pe.wait_ge(v_ready, b)
                        else:
                            pe.wait_ge(rot_ready, n - 1)
                    for w in range(2):
                        for h in range(2):
                            last = mm(bank(4 * which + 2 * w + h), wqk[:, 2 * which + w], xnt[:, b, 512 * h:512 * h + 512])
                    last.then_inc(proj_ps, 1)
                pe.wait_ge(rot_ready, 2 * b + 1)
                for k in range(NB):
                    last = mm(bank(k // 4, 128 * (k % 4), 128 * (k % 4) + 128), xnt[:, b, 128 * k:128 * k + 128], wv[:])
                last.then_inc(v_ps, 1)

            def slot(a, lo, hi):
                k = 2 * (a % 2) + lo // 512
                return psum[:, k, lo % 512:lo % 512 + hi - lo]

            def score_tile(g, s, a, first=False):
                j, i = a // NB, QORDER[a % NB]
                if a == 0:
                    pe.wait_ge(set_loaded[s], (g // SETS + 1) * LOADS if isinstance(g, int) else turn(g, s) * LOADS)
                if not (first and a < 2):
                    pe.wait_ge(tile_taken, g * USES + (a if a == 0 else a - 1))
                n = 128 * (i + 1)
                for lo in range(0, n, 512):
                    hi = min(n, lo + 512)
                    last = mm(slot(a, lo, hi), q_set[0:SHIFT, s, j, 128 * i:128 * i + 128], k_set[0:SHIFT, s, j, lo:hi])
                last.then_inc(tile_ps, 1)

            def transpose_max(g):
                pe.wait_ge(tile_taken, g * USES + TILES)
                M.transpose(psum[0:TILES, 0, 0:128], mx[:, 0:TILES], ident[:]).then_inc(tile_ps, 1)

            def score_chunk(g, s, c, j, first=False):
                if c == 0 and j == 0:
                    pe.wait_ge(shift_loaded[s], (g // SETS + 1) * SHIFTS if isinstance(g, int) else turn(g, s) * SHIFTS)
                if not (first and j < 2):
                    pe.wait_ge(exp_done, g * (NC * HG) + (HG * c + j - 1))
                at = 0
                for kb, q0, w in CHUNKS[c]:
                    last = mm(bank(4 + j % 2, at, at + w), k_set[:, s, j, 128 * kb:128 * kb + 128], q_set[:, s, j, q0:q0 + w])
                    at += w
                last.then_inc(st_ps, 1)

            def values(g, s, c):
                if c == 0:
                    pe.wait_ge(v_set_ready, g + 1)
                if c < 2:
                    pe.wait_ge(pv_free[c], g + 1)
                if DIAG[c]:
                    pe.wait_ge(diag_done, g * len(DIAG_CHUNKS) + (DIAG_CHUNKS.index(c) + 1))
                else:
                    pe.wait_ge(exp_done, g * (NC * HG) + HG * (c + 1))
                at = 0
                halves = [q0 // 512 for _, q0, _ in CHUNKS[c]]
                for n, (kb, q0, w) in enumerate(CHUNKS[c]):
                    h = q0 // 512
                    ends = c == HALF_END[h] and h not in halves[n + 1:]
                    for j in range(HG):
                        last = M.matmul(psum[32 * j:32 * j + 32, 6 + h, q0 % 512:q0 % 512 + w], v_set[:, s, kb, j],
                                        p_buf[:, c % 3, j, at:at + w], start=(c == h), stop=ends)
                    at += w
                last.then_inc(prob_free, 1)

            def outputs_t(g, h):
                pe.wait_ge(z_ready, g * 2 + h + 1)
                for k in range(4):
                    last = M.transpose(bank(6 + h, 128 * k, 128 * k + 128), z_buf[:, h, 128 * k:128 * k + 128], ident[:])
                last.then_inc(zt_ps, 1)

            pe.wait_ge(v_ready, B)
            pe.wait_ge(rot_ready, 2 * B)
            M.transpose(psum[0:TILES, 7, 0:128], ident[:, 0:TILES], ident[:]).then_inc(prob_free, 3)
            for a in range(TILES):
                score_tile(0, 0, a, first=True)
            transpose_max(0)
            for a in range(FIRST):
                score_tile(1, 1, a)
            for j in range(HG):
                score_chunk(0, 0, 0, j, first=True)

            def body(g, s, has_next, has_second, has_first):
                for what, dg, n, *j in body_plan(has_next, has_second, has_first):
                    if what == "tile":
                        score_tile(g + dg, (s + dg) % SETS, n)
                    elif what == "maxt":
                        transpose_max(g + dg)
                    elif what == "st":
                        score_chunk(g + dg, (s + dg) % SETS, n, j[0])
                    elif what == "pv":
                        values(g, s, n)
                    elif what == "zt":
                        outputs_t(g, n)

            turn = None
            with pe.Fori(0, (G - 2) // SETS) as i:
                for s in range(SETS):
                    def turn(gg, t, s=s, i=i):
                        return i + (1 if t >= s else 2)
                    body(i * SETS + s, s, True, True, True)
            body(G - 2, (G - 2) % SETS, True, True, False)
            body(G - 1, (G - 1) % SETS, False, False, False)

            for b in range(B):
                pe.wait_ge(o_tok_ready, b + 1)
                for k in range(NB):
                    last = M.transpose(bank(4 * b + k // 4, 128 * (k % 4), 128 * (k % 4) + 128), o_tok[:, b, k], ident[:])
                last.then_inc(att_t_ps, 1)
            for b in range(B):
                pe.wait_ge(att_t_ready, b + 1)
                for k in range(NB):
                    last = mm(bank(4 * b + 2 + k // 4, 128 * (k % 4), 128 * (k % 4) + 128), xnt[:, b, 128 * k:128 * k + 128], wo[:])
                last.then_inc(att_ps, 1)
            ffn(1)


W_COUNT = 19 + 2 * B
LOADS = 16 * 4 * PARTS
SHIFTS = 16 * PARTS


def kernel(**inputs):
    import concourse.bacc as bacc
    from concourse.bass_utils import run_bass_kernel_spmd

    a = {k: np.asarray(v) for k, v in inputs.items()}
    f32 = np.float32

    def turned(w, rotated):
        w = w.reshape(GB, HG, HD, -1)
        if rotated:
            w = np.roll(w, -HALF, axis=2)
        return w.transpose(0, 2, 1, 3).reshape(D, -1)

    wqk = np.stack([turned(a["L0_attn_" + n], r).T for n in ("Wq", "Wk") for r in (False, True)], axis=1)
    bqk = np.concatenate([turned(a["L0_attn_" + n], r) for n in ("bq", "bk") for r in (False, True)], axis=1)
    inv = (1.0 / (np.float32(10000.0) ** (np.arange(0, HD, 2, dtype=f32) / f32(HD)))).astype(f32)
    ang = (np.arange(T, dtype=f32)[:, None] * inv[None, :]).astype(f32)
    ang = np.concatenate([ang, ang], axis=1).astype(np.float64)
    sign = np.where(np.arange(HD) < HALF, -1.0, 1.0)
    rope = np.stack([np.cos(ang).T, (np.sin(ang) * sign).T]).astype(f32)
    rope = np.tile(np.repeat(rope, HG, axis=1), (1, GB, 1)).transpose(1, 0, 2)
    p = "L0_ffn_"
    pos = a[p + "position_ids"][:B]
    pos = np.concatenate([pos.reshape(B, MB, 128), np.broadcast_to(pos[:, -1:, None], (B, 1, 128))], axis=1).transpose(2, 0, 1)
    sent = [
        ("x", a["L0_attn_x"]), ("masks", a[p + "attention_mask"]), ("pos", pos),
        ("rw", a[p + "router_w"]), ("rb", a[p + "router_b"]), ("fwq", a[p + "wq"]), ("fwk", a[p + "wk"]),
        ("fwv", a[p + "wv"]), ("fwo", a[p + "wo"]), ("fw1", a[p + "w1"]), ("fw2", a[p + "w2"]),
        ("ln1", a[p + "ln1"]), ("ln2", a[p + "ln2"]), ("wqk", wqk), ("bqk", bqk), ("wv", a["L0_attn_Wv"].T),
        ("bv", a["L0_attn_bv"]), ("wo", a["L0_attn_Wo"].T), ("bo", a["L0_attn_bo"]), ("rope", rope), ("invf", inv),
    ]
    nc = bacc.Bacc("TRN2", target_bir_lowering=False, num_devices=1)
    arrays, args = {}, []
    for name, value in sent:
        v = np.ascontiguousarray(value)
        arrays[f"in_{name}"] = v
        args.append(nc.dram_tensor(f"in_{name}", v.shape, mybir.dt.from_np(v.dtype), kind="ExternalInput").ap())
    args.append(nc.dram_tensor("out", (B, T, D), mybir.dt.float32, kind="ExternalOutput").ap())
    build(nc, *args)
    r = run_bass_kernel_spmd(nc, [arrays], core_ids=[0])
    return r.results[0]["out"]
```

```python
from contextlib import ExitStack

import numpy as np

import concourse.bass as bass
from concourse import mybir

B, T, D, H = 2, 1024, 128, 16
HD = D // H
NB = T // 128
S_MASK = 512
MB = S_MASK // 128
F = 512
FB = F // 128
KEEP = int(0.125 * T) - 1
HALF = HD // 2
SCALE = float(1.0 / np.sqrt(HD))
LN_EPS, RMS_EPS = 1e-5, 1e-6

AUX_COS, AUX_NSIN, AUX_SIN, AUX_W = D, D + HALF, D + 2 * HALF, D + 3 * HALF
XW = AUX_W + 1

HG = 4
GB = H // HG
G = B * GB
PARTS = 3
STACK = PARTS * PARTS * HD
SHIFT = 128 - PARTS
SETS = 3
VW = 32
NEG = -1.0e30

CHUNKS = [[(0, 0, 512)], [(0, 512, 512)], [(1, 128, 384), (3, 384, 128)], [(2, 256, 256), (6, 768, 256)],
          [(1, 512, 512)], [(2, 512, 512)], [(3, 512, 512)], [(4, 512, 512)], [(5, 640, 384), (7, 896, 128)]]
NC = len(CHUNKS)
CMP_AT = [sum(T - 128 * i for i in range(k)) for k in range(NB + 1)]
DIAG = []
for _pieces in CHUNKS:
    _at, _starts = 0, []
    for _kb, _q0, _w in _pieces:
        if _kb * 128 == _q0:
            _starts.append(_at)
        _at += _w
    DIAG.append(_starts)
DIAG_CHUNKS = [c for c in range(NC) if DIAG[c]]
HALF_END = [3, NC - 1]
TILE_PLAN = [(7, 0, 2), (0, 2, 2), (1, 3, 3), (6, 0, 3), (5, 2, 2), (2, 0, 2), (3, 1, 3), (4, 2, 3)]
TILES = HG * NB
USES = TILES + 1
PROJ_BANK = [0, 4, 4, 0]
V_BANK = [0, 4]
UPPER = 4
FIRST = 14


def body_plan(has_next, has_second, has_first):
    tiles = []
    if has_second:
        tiles += [("tile", 1, a) for a in range(FIRST, TILES)] + [("maxt", 1, 0)]
    if has_first:
        tiles += [("tile", 2, a) for a in range(FIRST)]
    plan, done = [], 0
    n_pos = NC * HG if has_first else NC * HG * 2 // 3
    for n in range(2, NC + 2):
        for j in range(HG):
            if n < NC or has_next:
                plan.append(("st", n // NC, n % NC, j))
            if j == 1 and n - 2 < NC:
                plan.append(("pv", 0, n - 2, 1))
            if j == 3 and (n - 1 < NC or has_next):
                plan.append(("pv", (n - 1) // NC, (n - 1) % NC, 0))
            if (n, j) == (5, 1):
                plan.append(("evac", 0, 0))
            if (n, j) == (NC + 1, 2):
                plan.append(("evac", 0, 1))
            if (n, j) == (6, 2):
                plan.append(("zt", 0, 0))
            upto = min(len(tiles), ((n - 2) * HG + j + 1) * len(tiles) // n_pos)
            plan += tiles[done:upto]
            done = upto
    plan.append(("zt", 0, 1))
    return plan


def build(nc, x_d, masks_d, pos_d, rw_d, rb_d, fwq_d, fwk_d, fwv_d, fwo_d, fw1_d, fw2_d, ln1_d, ln2_d,
          wqk_d, bqk_d, wv_d, bv_d, wo_d, bo_d, rope_d, invf_d, out_d):
    f32, bf16, i32 = mybir.dt.float32, mybir.dt.bfloat16, mybir.dt.int32
    ACT, ALU, AX = mybir.ActivationFunctionType, mybir.AluOpType, mybir.AxisListType

    ctx = ExitStack()
    with ctx:
        def sb(name, shape, dt=f32):
            return ctx.enter_context(nc.sbuf_tensor(name, shape, dt))

        def sem(name):
            return ctx.enter_context(nc.semaphore(name))

        psum = ctx.enter_context(nc.psum_tensor("psum", [128, 8, 512], f32))

        def bank(n, lo=0, hi=512):
            return psum[:, n, lo:hi]

        ident = sb("ident", [128, 128])
        later = sb("later", [128, T], bf16)
        from_last = sb("from_last", [128, NB])
        iota_row = sb("iota_row", [128, 128])
        iota_col = sb("iota_col", [128, 1])
        headmask = sb("headmask", [128, H])
        ones_bf = sb("ones_bf", [128, 128], bf16)
        neghalf = sb("neghalf", [128, NB])
        diagmask = sb("diagmask", [128, T], bf16)
        rope_c = sb("rope_c", [128, 2, T])
        invf = sb("invf", [128, HALF])
        rw = sb("rw", [128, D])
        rb = sb("rb", [128, 1])
        fqkv = sb("fqkv", [128, 3 * D])
        fwo = sb("fwo", [128, GB, D])
        fw1 = sb("fw1", [128, F])
        fw2 = sb("fw2", [128, FB, D])
        ln1 = sb("ln1", [128, 1])
        ln2 = sb("ln2", [128, 1])
        wqk = sb("wqk", [128, 4, D])
        bqk = sb("bqk", [128, 4])
        wv = sb("wv", [128, D])
        bv = sb("bv", [128, D])
        wo = sb("wo", [128, D])
        bo = sb("bo", [128, D])
        masks = sb("masks", [128, B, MB + 1, S_MASK + 128])
        pos_i = sb("pos_i", [128, B, MB + 1], i32)
        vs = sb("vs", [128, B, H, VW])
        xa = sb("xa", [128, B * NB, D])
        xb = sb("xb", [128, B * NB, D])
        xn = sb("xn", [128, B * NB, XW])
        base = sb("base", [128, B * NB, D])
        stats = sb("stats", [128, B * NB, 6])
        mv = sb("mv", [128, B * NB, 2])
        veps = sb("veps", [128, B, NB])
        nmean = sb("nmean", [128, B, NB])
        rstd = sb("rstd", [128, B, NB])
        wcol = sb("wcol", [128, B, NB])
        thr = sb("thr", [128, B])
        drop = sb("drop", [128, B, NB])
        rcol = sb("rcol", [128, B, NB])
        after = sb("after", [128, B, NB])
        before_row = sb("before_row", [128, B, NB])
        dot = sb("dot", [128, B, NB])
        scr = sb("scr", [128, T])
        xs = sb("xs", [128, B, XW])
        ssq = sb("ssq", [128, B, 2])
        ms = sb("ms", [128, B, 2])
        rs = sb("rs", [128, B, 2])
        nmx = sb("nmx", [128, B, H])
        rsum = sb("rsum", [128, B, H])
        rrec = sb("rrec", [128, B, H])

        NA = B * (MB + 1) * HALF
        posf, ang, turns, red = (sb(n, [128, NA]) for n in ("posf", "ang", "turns", "red"))
        trig = sb("trig", [128, 3, NA])
        red2 = sb("red2", [128, 2, NA])

        ARENA = 28672
        arena = sb("arena", [128, ARENA])
        taken = {"ffn": 0, "att": 0}

        def part(who, shape, dt=f32):
            n = int(np.prod(shape))
            words = n if dt == f32 else n // 2
            at = taken[who]
            taken[who] = at + words
            assert taken[who] <= ARENA, (who, taken)
            ap = arena[:, at:at + words]
            if dt != f32:
                ap = ap.bitcast(dt)
            if len(shape) == 2:
                ap = ap.rearrange("p (a b) -> p a b", a=shape[0])
            if len(shape) == 3:
                ap = ap.rearrange("p (a b c) -> p a b c", a=shape[0], b=shape[1])
            if len(shape) == 4:
                ap = ap.rearrange("p (a b c d) -> p a b c d", a=shape[0], b=shape[1], c=shape[2])
            return ap

        ktm = part("ffn", [B, H, 128])
        slots = part("ffn", [B, T])
        slots_t = part("ffn", [B, NB + 1, 128])
        cmp_at = taken["ffn"]
        cmp = part("ffn", [B, CMP_AT[NB]], bf16)
        cmp_end = taken["ffn"]
        taken["ffn"] = cmp_at
        sc = part("ffn", [B, H, 128])
        taken["ffn"] = max(taken["ffn"], cmp_end)
        umask = part("ffn", [B, MB + 1, 128])
        prob = part("ffn", [B, H, 128])
        ra = part("ffn", [B, 2 * H, 2, HALF])
        rbuf = part("ffn", [B, 2 * H, 2, HALF])
        qk = part("ffn", [B, 2 * D])
        qt = part("ffn", [B, D])
        msel = part("ffn", [B, D])
        x1 = part("ffn", [B, D])
        x2 = part("ffn", [B, D])
        proc = part("ffn", [B, D])
        junk_a = part("ffn", [2 * B, D])
        rows_at = taken["ffn"]
        wrow = part("ffn", [B, T])
        rrow = part("ffn", [B, T])
        taken["ffn"] = rows_at
        ot = part("ffn", [B, GB * 128])
        usq = part("ffn", [B, F])
        th = part("ffn", [B, F])
        gel = part("ffn", [B, F])
        hn = part("ffn", [B, D])
        ht = part("ffn", [B, D])

        q_set = part("att", [SETS, HG, T], bf16)
        k_set = part("att", [SETS, HG, T], bf16)
        v_all = part("att", [G, NB * HG * HD])
        v_set = part("att", [SETS, NB, HG, VW])
        p_at = taken["att"]
        p_buf = part("att", [3, HG, 512])
        p_end = taken["att"]
        taken["att"] = p_at
        xnt = part("att", [B, T])
        p0 = part("att", [PARTS, T], bf16)
        rq = part("att", [2, T])
        assert taken["att"] <= p_end
        taken["att"] = p_at + B * T
        o_tok = part("att", [B, NB, D])
        taken["att"] = p_end
        o_all = part("att", [G, NB * HG * HD])
        z_buf = part("att", [2, 512])
        zrec = part("att", [2, 16])
        mx = part("att", [1, TILES])[:, 0]
        shift = part("att", [PARTS, 128], bf16)
        srem = part("att", [1, 128])[:, 0]
        junk_v = part("att", [3, T], bf16)
        parts = [[p0[:, p] for p in range(PARTS)],
                 [z_buf[:, 0].bitcast(bf16), z_buf[:, 1].bitcast(bf16), scr[:, 0:T // 2].bitcast(bf16)]]
        rt = xa[:, 0:2 * NB].rearrange("p n d -> p (n d)").rearrange("p (two t) -> p two t", two=2)

        qk_scr = [nc.dram_tensor(f"{n}_parts", (G, PARTS * HD, HG * T), bf16, kind="Internal").ap() for n in ("q", "k")]

        loaded_x, loaded_r = [sem(f"loaded_x{b}") for b in range(B)], sem("loaded_r")
        loaded_p = sem("loaded_p")
        loaded_f, loaded_m, loaded_a = sem("loaded_f"), sem("loaded_m"), sem("loaded_a")
        pool_step, vec_step, act_step = sem("pool_step"), sem("vec_step"), sem("act_step")
        ident_ready, consts_ready = sem("ident_ready"), sem("consts_ready")
        angles_ready, trig_ready, aux_trig = sem("angles_ready"), sem("trig_ready"), sem("aux_trig")
        mask_wide = sem("mask_wide")
        xn_att_ready = sem("xn_att_ready")
        veps_ready, rstd_ready, xn_ready = sem("veps_ready"), sem("rstd_ready"), sem("xn_ready")
        vs_clear, half_done = sem("vs_clear"), sem("half_done")
        rrec_ready, norm_ready, last_norm_ready = sem("rrec_ready"), sem("norm_ready"), sem("last_norm_ready")
        nmean_ready = sem("nmean_ready")
        wcol_ready, aux_w, wrow_ps = sem("wcol_ready"), sem("aux_w"), sem("wrow_ps")
        wrow_ready, dot_ready = sem("wrow_ready"), sem("dot_ready")
        cmp_ready, rank_ps, rrow_ready = sem("cmp_ready"), sem("rank_ps"), sem("rrow_ready")
        before_ready, rrow_ps = sem("before_ready"), sem("rrow_ps")
        rcol_ps, drop_ready, slots_ready = sem("rcol_ps"), sem("drop_ready"), sem("slots_ready")
        slots_t_ready, clamp_ready, gather_ps = sem("slots_t_ready"), sem("clamp_ready"), sem("gather_ps")
        xs_ready, ssq_ready, ms_ready, rs_ready = sem("xs_ready"), sem("ssq_ready"), sem("ms_ready"), sem("rs_ready")
        hn_ready, ht_ps, ht_ready = sem("hn_ready"), sem("ht_ps"), sem("ht_ready")
        u_ps, u_ready, msel_ps, msel_ready = sem("u_ps"), sem("u_ready"), sem("msel_ps"), sem("msel_ready")
        qkv_ps, qk_ready, vs_ready = sem("qkv_ps"), sem("qk_ready"), sem("vs_ready")
        qkt_ps, qkt_ready, ktm_ready_a = sem("qkt_ps"), sem("qkt_ready"), sem("ktm_ready_a")
        sc_ps = sem("sc_ps")
        sc_taken, mx_ready, exp_ready = sem("sc_taken"), sem("mx_ready"), sem("exp_ready")
        pt_ps, pt_ready_v, pt_ready_a = sem("pt_ps"), sem("pt_ready_v"), sem("pt_ready_a")
        o_ps, o_ready, ot_ps, ot_ready = sem("o_ps"), sem("o_ready"), sem("ot_ps"), sem("ot_ready")
        x1_ps, x1_ready, hid_ps = sem("x1_ps"), sem("x1_ready"), sem("hid_ps")
        usq_ready, arg_ready, tanh_ready, gel_ready = sem("usq_ready"), sem("arg_ready"), sem("tanh_ready"), sem("gel_ready")
        x2_ps, proc_ready, base_ready = sem("x2_ps"), sem("proc_ready"), sem("base_ready")
        y_ps, y_ready, stored = sem("y_ps"), sem("y_ready"), sem("stored")
        sets_clear, ones_ready, ones_v = sem("sets_clear"), sem("ones_ready"), sem("ones_v")
        xnt_ps, xnt_ready = sem("xnt_ps"), sem("xnt_ready")
        proj_ps, rot_ready, hi_ready, rem_ready, mid_ready = (
            sem("proj_ps"), sem("rot_ready"), sem("hi_ready"), sem("rem_ready"), sem("mid_ready"))
        low_ready, v_ps, v_ready = sem("low_ready"), sem("v_ps"), sem("v_ready")
        parts_stored = [sem("parts_stored0"), sem("parts_stored1")]
        set_loaded = [sem(f"set_loaded{i}") for i in range(SETS)]
        shift_loaded = [sem(f"shift_loaded{i}") for i in range(SETS)]
        v_set_ready = sem("v_set_ready")
        tile_ps, tile_taken = sem("tile_ps"), sem("tile_taken")
        tiles_seen, diags_seen = sem("tiles_seen"), sem("diags_seen")
        shift_step, shift_ready = sem("shift_step"), sem("shift_ready")
        st_ps, exp_done, diag_done = sem("st_ps"), sem("exp_done"), sem("diag_done")
        prob_free = sem("prob_free")
        z_ready, zt_ps, zrec_ready = sem("z_ready"), sem("zt_ps"), sem("zrec_ready")
        pv_free = [sem("pv_free0"), sem("pv_free1")]
        o_tok_ready, att_t_ps, att_t_ready, att_ps, att_base = sem("o_tok_ready"), sem("att_t_ps"), sem("att_t_ready"), sem("att_ps"), sem("att_base")

        class Step:

            def __init__(self, eng, s):
                self.eng, self.s, self.n = eng, s, 0

            def __call__(self, ins):
                self.n += 1
                ins.then_inc(self.s, 1)
                self.eng.wait_ge(self.s, self.n)

        def blocks(t, b):
            return t[:, b * NB:(b + 1) * NB]

        W_LOADS = 0
        ffn_tokens = {0: (xa, xb), 1: (xa, xb)}
        block = ctx.enter_context(nc.Block())

        @block.sync
        def _(sp):
            for b in range(B):
                sp.dma_start(blocks(xa, b), x_d[b].rearrange("(n p) d -> p n d", p=128)).then_inc(loaded_x[b], 16)

            def load(done, *pairs):
                for dst, src in pairs:
                    sp.dma_start(dst, src).then_inc(done, 16)

            load(loaded_r, (rw[:], rw_d.rearrange("d o -> o d").partition_broadcast(128).rearrange("p o d -> p (o d)")),
                 (rb[:], rb_d.partition_broadcast(128)))
            load(loaded_p, (invf[:], invf_d.partition_broadcast(128)), (pos_i[:], pos_d))
            load(loaded_f, (ln1[:], ln1_d.rearrange("(p o) -> p o", o=1)), (ln2[:], ln2_d.rearrange("(p o) -> p o", o=1)),
                 (fqkv[:, 0:D], fwq_d), (fqkv[:, D:2 * D], fwk_d), (fqkv[:, 2 * D:], fwv_d), (fwo[:], fwo_d),
                 (fw1[:], fw1_d), (fw2[:], fw2_d.rearrange("(n p) d -> p n d", p=128)))
            for b in range(B):
                load(loaded_m, (masks[:, b, 0:MB, 0:S_MASK], masks_d[b, 0].rearrange("(n p) c -> p n c", p=128)),
                     (masks[:, b, MB, 0:S_MASK], masks_d[b, 0, S_MASK - 1].partition_broadcast(128)))
            load(loaded_a, (bv[:], bv_d.partition_broadcast(128)), (bo[:], bo_d.partition_broadcast(128)),
                 (wqk[:], wqk_d), (bqk[:], bqk_d), (wv[:], wv_d), (wo[:], wo_d), (rope_c[:], rope_d))

            def load_set(g, which=(0, 1)):
                s = g % SETS
                for p in range(PARTS):
                    rows = slice(p * PARTS * HD, (p + 1) * PARTS * HD)
                    src = qk_scr[0][g, p * HD:(p + 1) * HD, :]
                    if 0 in which:
                        sp.dma_start(q_set[rows, s].rearrange("p a b -> p (a b)"),
                                     src.unsqueeze(0).to_broadcast([PARTS, HD, HG * T])).then_inc(set_loaded[s], 16)
                    if 1 in which:
                        sp.dma_start(k_set[rows, s].rearrange("p a b -> p (a b)"), qk_scr[1][g]).then_inc(set_loaded[s], 16)

            for n in range(2 * B):
                b, which = divmod(n, 2)
                for p in range(PARTS):
                    sp.wait_ge((hi_ready, mid_ready, low_ready)[p], n + 1)
                    sp.dma_start(
                        qk_scr[which][b * GB:(b + 1) * GB, p * HD:(p + 1) * HD, :].rearrange("g d (j t) -> g (d j) t", j=HG),
                        parts[n % 2][p]).then_inc(parts_stored[n % 2], 16)
                if n == 1:
                    sp.wait_ge(sets_clear, 1)
                    sp.wait_ge(ones_ready, SETS)
                    for which in range(2):
                        sp.wait_ge(parts_stored[which], 16 * PARTS)
                        load_set(0, (which,))
                    for g in range(1, SETS):
                        load_set(g)
            for half in parts_stored:
                sp.wait_ge(half, 16 * PARTS * B)
            for g in range(G):
                sp.wait_ge(shift_ready, g + 1)
                for r in range(PARTS):
                    sp.dma_start(q_set[SHIFT + r:SHIFT + r + 1, g % SETS].rearrange("p j (i c) -> p (j i) c", c=128),
                                 shift[0:TILES, r, :]).then_inc(shift_loaded[g % SETS], 16)
                if 1 <= g <= G - SETS:
                    sp.wait_ge(st_ps, NC * HG * g)
                    load_set(g - 1 + SETS)
            for b in range(B):
                sp.wait_ge(y_ready, B * 2 + b + 1)
                sp.dma_start(out_d[b].rearrange("(n p) d -> p n d", p=128), blocks(xb, b)).then_inc(stored, 16)
            sp.wait_ge(stored, 16 * B)

        @block.gpsimd
        def _(gp):
            step = Step(gp, pool_step)

            def root(n, b):
                gp.wait_ge(veps_ready, B * n + b + 1)
                nc.gpsimd.tensor_tensor(rstd[:, b], veps[:, b], neghalf[:], ALU.pow).then_inc(rstd_ready, 1)

            step(nc.gpsimd.memset(neghalf[:], -0.5))
            step(nc.gpsimd.memset(ident[:], 0.0))
            nc.gpsimd.affine_select(out=ident[:], in_=ident[:], compare_op=ALU.not_equal, fill=1.0, base=0,
                                    pattern=[[1, 128]], channel_multiplier=-1).then_inc(ident_ready, 1)
            step(nc.gpsimd.memset(later[:], 1.0))
            step(nc.gpsimd.affine_select(out=later[:, 0:128], in_=later[:, 0:128], compare_op=ALU.is_gt, fill=0.0, base=0,
                                         pattern=[[1, 128]], channel_multiplier=-1))
            step(nc.gpsimd.iota(from_last[:], pattern=[[-128, NB]], base=T - 1, channel_multiplier=-1,
                                allow_small_or_imprecise_dtypes=True))
            step(nc.gpsimd.memset(diagmask[:], 0.0))
            dm = diagmask[:, T - 128:T]
            step(nc.gpsimd.affine_select(out=dm, in_=dm, compare_op=ALU.is_ge, fill=NEG, base=0,
                                         pattern=[[-1, 128]], channel_multiplier=1))
            for b in range(B):
                root(0, b)
            step(nc.gpsimd.memset(headmask[:], 1.0))
            step(nc.gpsimd.affine_select(out=headmask[:], in_=headmask[:], compare_op=ALU.is_ge, fill=0.0, base=0,
                                         pattern=[[-HD, H]], channel_multiplier=1))
            step(nc.gpsimd.affine_select(out=headmask[:], in_=headmask[:], compare_op=ALU.is_ge, fill=0.0, base=HD - 1,
                                         pattern=[[HD, H]], channel_multiplier=-1))
            step(nc.gpsimd.iota(iota_row[:], pattern=[[1, 128]], base=0, channel_multiplier=0,
                                allow_small_or_imprecise_dtypes=True))
            step(nc.gpsimd.iota(iota_col[:], pattern=[[0, 1]], base=0, channel_multiplier=1,
                                allow_small_or_imprecise_dtypes=True))
            nc.gpsimd.memset(ones_bf[:], 1.0).then_inc(consts_ready, 1)
            nc.gpsimd.memset(vs[:].rearrange("p b h w -> p (b h w)"), 0.0).then_inc(vs_clear, 1)

            TWO_PI = 2.0 * np.pi
            C1 = 6.28125
            C2 = float(np.float32(np.round((TWO_PI - C1) * 2.0 ** 21) / 2.0 ** 21))
            C3 = float(np.float32(TWO_PI - C1 - C2))
            MAGIC = 1.5 * 2.0 ** 23
            PI_IN = 3.1415925
            NP = B * (MB + 1)

            def angles():
                ts, tt = nc.gpsimd.tensor_scalar, nc.gpsimd.tensor_tensor
                gp.wait_ge(loaded_p, 16 * 2)
                step(nc.gpsimd.tensor_copy(posf[:, 0:NP], pos_i[:].rearrange("p b n -> p (b n)")))
                step(tt(ang[:].rearrange("p (a f) -> p a f", f=HALF), posf[:, 0:NP].unsqueeze(2).to_broadcast([128, NP, HALF]),
                        invf[:].unsqueeze(1).to_broadcast([128, NP, HALF]), ALU.mult))
                for k, (turn, add) in enumerate(((0.25, np.pi / 2), (0.0, 0.0))):
                    step(ts(turns[:], ang[:], float(1.0 / TWO_PI), turn, ALU.mult, ALU.add))
                    step(ts(turns[:], turns[:], MAGIC, None, ALU.add))
                    step(ts(turns[:], turns[:], MAGIC, None, ALU.subtract))
                    src = ang
                    for part_of_turn in (C1, C2, C3):
                        step(ts(posf[:], turns[:], part_of_turn, None, ALU.mult))
                        step(tt(red[:], src[:], posf[:], ALU.subtract))
                        src = red
                    step(ts(red[:], red[:], float(add), PI_IN, ALU.add, ALU.min))
                    nc.gpsimd.tensor_scalar(red2[:, k], red[:], -PI_IN, None, ALU.max).then_inc(angles_ready, 1)
                    gp.wait_ge(angles_ready, k + 1)
                gp.wait_ge(trig_ready, 2)
                step(ts(trig[:, 1], trig[:, 2], -1.0, None, ALU.mult))
                for b in range(B):
                    src = trig[:].rearrange("p k (b n f) -> p b n k f", b=B, n=MB + 1)[:, b]
                    dst = blocks(xn, b)[:, :, AUX_COS:AUX_W].rearrange("p n (k f) -> p n k f", k=3)
                    nc.gpsimd.tensor_copy(dst[:, 0:MB], src[:, 0:MB]).then_inc(aux_trig, 1)
                    nc.gpsimd.tensor_copy(dst[:, MB:NB], src[:, MB:MB + 1].to_broadcast([128, NB - MB, 3, HALF])).then_inc(aux_trig, 1)

            def ffn(f):
                xi, _ = ffn_tokens[f]
                if f:
                    for b in range(B):
                        root(2, b)
                if f == 0:
                    angles()
                for b in range(B):
                    gp.wait_ge(wcol_ready, B * f + b + 1)
                    gp.wait_ge(xn_ready, B * f + b + 1)
                    nc.gpsimd.tensor_copy(blocks(xn, b)[:, :, AUX_W], wcol[:, b]).then_inc(aux_w, 1)
                def rms_root(k, b):
                    gp.wait_ge(ssq_ready, 2 * B * f + B * k + b + 1)
                    step(nc.gpsimd.tensor_scalar(ms[:, b, k:k + 1], ssq[:, b, k:k + 1], 1.0 / D, RMS_EPS, ALU.mult, ALU.add))
                    nc.gpsimd.tensor_tensor(rs[:, b, k:k + 1], ms[:, b, k:k + 1], neghalf[:, 0:1], ALU.pow).then_inc(rs_ready, 1)

                def one_hot(b):
                    gp.wait_ge(rrow_ready, B * f + b + 1)
                    nc.gpsimd.tensor_scalar(slots[:, b], rrow[:, b], iota_col[:, 0:1], None, ALU.is_equal).then_inc(slots_ready, 1)

                one_hot(0)
                rms_root(0, 0)
                rms_root(0, 1)
                one_hot(1)
                for b in range(B):
                    gp.wait_ge(drop_ready, B * f + b + 1)
                    step(nc.gpsimd.tensor_tensor(blocks(base, b), blocks(xn, b)[:, :, 0:D],
                                                 drop[:, b].unsqueeze(2).to_broadcast([128, NB, D]), ALU.mult))
                    nc.gpsimd.tensor_tensor(blocks(base, b), blocks(base, b), blocks(xi, b), ALU.add).then_inc(base_ready, 1)
                for n in range(2 * B - 1):
                    b, half = divmod(n, 2)
                    hs = slice(8 * half, 8 * half + 8)
                    gp.wait_ge(rrec_ready, 2 * B * f + n + 1)
                    nc.gpsimd.tensor_tensor(prob[:, b, hs, 0:KEEP], prob[:, b, hs, 0:KEEP],
                                            rrec[:, b, hs].unsqueeze(2).to_broadcast([128, 8, KEEP]), ALU.mult).then_inc(norm_ready, 1)
                for b in range(B):
                    rms_root(1, b)

            ffn(0)

            for b in range(B):
                root(1, b)
            gp.wait_ge(y_ready, B)
            step(nc.gpsimd.memset(v_set[:].rearrange("p s n j w -> p (s n j w)"), 0.0))
            nc.gpsimd.memset(v_set[:, :, :, :, HD].rearrange("p s n j -> p s (n j)"), 1.0).then_inc(ones_v, 1)
            nc.gpsimd.memset(q_set[:].rearrange("p s j t -> p (s j t)"), 0.0).then_inc(sets_clear, 1)
            for b in range(B):
                gp.wait_ge(y_ready, b + 1)
                gp.wait_ge(loaded_a, 16 * 7)
                nc.gpsimd.tensor_tensor(blocks(base, b), blocks(xb, b),
                                        bo[:].unsqueeze(1).to_broadcast([128, NB, D]), ALU.add).then_inc(att_base, 1)
                for which in range(2):
                    n = 2 * b + which
                    gp.wait_ge(mid_ready, n + 1)
                    nc.gpsimd.tensor_tensor(parts[n % 2][2], rt[:, n % 2], parts[n % 2][1], ALU.subtract).then_inc(low_ready, 1)

            def v_to_set(g, s):
                nc.gpsimd.tensor_copy(v_set[:, s, :, :, 0:HD].rearrange("p n j w -> p (n j) w"), v_all[:, g].rearrange("p (a w) -> p a w", w=HD)
                                      if isinstance(g, int) else
                                      v_all[:, bass.ds(g, 1)].rearrange("p o (a w) -> p (o a) w", w=HD)).then_inc(v_set_ready, 1)

            gp.wait_ge(ones_v, 1)
            gp.wait_ge(v_ready, B)
            v_to_set(0, 0)
            v_to_set(1, 1)

            def diagonal(g, c):
                gp.wait_ge(exp_done, g * (NC * HG) + HG * (c + 1))
                gp.sem_inc(diags_seen, 1)
                for at in DIAG[c]:
                    v = p_buf[:, c % 3, :, at:at + 128]
                    last = nc.gpsimd.affine_select(out=v, in_=v, compare_op=ALU.is_ge, fill=0.0, base=0,
                                                   pattern=[[0, HG], [1, 128]], channel_multiplier=-1)
                last.then_inc(diag_done, 1)

            diagonal(0, 0)

            def body(g, s, has_next, copies_v):
                for c in DIAG_CHUNKS[1:]:
                    diagonal(g, c)
                    if c == 3 and copies_v:
                        gp.wait_ge(prob_free, g * NC + 3)
                        v_to_set(g + 2, (s + 2) % SETS)
                if has_next:
                    diagonal(g + 1, 0)

            with gp.Fori(0, (G - 2) // SETS) as i:
                for s in range(SETS):
                    body(i * SETS + s, s, True, True)
            body(G - 2, (G - 2) % SETS, True, False)
            body(G - 1, (G - 1) % SETS, False, False)

            ffn(1)

        @block.vector
        def _(ve):
            V = nc.vector
            step = Step(ve, vec_step)

            def moments(n, b, xi):
                if n == 0:
                    ve.wait_ge(loaded_x[b], 16)
                else:
                    ve.wait_ge(y_ready, B * (n - 1) + b + 1)
                for k in range(b * NB, (b + 1) * NB):
                    V.bn_stats(stats[:, k], xi[:, k]).then_inc(vec_step, 1)
                step.n += NB
                ve.wait_ge(vec_step, step.n)
                for k in range(b * NB, (b + 1) * NB):
                    V.bn_aggr(mv[:, k], stats[:, k]).then_inc(vec_step, 1)
                step.n += NB
                ve.wait_ge(vec_step, step.n)
                V.tensor_scalar(veps[:, b], blocks(mv, b)[:, :, 1], LN_EPS, None, ALU.add).then_inc(veps_ready, 1)
                if n != 1:
                    V.tensor_scalar(nmean[:, b], blocks(mv, b)[:, :, 0], -1.0, None, ALU.mult).then_inc(nmean_ready, 1)

            def ffn(f):
                xi, xo = ffn_tokens[f]
                prod = scr[:].rearrange("p (n d) -> p n d", n=NB)

                def products(b):
                    if b or f:
                        ve.wait_ge(dot_ready, B * f + b)
                    for k in range(NB):
                        last = V.scalar_tensor_tensor(prod[:, k], xi[:, b * NB + k], mv[:, b * NB + k, 0:1], rw[:],
                                                      ALU.subtract, ALU.mult, accum_out=dot[:, b, k:k + 1])
                    last.then_inc(dot_ready, 1)

                def router(b):
                    ve.wait_ge(rstd_ready, 2 * B * f + b + 1)
                    ve.wait_ge(dot_ready, B * f + b + 1)
                    step(V.tensor_tensor(wcol[:, b], dot[:, b], rstd[:, b], ALU.mult))
                    V.tensor_scalar(wcol[:, b], wcol[:, b], rb[:, 0:1], None, ALU.add).then_inc(wcol_ready, 1)

                if f == 0:
                    for b in range(B):
                        moments(0, b, xi)
                    ve.wait_ge(loaded_r, 16 * 2)
                products(0)
                router(0)
                products(1)
                router(1)

                def compare(b, ks):
                    for k in ks:
                        V.scalar_tensor_tensor(cmp[:, b, CMP_AT[k]:CMP_AT[k + 1]], wrow[:, b, 128 * k:T], wcol[:, b, k:k + 1],
                                               later[:, 0:T - 128 * k], ALU.is_le, ALU.mult,
                                               accum_out=after[:, b, k:k + 1]).then_inc(cmp_ready, 1)

                def later_before(b):
                    ve.wait_ge(cmp_ready, NB * (B * f + b + 1))
                    V.tensor_tensor(before_row[:, b], from_last[:], after[:, b], ALU.subtract).then_inc(before_ready, 1)

                def one_hot(b):
                    n = B * f + b + 1
                    ve.wait_ge(before_ready, n)
                    ve.wait_ge(rank_ps, n)
                    step(V.tensor_tensor(rcol[:, b], bank(4 * b + 2, 0, NB), before_row[:, b], ALU.add))
                    V.tensor_tensor(slots_t[:, b, 0:NB], iota_row[:].unsqueeze(1).to_broadcast([128, NB, 128]),
                                    rcol[:, b].unsqueeze(2).to_broadcast([128, NB, 128]), ALU.is_equal).then_inc(slots_t_ready, 1)
                    ve.wait_ge(slots_t_ready, n)
                    V.tensor_reduce(slots_t[:, b, NB], slots_t[:, b, MB:NB].rearrange("p n s -> p s n"), AX.X,
                                    ALU.add).then_inc(clamp_ready, 1)

                def rope(b):
                    ve.wait_ge(qkv_ps, B * f + b + 1)
                    src = bank(4 * b + 2, 0, 2 * D).rearrange("p (h a c) -> p h a c", h=2 * H, a=2)

                    def row(at):
                        return xs[:, b, at:at + HALF].unsqueeze(1).to_broadcast([128, 2 * H, HALF])
                    V.tensor_tensor(ra[:, b, :, 0], src[:, :, 0], row(AUX_COS), ALU.mult)
                    V.tensor_tensor(ra[:, b, :, 1], src[:, :, 1], row(AUX_COS), ALU.mult)
                    V.tensor_tensor(rbuf[:, b, :, 0], src[:, :, 1], row(AUX_NSIN), ALU.mult)
                    step(V.tensor_tensor(rbuf[:, b, :, 1], src[:, :, 0], row(AUX_SIN), ALU.mult))
                    V.tensor_tensor(qk[:, b], ra[:, b].rearrange("p h a c -> p (h a c)"),
                                    rbuf[:, b].rearrange("p h a c -> p (h a c)"), ALU.add).then_inc(qk_ready, 1)

                def threshold(b):
                    n = B * f + b + 1
                    ve.wait_ge(rrow_ready, n)
                    if b:
                        ve.wait_ge(drop_ready, n - 1)
                    else:
                        ve.wait_ge(dot_ready, B * (f + 1))
                    step(V.scalar_tensor_tensor(scr[:], rrow[:, b], float(KEEP), wrow[:, b], ALU.is_equal, ALU.mult,
                                                accum_out=thr[:, b:b + 1]))
                    V.tensor_scalar(drop[:, b], wcol[:, b], thr[:, b:b + 1], 0.5, ALU.is_le, ALU.mult).then_inc(drop_ready, 1)

                if f == 0:
                    ve.wait_ge(consts_ready, 1)
                ve.wait_ge(wrow_ready, B * f + 1)
                compare(0, range(NB))
                later_before(0)
                ve.wait_ge(wrow_ready, B * f + 2)
                compare(1, range(2))
                one_hot(0)
                compare(1, range(2, NB))
                later_before(1)
                one_hot(1)
                rope(0)
                threshold(0)
                threshold(1)
                rope(1)

                def keys(b):
                    n = B * f + b + 1
                    ve.wait_ge(qkt_ps, n)
                    V.tensor_copy(qt[:, b], bank(4 * b + 3, 0, D))
                    V.tensor_tensor(ktm[:, b, 0:H // 2], bank(4 * b + 3, D, 2 * D).unsqueeze(1).to_broadcast([128, H // 2, 128]),
                                    headmask[:, 0:H // 2].unsqueeze(2).to_broadcast([128, H // 2, 128]), ALU.mult).then_inc(qkt_ready, 1)

                def masked(b, half):
                    m = 2 * (B * f + b) + half + 1
                    hs = slice(8 * half, 8 * half + 8)
                    ve.wait_ge(msel_ready, B * f + b + 1)
                    ve.wait_ge(sc_ps, m)
                    V.scalar_tensor_tensor(sc[:, b, hs], psum[:, 4 * half:4 * half + 2].rearrange("p a (h k) -> p (a h) k", k=128),
                                           SCALE, msel[:, b].unsqueeze(1).to_broadcast([128, 8, 128]), ALU.mult,
                                           ALU.add).then_inc(sc_taken, 1)
                    ve.wait_ge(sc_taken, m)
                    V.tensor_reduce(nmx[:, b, hs], sc[:, b, hs, 0:KEEP], AX.X, ALU.max, negate=True).then_inc(mx_ready, 1)

                def over_sums(b, half):
                    hs = slice(8 * half, 8 * half + 8)
                    m = 2 * (B * f + b) + half + 1
                    ve.wait_ge(exp_ready, m)
                    V.reciprocal(rrec[:, b, hs], rsum[:, b, hs]).then_inc(rrec_ready, 1)
                    if (b, half) == (B - 1, 1):
                        ve.wait_ge(rrec_ready, m)
                        V.tensor_tensor(prob[:, b, hs, 0:KEEP], prob[:, b, hs, 0:KEEP],
                                        rrec[:, b, hs].unsqueeze(2).to_broadcast([128, 8, KEEP]), ALU.mult).then_inc(last_norm_ready, 1)

                keys(0)
                masked(0, 0)
                masked(0, 1)
                keys(1)
                over_sums(0, 0)
                masked(1, 0)
                over_sums(0, 1)
                masked(1, 1)
                over_sums(1, 0)
                for half in range(2):
                    ve.wait_ge(pt_ps, 2 * B * f + half + 1)
                    V.tensor_copy(ktm[0:KEEP, 0, 8 * half:8 * half + 8],
                                  psum[0:KEEP, 4 * half:4 * half + 2].rearrange("p a (h k) -> p (a h) k", k=128)).then_inc(pt_ready_v, 1)
                over_sums(1, 1)
                for b in range(B):
                    ve.wait_ge(x1_ps, B * f + b + 1)
                    V.tensor_tensor(x1[:, b], bank(4 * b + 3, 0, D), xs[:, b, 0:D], ALU.add).then_inc(x1_ready, 1)
                for b in range(B):
                    n = B * f + b + 1
                    ve.wait_ge(usq_ready, n)
                    step(V.tensor_scalar(usq[:, b], usq[:, b], 0.044715, 1.0, ALU.mult, ALU.add))
                    V.tensor_tensor(usq[:, b], usq[:, b], bank(4 * b), ALU.mult).then_inc(arg_ready, 1)
                for b in range(B):
                    ve.wait_ge(tanh_ready, B * f + b + 1)
                    V.scalar_tensor_tensor(gel[:, b], th[:, b], 1.0, bank(4 * b), ALU.add, ALU.mult).then_inc(gel_ready, 1)
                for b in range(B):
                    ve.wait_ge(x2_ps, B * f + b + 1)
                    step(V.scalar_tensor_tensor(x2[:, b], bank(4 * b + 3, 0, D), 0.5, x1[:, b], ALU.mult, ALU.add))
                    V.tensor_scalar(proc[:, b], x2[:, b], xs[:, b, AUX_W:AUX_W + 1], 0.5, ALU.mult, ALU.mult).then_inc(proc_ready, 1)
                for b in range(B):
                    ve.wait_ge(y_ps, B * f + b + 1)
                    ve.wait_ge(base_ready, B * f + b + 1)
                    V.tensor_tensor(blocks(xo, b), psum[:, 4 * b:4 * b + 2].rearrange("p a (n d) -> p (a n) d", d=D),
                                    blocks(base, b), ALU.add).then_inc(y_ready, 1)
                    if f == 0:
                        moments(1, b, xo)

            ffn(0)

            ve.wait_ge(loaded_a, 16 * 7)
            for b in range(B):
                ve.wait_ge(rstd_ready, B + b + 1)
                for k in range(NB):
                    last = V.tensor_scalar(xn[:, b * NB + k, 0:D], xb[:, b * NB + k], mv[:, b * NB + k, 0:1],
                                           rstd[:, b, k:k + 1], ALU.subtract, ALU.mult)
                last.then_inc(xn_att_ready, 1)

            def rotate(n):
                which, first = n % 2, PROJ_BANK[n]
                two = psum[:, first:first + 2].rearrange("p a c -> p (a c)")
                turned = psum[:, first + 2:first + 4].rearrange("p a c -> p (a c)")
                ve.wait_ge(proj_ps, n + 1)
                if n >= 2:
                    ve.wait_ge(hi_ready, n - 1)
                    ve.wait_ge(rem_ready, n - 1)
                V.scalar_tensor_tensor(rq[:, n % 2], two, bqk[:, 2 * which:2 * which + 1], rope_c[:, 0], ALU.add, ALU.mult).then_inc(vec_step, 1)
                if n >= 2:
                    ve.wait_ge(mid_ready, n - 1)
                    ve.wait_ge(low_ready, n - 1)
                V.scalar_tensor_tensor(rt[:, n % 2], turned, bqk[:, 2 * which + 1:2 * which + 2], rope_c[:, 1], ALU.add, ALU.mult).then_inc(vec_step, 1)
                step.n += 2
                ve.wait_ge(vec_step, step.n)
                V.tensor_tensor(rq[:, n % 2], rq[:, n % 2], rt[:, n % 2], ALU.add).then_inc(rot_ready, 1)

            def remainder(n):
                ve.wait_ge(rot_ready, n + 1)
                ve.wait_ge(hi_ready, n + 1)
                V.tensor_tensor(rt[:, n % 2], rq[:, n % 2], parts[n % 2][0], ALU.subtract).then_inc(rem_ready, 1)

            def v_biased(b):
                ve.wait_ge(v_ps, b + 1)
                for g in range(GB):
                    last = V.tensor_tensor(
                        v_all[:, b * GB + g].rearrange("p (n e) -> p n e", n=NB),
                        psum[:, V_BANK[b]:V_BANK[b] + 2].rearrange("p a (n e) -> p (a n) e", e=D)[:, :, g * 32:g * 32 + 32],
                        bv[:, g * 32:g * 32 + 32].unsqueeze(1).to_broadcast([128, NB, 32]), ALU.add)
                last.then_inc(v_ready, 1)

            rotate(0)
            rotate(1)
            remainder(0)
            v_biased(0)
            remainder(1)
            rotate(2)
            rotate(3)
            remainder(2)
            v_biased(1)
            remainder(3)

            def tile_max(g, a, first=False):
                j, (i, first_bank, _) = a // NB, TILE_PLAN[a % NB]
                n = 128 * (i + 1)
                ve.wait_ge(tile_ps, g * USES + a + 1)
                if first:
                    first_bank += UPPER * (j % 2)
                    if a >= 3:
                        ve.wait_ge(tile_taken, a - 2)
                ve.sem_inc(tiles_seen, 1)
                V.tensor_tensor_reduce(out=junk_v[:, a % 3, 0:n],
                                       in0=psum[:, first_bank:first_bank + (n + 511) // 512].rearrange("p a c -> p (a c)")[:, 0:n],
                                       in1=diagmask[:, T - n:T], scale=1.0, scalar=-3.0e38,
                                       op0=ALU.add, op1=ALU.max, accum_out=mx[:, j * NB + i:j * NB + i + 1]).then_inc(tile_taken, 1)

            def max_parts(g):
                ps = psum[0:TILES, 0, 0:128]
                ve.wait_ge(tile_ps, g * USES + USES)
                V.tensor_scalar(shift[0:TILES, 0], ps, -1.0, None, ALU.mult).then_inc(shift_step, 1)
                ve.wait_ge(shift_step, g * 2 + 1)
                V.scalar_tensor_tensor(srem[0:TILES], ps, -1.0, shift[0:TILES, 0], ALU.mult, ALU.subtract).then_inc(tile_taken, 1)
                ve.wait_ge(tile_taken, g * USES + USES)
                V.tensor_copy(shift[0:TILES, 1], srem[0:TILES]).then_inc(shift_step, 1)
                ve.wait_ge(shift_step, g * 2 + 2)
                V.tensor_tensor(shift[0:TILES, 2], srem[0:TILES], shift[0:TILES, 1], ALU.subtract).then_inc(shift_ready, 1)

            def normalise(g, h):
                z = psum[:, 6 + h].rearrange("p (n j w) -> p n j w", n=4, j=HG)
                ve.wait_ge(zt_ps, g * 2 + h + 1)
                V.reciprocal(zrec[:, h].rearrange("p (n j) -> p n j", n=4), z[:, :, :, HD]).then_inc(zrec_ready, 1)
                ve.wait_ge(zrec_ready, g * 2 + h + 1)
                dst = o_all[:, g, h * 128:(h + 1) * 128] if isinstance(g, int) else \
                    o_all[:, bass.ds(g, 1), h * 128:(h + 1) * 128].rearrange("p o e -> p (o e)")
                V.tensor_tensor(dst.rearrange("p (n j w) -> p n j w", n=4, j=HG), z[:, :, :, 0:HD],
                                zrec[:, h].rearrange("p (n j) -> p n j", n=4).unsqueeze(3).to_broadcast([128, 4, HG, HD]),
                                ALU.mult).then_inc(pv_free[h], 1)

            for a in range(TILES):
                tile_max(0, a, first=True)
            max_parts(0)
            for a in range(FIRST):
                tile_max(1, a)
            V.memset(zrec[:, 0], 0.0).then_inc(pv_free[0], 1)
            V.memset(zrec[:, 1], 0.0).then_inc(pv_free[1], 1)

            def body(g, has_next, has_second, has_first):
                for what, dg, n, *_ in body_plan(has_next, has_second, has_first):
                    if what == "tile":
                        tile_max(g + dg, n)
                    elif what == "maxt":
                        max_parts(g + dg)
                    elif what == "zt":
                        normalise(g, n)

            with ve.Fori(0, (G - 2) // SETS) as i:
                for s in range(SETS):
                    body(i * SETS + s, True, True, True)
            body(G - 2, True, True, False)
            body(G - 1, False, False, False)

            for b in range(B):
                ve.wait_ge(pv_free[0], G + 1)
                ve.wait_ge(pv_free[1], G + 1)
                V.tensor_copy(o_tok[:, b].rearrange("p n (g e) -> p n g e", g=GB),
                              o_all[:, b * GB:(b + 1) * GB].rearrange("p g (n e) -> p n g e", n=NB)).then_inc(o_tok_ready, 1)
            for b in range(B):
                ve.wait_ge(att_t_ps, b + 1)
                V.tensor_copy(xnt[:, b], psum[:, 4 * b:4 * b + 2].rearrange("p a c -> p (a c)")).then_inc(att_t_ready, 1)
            for b in range(B):
                ve.wait_ge(att_ps, b + 1)
                ve.wait_ge(att_base, b + 1)
                V.tensor_tensor(blocks(xa, b), psum[:, 4 * b + 2:4 * b + 4].rearrange("p a (n d) -> p (a n) d", d=D),
                                blocks(base, b), ALU.add).then_inc(y_ready, 1)
                moments(2, b, xa)
            ffn(1)

        @block.scalar
        def _(ac):
            A = nc.scalar
            step = Step(ac, act_step)

            def ffn(f):
                def squares(k, b, src):
                    A.activation(junk_a[:, B * k + b], src, ACT.Square, accum_out=ssq[:, b, k:k + 1]).then_inc(ssq_ready, 1)

                def normalised(k, b, src):
                    n = 2 * B * f + B * k + b + 1
                    ac.wait_ge(rs_ready, n)
                    A.activation(hn[:, b], src, ACT.Copy, scale=rs[:, b, k:k + 1]).then_inc(hn_ready, 1)
                    ac.wait_ge(ht_ps, n)
                    A.activation(ht[:, b], bank(4 * b + 2, 0, D), ACT.Copy, scale=(ln1, ln2)[k][:, 0:1]).then_inc(ht_ready, 1)

                def weight_rows(b):
                    ac.wait_ge(wrow_ps, B * f + b + 1)
                    A.activation(wrow[:, b], psum[:, 4 * b:4 * b + 2].rearrange("p a c -> p (a c)"), ACT.Copy).then_inc(wrow_ready, 1)

                def rank_rows(b):
                    ac.wait_ge(rrow_ps, B * f + b + 1)
                    A.activation(rrow[:, b], psum[:, 4 * b:4 * b + 2].rearrange("p a c -> p (a c)"), ACT.Copy).then_inc(rrow_ready, 1)

                def gathered(b):
                    n = B * f + b + 1
                    ac.wait_ge(gather_ps, n)
                    A.activation(xs[:, b], bank(4 * b + 3, 0, XW), ACT.Copy).then_inc(xs_ready, 1)
                    ac.wait_ge(xs_ready, n)
                    squares(0, b, xs[:, b, 0:D])

                def values(b):
                    ac.wait_ge(qk_ready, B * f + b + 1)
                    if f == 0 and b == 0:
                        ac.wait_ge(vs_clear, 1)
                    A.activation(vs[:, b, :, 0:HD], bank(4 * b + 2, 2 * D, 3 * D).rearrange("p (h c) -> p h c", h=H),
                                 ACT.Copy).then_inc(vs_ready, 1)

                def mask_rows(b):
                    ac.wait_ge(u_ps, B * f + b + 1)
                    A.activation(umask[:, b].rearrange("p n s -> p (n s)"),
                                 psum[:, 4 * b:4 * b + 2].rearrange("p a c -> p (a c)")[:, 0:(MB + 1) * 128], ACT.Copy).then_inc(u_ready, 1)

                def mask_columns(b):
                    ac.wait_ge(msel_ps, B * f + b + 1)
                    A.activation(msel[:, b], bank(4 * b + 3, 0, D), ACT.Copy).then_inc(msel_ready, 1)

                def normalised_tokens(b):
                    tokens = ffn_tokens[f][0]
                    ac.wait_ge(nmean_ready, B * f + b + 1)
                    for k in range(NB):
                        A.activation(xn[:, b * NB + k, 0:D], tokens[:, b * NB + k], ACT.Identity, bias=nmean[:, b, k:k + 1]).then_inc(act_step, 1)
                    step.n += NB
                    ac.wait_ge(act_step, step.n)
                    ac.wait_ge(rstd_ready, 2 * B * f + b + 1)
                    for k in range(NB):
                        last = A.activation(xn[:, b * NB + k, 0:D], xn[:, b * NB + k, 0:D], ACT.Copy, scale=rstd[:, b, k:k + 1])
                    last.then_inc(xn_ready, 1)

                def keys(b):
                    ac.wait_ge(qkt_ps, B * f + b + 1)
                    for h in range(H // 2, H):
                        last = A.activation(ktm[:, b, h], bank(4 * b + 2, 0, D), ACT.Copy, scale=headmask[:, h:h + 1])
                    last.then_inc(ktm_ready_a, 1)

                def exps(b, half):
                    ac.wait_ge(mx_ready, 2 * (B * f + b) + half + 1)
                    for h in range(8 * half, 8 * half + 8):
                        last = A.activation(prob[:, b, h, 0:KEEP], sc[:, b, h, 0:KEEP], ACT.Exp, bias=nmx[:, b, h:h + 1],
                                            accum_out=rsum[:, b, h:h + 1])
                    last.then_inc(exp_ready, 1)

                normalised_tokens(0)
                weight_rows(0)
                weight_rows(1)
                normalised_tokens(1)
                if f == 0:
                    for k in range(2):
                        ac.wait_ge(angles_ready, k + 1)
                        A.activation(trig[:, 2 * k], red2[:, k], ACT.Sin).then_inc(trig_ready, 1)
                if f == 0:
                    ac.wait_ge(loaded_m, 16 * 2 * B)
                    for b in range(B):
                        A.activation(masks[:, b, :, S_MASK:], masks[:, b, :, S_MASK - 1:S_MASK].to_broadcast([128, MB + 1, 128]),
                                     ACT.Copy).then_inc(mask_wide, 1)
                rank_rows(0)
                gathered(0)
                normalised(0, 0, xs[:, 0, 0:D])
                rank_rows(1)
                gathered(1)
                values(0)
                normalised(0, 1, xs[:, 1, 0:D])
                mask_rows(0)
                mask_columns(0)
                values(1)
                keys(0)
                mask_rows(1)
                mask_columns(1)
                exps(0, 0)
                keys(1)
                exps(0, 1)
                exps(1, 0)
                exps(1, 1)
                ac.wait_ge(slots_ready, B * (f + 1))
                ac.wait_ge(drop_ready, B * (f + 1))

                def outputs(b):
                    ac.wait_ge(o_ps, B * f + b + 1)
                    A.activation(ot[:, b], bank(4 * b + 2), ACT.Copy).then_inc(ot_ready, 1)

                def turned(half):
                    ac.wait_ge(pt_ps, 2 * (B * f + 1) + half + 1)
                    A.activation(ktm[0:KEEP, 1, 8 * half:8 * half + 8],
                                 psum[0:KEEP, 4 * half:4 * half + 2].rearrange("p a (h k) -> p (a h) k", k=128), ACT.Copy).then_inc(pt_ready_a, 1)

                def squares_of_sum(b):
                    ac.wait_ge(x1_ready, B * f + b + 1)
                    squares(1, b, x1[:, b])

                turned(0)
                outputs(0)
                turned(1)
                squares_of_sum(0)
                outputs(1)
                normalised(1, 0, x1[:, 0])
                squares_of_sum(1)

                def hidden_squares(b):
                    ac.wait_ge(hid_ps, B * f + b + 1)
                    A.activation(usq[:, b], bank(4 * b), ACT.Square).then_inc(usq_ready, 1)

                hidden_squares(0)
                normalised(1, 1, x1[:, 1])
                hidden_squares(1)
                for b in range(B):
                    ac.wait_ge(arg_ready, B * f + b + 1)
                    A.activation(th[:, b], usq[:, b], ACT.Tanh, scale=float(np.sqrt(2.0 / np.pi))).then_inc(tanh_ready, 1)

            ffn(0)

            ac.wait_ge(y_ready, B)
            def ones(s):
                A.activation(k_set[:, s].rearrange("p j t -> p (j t)"), ones_bf[:, 0:1].to_broadcast([128, HG * T]),
                             ACT.Copy).then_inc(ones_ready, 1)
            ones(0)
            for b in range(B):
                ac.wait_ge(xnt_ps, b + 1)
                A.activation(xnt[:, b], psum[:, 4 + 2 * b:6 + 2 * b].rearrange("p a c -> p (a c)"), ACT.Copy).then_inc(xnt_ready, 1)
            for s in range(1, SETS):
                ones(s)

            def high(n):
                ac.wait_ge(rot_ready, n + 1)
                if n >= 2:
                    ac.wait_ge(parts_stored[n % 2], 16 * PARTS)
                A.activation(parts[n % 2][0], rq[:, n % 2], ACT.Copy).then_inc(hi_ready, 1)

            def middle(n):
                ac.wait_ge(rem_ready, n + 1)
                A.activation(parts[n % 2][1], rt[:, n % 2], ACT.Copy).then_inc(mid_ready, 1)

            high(0)
            high(1)
            middle(0)
            middle(1)
            high(2)
            high(3)
            middle(2)
            middle(3)

            def exps(g, c, j):
                e = g * (NC * HG) + (HG * c + j)
                ac.wait_ge(st_ps, e + 1)
                if j == 0:
                    ac.wait_ge(prob_free, g * NC + (c + 1))
                A.activation(p_buf[:, c % 3, j], bank(4 + j % 2), ACT.Exp, scale=SCALE).then_inc(exp_done, 1)

            def evacuate(g, h):
                if h == 0:
                    ac.wait_ge(half_done, g + 1)
                else:
                    ac.wait_ge(prob_free, g * NC + NC + 3)
                A.activation(z_buf[:, h], bank(6 + h), ACT.Copy).then_inc(z_ready, 1)

            for half in parts_stored:
                ac.wait_ge(half, 16 * PARTS * B)
            for c in range(2):
                for j in range(HG):
                    exps(0, c, j)

            def body(g, has_next, has_second, has_first):
                for what, dg, n, *j in body_plan(has_next, has_second, has_first):
                    if what == "st":
                        exps(g + dg, n, j[0])
                    elif what == "evac":
                        evacuate(g, n)

            with ac.Fori(0, (G - 2) // SETS) as i:
                for s in range(SETS):
                    body(i * SETS + s, True, True, True)
            body(G - 2, True, True, False)
            body(G - 1, False, False, False)

            ffn(1)

        @block.tensor
        def _(pe):
            M = nc.tensor

            def mm(out, w, m, start=True, stop=True):
                return M.matmul(out, w, m, start=start, stop=stop)

            def ffn(f):
                for b in range(B):
                    pe.wait_ge(wcol_ready, B * f + b + 1)
                    for k in range(NB):
                        last = M.transpose(bank(4 * b + k // 4, 128 * (k % 4), 128 * (k % 4) + 128),
                                           wcol[:, b, k:k + 1].to_broadcast([128, 128]), ident[:])
                    last.then_inc(wrow_ps, 1)

                def ranks(b, ks):
                    cols = bank(4 * b + 2)
                    if 0 in ks:
                        mm(cols[:, 0:NB], ones_bf[:], diagmask[:, 0:NB], stop=False)
                    for k in ks:
                        pe.wait_ge(cmp_ready, NB * (B * f + b) + k + 1)
                        for i in range(k, NB):
                            at = CMP_AT[k] + 128 * (i - k)
                            last = mm(cols[:, i:i + 1], cmp[:, b, at:at + 128], ones_bf[:, 0:1], start=False, stop=(k == NB - 1))
                        if k == NB - 1:
                            last.then_inc(rank_ps, 1)
                        for h in range(k // MB, 2):
                            lo = max(128 * k, 512 * h)
                            at = CMP_AT[k] + lo - 128 * k
                            mm(bank(4 * b + h, lo - 512 * h, 512), ones_bf[:], cmp[:, b, at:at + 512 * (h + 1) - lo],
                               start=(k == 0), stop=False)

                def rank_rows(b):
                    pe.wait_ge(before_ready, B * f + b + 1)
                    for k in range(NB):
                        last = mm(bank(4 * b + k // 4, 128 * (k % 4), 128 * (k % 4) + 128),
                                  before_row[:, b, k:k + 1].to_broadcast([128, 128]), ident[:], start=False, stop=(k % 4 == 3))
                    last.then_inc(rrow_ps, 1)

                def gather(b):
                    n = B * f + b + 1
                    pe.wait_ge(slots_t_ready, n)
                    pe.wait_ge(aux_w, n)
                    if f == 0:
                        pe.wait_ge(aux_trig, 2 * B)
                    for k in range(NB):
                        last = mm(bank(4 * b + 3, 0, XW), slots_t[:, b, k], xn[:, b * NB + k, :], start=(k == 0), stop=(k == NB - 1))
                    last.then_inc(gather_ps, 1)

                def normed_t(k, b):
                    pe.wait_ge(hn_ready, 2 * B * f + B * k + b + 1)
                    M.transpose(bank(4 * b + 2, 0, D), hn[:, b], ident[:]).then_inc(ht_ps, 1)

                def qkv(b):
                    pe.wait_ge(ht_ready, 2 * B * f + b + 1)
                    mm(bank(4 * b + 2, 0, 3 * D), ht[:, b], fqkv[:]).then_inc(qkv_ps, 1)

                def mask_rows(b, cs):
                    n = B * f + b + 1
                    pe.wait_ge(clamp_ready, n)
                    pe.wait_ge(rrow_ready, n)
                    for c in cs:
                        for k in range(MB + 1):
                            last = mm(bank(4 * b + c // 4, 128 * (c % 4), 128 * (c % 4) + 128),
                                      masks[:, b, k, 128 * c:128 * c + 128], slots_t[:, b, k if k < MB else NB],
                                      start=(k == 0), stop=(k == MB))
                    if MB in cs:
                        last.then_inc(u_ps, 1)

                if f == 0:
                    pe.wait_ge(consts_ready, 1)
                ranks(0, range(NB))
                rank_rows(0)
                ranks(1, range(2))
                if f == 0:
                    pe.wait_ge(loaded_f, 16 * 8)
                gather(0)
                ranks(1, range(2, 4))
                if f == 0:
                    pe.wait_ge(mask_wide, B)
                mask_rows(0, range(2))
                ranks(1, range(4, NB))
                normed_t(0, 0)
                gather(1)
                rank_rows(1)
                qkv(0)
                mask_rows(0, range(2, MB + 1))
                def mask_columns(b):
                    n = B * f + b + 1
                    pe.wait_ge(u_ready, n)
                    pe.wait_ge(xs_ready, n)
                    for k in range(MB + 1):
                        last = mm(bank(4 * b + 3, 0, D), umask[:, b, k], slots_t[:, b, k if k < MB else NB],
                                  start=(k == 0), stop=(k == MB))
                    last.then_inc(msel_ps, 1)

                def turned(b):
                    n = B * f + b + 1
                    pe.wait_ge(qk_ready, n)
                    pe.wait_ge(msel_ready, n)
                    pe.wait_ge(vs_ready, n)
                    M.transpose(bank(4 * b + 3, 0, D), qk[:, b, 0:D], ident[:])
                    M.transpose(bank(4 * b + 3, D, 2 * D), qk[:, b, D:2 * D], ident[:])
                    M.transpose(bank(4 * b + 2, 0, D), qk[:, b, D:2 * D], ident[:]).then_inc(qkt_ps, 1)

                def scores(b, half):
                    if half == 0:
                        pe.wait_ge(qkt_ready, B * f + b + 1)
                        pe.wait_ge(u_ready, B * f + 1)
                    else:
                        pe.wait_ge(ktm_ready_a, B * f + b + 1)
                        pe.wait_ge(u_ready, B * f + 2)
                    if b:
                        pe.wait_ge(sc_taken, 2 * B * f + half + 1)
                    for q in range(2):
                        h = 8 * half + 4 * q
                        last = mm(bank(4 * half + q), qt[:, b], ktm[:, b, h:h + 4].rearrange("p h k -> p (h k)"))
                    last.then_inc(sc_ps, 1)

                normed_t(0, 1)
                mask_rows(1, range(2))
                qkv(1)
                mask_columns(0)
                mask_rows(1, range(2, 3))
                turned(0)
                mask_rows(1, range(3, MB + 1))
                scores(0, 0)
                mask_columns(1)
                scores(0, 1)
                turned(1)
                scores(1, 0)
                scores(1, 1)

                def prob_turned(b, half):
                    if (b, half) == (B - 1, 1):
                        pe.wait_ge(last_norm_ready, f + 1)
                    else:
                        pe.wait_ge(norm_ready, (2 * B - 1) * f + 2 * b + half + 1)
                    if b:
                        pe.wait_ge(pt_ready_v, 2 * f + half + 1)
                    else:
                        pe.wait_ge(sc_taken, 2 * (B * f + 1) + half + 1)
                    for q in range(8):
                        last = M.transpose(psum[0:KEEP, 4 * half + q // 4, 128 * (q % 4):128 * (q % 4) + 128],
                                           prob[:, b, 8 * half + q, 0:KEEP], ident[:])
                    last.then_inc(pt_ps, 1)

                def outputs(b):
                    pe.wait_ge((pt_ready_v, pt_ready_a)[b], 2 * (f + 1))
                    for h in range(H):
                        j = h % HG
                        last = mm(psum[32 * j:32 * j + 32, 4 * b + 2, 128 * (h // HG):128 * (h // HG) + 128],
                                  vs[0:KEEP, b, h], ktm[0:KEEP, b, h])
                    last.then_inc(o_ps, 1)

                def project(b):
                    pe.wait_ge(ot_ready, B * f + b + 1)
                    for g in range(GB):
                        last = mm(bank(4 * b + 3, 0, D), ot[:, b, 128 * g:128 * g + 128], fwo[:, g], start=(g == 0), stop=(g == GB - 1))
                    last.then_inc(x1_ps, 1)

                def hidden(b):
                    pe.wait_ge(ht_ready, 2 * B * f + B + b + 1)
                    for k in range(FB):
                        last = mm(bank(4 * b, 128 * k, 128 * k + 128), fw1[:, 128 * k:128 * k + 128], ht[:, b])
                    last.then_inc(hid_ps, 1)

                prob_turned(0, 0)
                prob_turned(0, 1)
                prob_turned(1, 0)
                outputs(0)
                prob_turned(1, 1)
                project(0)
                outputs(1)
                normed_t(1, 0)
                project(1)
                hidden(0)
                normed_t(1, 1)
                hidden(1)
                for b in range(B):
                    pe.wait_ge(gel_ready, B * f + b + 1)
                    for k in range(FB):
                        last = mm(bank(4 * b + 3, 0, D), gel[:, b, 128 * k:128 * k + 128], fw2[:, k], start=(k == 0), stop=(k == FB - 1))
                    last.then_inc(x2_ps, 1)
                for b in range(B):
                    n = B * f + b + 1
                    pe.wait_ge(proc_ready, n)
                    pe.wait_ge(slots_ready, n)
                    for k in range(NB):
                        last = mm(bank(4 * b + k // 4, 128 * (k % 4), 128 * (k % 4) + 128),
                                  slots[0:KEEP, b, 128 * k:128 * k + 128], proc[0:KEEP, b])
                    last.then_inc(y_ps, 1)

            pe.wait_ge(ident_ready, 1)
            ffn(0)
            pe.wait_ge(loaded_a, 16 * 7)

            for b in range(B):
                pe.wait_ge(xn_att_ready, b + 1)
                if b == 0:
                    pe.wait_ge(y_ready, B)
                for k in range(NB):
                    last = M.transpose(bank(4 + 2 * b + k // 4, 128 * (k % 4), 128 * (k % 4) + 128), xn[:, b * NB + k, 0:D], ident[:])
                last.then_inc(xnt_ps, 1)

            def project(n):
                b, which = divmod(n, 2)
                for w in range(2):
                    for h in range(2):
                        last = mm(bank(PROJ_BANK[n] + 2 * w + h), wqk[:, 2 * which + w], xnt[:, b, 512 * h:512 * h + 512])
                last.then_inc(proj_ps, 1)

            def project_v(b):
                for k in range(NB):
                    last = mm(bank(V_BANK[b] + k // 4, 128 * (k % 4), 128 * (k % 4) + 128), xnt[:, b, 128 * k:128 * k + 128], wv[:])
                last.then_inc(v_ps, 1)

            pe.wait_ge(xnt_ready, 1)
            project(0)
            pe.wait_ge(xnt_ready, 2)
            project(1)
            pe.wait_ge(rot_ready, 1)
            project_v(0)
            pe.wait_ge(rot_ready, 2)
            project(2)
            pe.wait_ge(v_ready, 1)
            project(3)
            pe.wait_ge(rot_ready, 3)
            project_v(1)

            def score_tile(g, s, a, first=False):
                j, (i, first_bank, lag) = a // NB, TILE_PLAN[a % NB]
                if first:
                    first_bank += UPPER * (j % 2)
                    if a % NB < lag:
                        lag += NB
                if a == 0:
                    pe.wait_ge(set_loaded[s], (g // SETS + 1) * LOADS if isinstance(g, int) else turn(g, s) * LOADS)
                before = max(a - lag + 1, 0)
                if not (first and before == 0):
                    pe.wait_ge(tile_taken, g * USES + before)
                n = 128 * (i + 1)
                for lo in range(0, n, 512):
                    hi = min(n, lo + 512)
                    last = mm(bank(first_bank + lo // 512, 0, hi - lo), q_set[0:SHIFT, s, j, 128 * i:128 * i + 128],
                              k_set[0:SHIFT, s, j, lo:hi])
                last.then_inc(tile_ps, 1)

            def transpose_max(g):
                pe.wait_ge(tile_taken, g * USES + TILES)
                M.transpose(psum[0:TILES, 0, 0:128], mx[:, 0:TILES], ident[:]).then_inc(tile_ps, 1)

            def score_chunk(g, s, c, j, first=False):
                if c == 0 and j == 0:
                    pe.wait_ge(shift_loaded[s], (g // SETS + 1) * SHIFTS if isinstance(g, int) else turn(g, s) * SHIFTS)
                if not (first and c == 0 and j < 2):
                    pe.wait_ge(exp_done, g * (NC * HG) + (HG * c + j - 1))
                at = 0
                for kb, q0, w in CHUNKS[c]:
                    last = mm(bank(4 + j % 2, at, at + w), k_set[:, s, j, 128 * kb:128 * kb + 128], q_set[:, s, j, q0:q0 + w])
                    at += w
                last.then_inc(st_ps, 1)

            def values(g, s, c, part_of):
                if part_of == 0:
                    if c == 0:
                        pe.wait_ge(v_set_ready, g + 1)
                    if c < 2:
                        pe.wait_ge(pv_free[c], g + 1)
                    if DIAG[c]:
                        pe.wait_ge(diag_done, g * len(DIAG_CHUNKS) + (DIAG_CHUNKS.index(c) + 1))
                    else:
                        pe.wait_ge(exp_done, g * (NC * HG) + HG * (c + 1))
                at = 0
                for n, (kb, q0, w) in enumerate(CHUNKS[c]):
                    h = q0 // 512
                    lo, hi = max(at, 256 * part_of), min(at + w, 256 * part_of + 256)
                    if lo < hi:
                        q = q0 % 512 + lo - at
                        ends = c == HALF_END[h] and (hi == 512 or CHUNKS[c][n][1] // 512 != CHUNKS[c][-1][1] // 512)
                        for j in range(HG):
                            last = M.matmul(psum[32 * j:32 * j + 32, 6 + h, q:q + hi - lo], v_set[:, s, kb, j],
                                            p_buf[:, c % 3, j, lo:hi], start=(c == h and part_of == 0), stop=ends)
                        if ends and h == 0:
                            last.then_inc(half_done, 1)
                    at += w
                if part_of == 1:
                    last.then_inc(prob_free, 1)

            def outputs_t(g, h):
                pe.wait_ge(z_ready, g * 2 + h + 1)
                for k in range(4):
                    last = M.transpose(bank(6 + h, 128 * k, 128 * k + 128), z_buf[:, h, 128 * k:128 * k + 128], ident[:])
                last.then_inc(zt_ps, 1)

            pe.wait_ge(rot_ready, 2 * B)
            for a in range(TILES):
                if a == NB:
                    pe.wait_ge(v_ready, B)
                score_tile(0, 0, a, first=True)
            transpose_max(0)
            M.transpose(psum[0:TILES, 7, 0:128], ident[:, 0:TILES], ident[:]).then_inc(prob_free, 3)
            ahead = FIRST - 2 * HG
            for a in range(ahead):
                score_tile(1, 1, a)
            for n in range(2 * HG):
                score_tile(1, 1, ahead + n)
                score_chunk(0, 0, n // HG, n % HG, first=True)
            values(0, 0, 0, 0)

            def body(g, s, has_next, has_second, has_first):
                for what, dg, n, *j in body_plan(has_next, has_second, has_first):
                    if what == "tile":
                        score_tile(g + dg, (s + dg) % SETS, n)
                    elif what == "maxt":
                        transpose_max(g + dg)
                    elif what == "st":
                        score_chunk(g + dg, (s + dg) % SETS, n, j[0])
                    elif what == "pv":
                        values(g + dg, (s + dg) % SETS, n, j[0])
                    elif what == "zt":
                        outputs_t(g, n)

            turn = None
            with pe.Fori(0, (G - 2) // SETS) as i:
                for s in range(SETS):
                    def turn(gg, t, s=s, i=i):
                        return i + (1 if t >= s else 2)
                    body(i * SETS + s, s, True, True, True)
            body(G - 2, (G - 2) % SETS, True, True, False)
            body(G - 1, (G - 1) % SETS, False, False, False)

            for b in range(B):
                pe.wait_ge(o_tok_ready, b + 1)
                for k in range(NB):
                    last = M.transpose(bank(4 * b + k // 4, 128 * (k % 4), 128 * (k % 4) + 128), o_tok[:, b, k], ident[:])
                last.then_inc(att_t_ps, 1)
            for b in range(B):
                pe.wait_ge(att_t_ready, b + 1)
                for k in range(NB):
                    last = mm(bank(4 * b + 2 + k // 4, 128 * (k % 4), 128 * (k % 4) + 128), xnt[:, b, 128 * k:128 * k + 128], wo[:])
                last.then_inc(att_ps, 1)
            ffn(1)


LOADS = 16 * 2 * PARTS
SHIFTS = 16 * PARTS


def kernel(**inputs):
    import concourse.bacc as bacc
    from concourse.bass_utils import run_bass_kernel_spmd

    a = {k: np.asarray(v) for k, v in inputs.items()}
    f32 = np.float32

    def turned(w, rotated):
        w = w.reshape(GB, HG, HD, -1)
        if rotated:
            w = np.roll(w, -HALF, axis=2)
        return w.transpose(0, 2, 1, 3).reshape(D, -1)

    wqk = np.stack([turned(a["L0_attn_" + n], r).T for n in ("Wq", "Wk") for r in (False, True)], axis=1)
    bqk = np.concatenate([turned(a["L0_attn_" + n], r) for n in ("bq", "bk") for r in (False, True)], axis=1)
    inv = (1.0 / (np.float32(10000.0) ** (np.arange(0, HD, 2, dtype=f32) / f32(HD)))).astype(f32)
    ang = (np.arange(T, dtype=f32)[:, None] * inv[None, :]).astype(f32)
    ang = np.concatenate([ang, ang], axis=1).astype(np.float64)
    sign = np.where(np.arange(HD) < HALF, -1.0, 1.0)
    rope = np.stack([np.cos(ang).T, (np.sin(ang) * sign).T]).astype(f32)
    rope = np.tile(np.repeat(rope, HG, axis=1), (1, GB, 1)).transpose(1, 0, 2)
    p = "L0_ffn_"
    fwo = np.zeros((HG, VW, GB, D), f32)
    fwo[:, :HD] = a[p + "wo"].reshape(GB, HG, HD, D).transpose(1, 2, 0, 3)
    fwo = fwo.reshape(HG * VW, GB, D)
    pos = a[p + "position_ids"][:B]
    pos = np.concatenate([pos.reshape(B, MB, 128), np.broadcast_to(pos[:, -1:, None], (B, 1, 128))], axis=1).transpose(2, 0, 1)
    sent = [
        ("x", a["L0_attn_x"]), ("masks", a[p + "attention_mask"]), ("pos", pos),
        ("rw", a[p + "router_w"]), ("rb", a[p + "router_b"]), ("fwq", a[p + "wq"]), ("fwk", a[p + "wk"]),
        ("fwv", a[p + "wv"]), ("fwo", fwo), ("fw1", a[p + "w1"]), ("fw2", a[p + "w2"]),
        ("ln1", a[p + "ln1"]), ("ln2", a[p + "ln2"]), ("wqk", wqk), ("bqk", bqk), ("wv", a["L0_attn_Wv"].T),
        ("bv", a["L0_attn_bv"]), ("wo", a["L0_attn_Wo"].T), ("bo", a["L0_attn_bo"]), ("rope", rope), ("invf", inv),
    ]
    nc = bacc.Bacc("TRN2", target_bir_lowering=False, num_devices=1)
    arrays, args = {}, []
    for name, value in sent:
        v = np.ascontiguousarray(value)
        arrays[f"in_{name}"] = v
        args.append(nc.dram_tensor(f"in_{name}", v.shape, mybir.dt.from_np(v.dtype), kind="ExternalInput").ap())
    args.append(nc.dram_tensor("out", (B, T, D), mybir.dt.float32, kind="ExternalOutput").ap())
    build(nc, *args)
    r = run_bass_kernel_spmd(nc, [arrays], core_ids=[0])
    return r.results[0]["out"]
```

```python
from contextlib import ExitStack

import numpy as np

import concourse.bass as bass
from concourse import mybir

B, T, D, H = 2, 1024, 128, 16
HD = D // H
NB = T // 128
S_MASK = 512
MB = S_MASK // 128
F = 512
FB = F // 128
KEEP = int(0.125 * T) - 1
HALF = HD // 2
SCALE = float(1.0 / np.sqrt(HD))
LN_EPS, RMS_EPS = 1e-5, 1e-6

AUX_COS, AUX_NSIN, AUX_SIN, AUX_W = D, D + HALF, D + 2 * HALF, D + 3 * HALF
XW = AUX_W + 1

HG = 4
GB = H // HG
G = B * GB
PARTS = 3
STACK = PARTS * PARTS * HD
SHIFT = 128 - PARTS
SETS = 3
VW = 32
NEG = -1.0e30

CHUNKS = [[(0, 0, 512)], [(0, 512, 512)], [(1, 128, 384), (3, 384, 128)], [(2, 256, 256), (6, 768, 256)],
          [(1, 512, 512)], [(2, 512, 512)], [(3, 512, 512)], [(4, 512, 512)], [(5, 640, 384), (7, 896, 128)]]
NC = len(CHUNKS)
CMP_AT = [sum(T - 128 * i for i in range(k)) for k in range(NB + 1)]
DIAG = []
for _pieces in CHUNKS:
    _at, _starts = 0, []
    for _kb, _q0, _w in _pieces:
        if _kb * 128 == _q0:
            _starts.append(_at)
        _at += _w
    DIAG.append(_starts)
DIAG_CHUNKS = [c for c in range(NC) if DIAG[c]]
HALF_END = [3, NC - 1]
TILE_PLAN = [(7, 0, 2), (0, 2, 2), (1, 3, 3), (6, 0, 3), (5, 2, 2), (2, 0, 2), (3, 1, 3), (4, 2, 3)]
TILES = HG * NB
USES = TILES + 1
PROJ_BANK = [0, 4, 4, 0]
V_BANK = [0, 4]
MAX_BANK = 2
PAUSE = 2
FIRST = 16


def head_and_tile(a, first):
    if not first:
        return a // NB, TILE_PLAN[a % NB]
    pair, n = divmod(a, 2 * NB)
    i, bank, lag = TILE_PLAN[n // 2]
    return 2 * pair + n % 2, (i, bank + 4 * (n % 2), 2 * lag)


def body_plan(has_next, has_second, has_first):
    tiles = []
    if has_second:
        tiles += [("tile", 1, a) for a in range(FIRST, TILES)] + [("none", 1, 0)] * PAUSE + [("maxt", 1, 0)]
    if has_first:
        tiles += [("tile", 2, a) for a in range(FIRST)]
    plan, done = [], 0
    last = not has_next
    n_pos = NC * HG if has_first else NC * HG // 2
    for n in range(2, NC + 2):
        for j in range(HG):
            if n < NC or has_next:
                plan.append(("st", n // NC, n % NC, j))
            if j == 1 and n - 2 < NC:
                plan.append(("pv", 0, n - 2, 1))
            if j == 3 and (n - 1 < NC or has_next):
                plan.append(("pv", (n - 1) // NC, (n - 1) % NC, 0))
            if (n, j) == (5, 1):
                plan.append(("evac", 0, 0))
            if (n, j) == (NC + 1, 2):
                plan.append(("evac", 0, 1))
            if (n, j) == (6, 2):
                plan.append(("zt", 0, 0))
            if last and j == 0 and n in (3, 4, 5):
                plan.append((("o_tok", "o_turn", "o_proj")[n - 3], 0, 0))
            upto = min(len(tiles), ((n - 2) * HG + j + 1) * len(tiles) // n_pos)
            plan += tiles[done:upto]
            done = upto
    plan.append(("zt", 0, 1))
    return plan


def build(nc, x_d, masks_d, pos_d, rw_d, rb_d, fwq_d, fwk_d, fwv_d, fwo_d, fw1_d, fw2_d, ln1_d, ln2_d,
          wqk_d, bqk_d, wv_d, bv_d, wo_d, bo_d, rope_d, invf_d, out_d):
    f32, bf16, i32 = mybir.dt.float32, mybir.dt.bfloat16, mybir.dt.int32
    ACT, ALU, AX = mybir.ActivationFunctionType, mybir.AluOpType, mybir.AxisListType

    ctx = ExitStack()
    with ctx:
        def sb(name, shape, dt=f32):
            return ctx.enter_context(nc.sbuf_tensor(name, shape, dt))

        def sem(name):
            return ctx.enter_context(nc.semaphore(name))

        psum = ctx.enter_context(nc.psum_tensor("psum", [128, 8, 512], f32))

        def bank(n, lo=0, hi=512):
            return psum[:, n, lo:hi]

        ident = sb("ident", [128, 128])
        later = sb("later", [128, T], bf16)
        from_last = sb("from_last", [128, NB])
        iota_row = sb("iota_row", [128, 128])
        headmask = sb("headmask", [128, H])
        ones_bf = sb("ones_bf", [128, 128], bf16)
        neghalf = sb("neghalf", [128, NB])
        diagmask = sb("diagmask", [128, T], bf16)
        rope_c = sb("rope_c", [128, 2, T])
        invf = sb("invf", [128, HALF])
        rw = sb("rw", [128, D])
        rb = sb("rb", [128, 1])
        fqkv = sb("fqkv", [128, 3 * D])
        fwo = sb("fwo", [128, GB, D])
        fw1 = sb("fw1", [128, F])
        fw2 = sb("fw2", [128, FB, D])
        ln1 = sb("ln1", [128, 1])
        ln2 = sb("ln2", [128, 1])
        wqk = sb("wqk", [128, 4, D])
        bqk = sb("bqk", [128, 4])
        wv = sb("wv", [128, D])
        bv = sb("bv", [128, D])
        wo = sb("wo", [128, D])
        bo = sb("bo", [128, D])
        masks = sb("masks", [128, B, MB + 1, S_MASK + 128])
        pos_i = sb("pos_i", [128, B, MB + 1], i32)
        vs = sb("vs", [128, B, H, VW])
        xa = sb("xa", [128, B * NB, D])
        xb = sb("xb", [128, B * NB, D])
        xn = sb("xn", [128, B * NB, XW])
        base = sb("base", [128, B * NB, D])
        stats = sb("stats", [128, B * NB, 6])
        mv = sb("mv", [128, B * NB, 2])
        veps = sb("veps", [128, B, NB])
        nmean = sb("nmean", [128, B, NB])
        rstd = sb("rstd", [128, B, NB])
        wcol = sb("wcol", [128, B, NB])
        at_rank = sb("at_rank", [128, B, NB])
        quarter_w = sb("quarter_w", [128, B])
        thr_part = sb("thr_part", [128, B])
        ones_col = sb("ones_col", [128, 1])
        past = sb("past", [128, B, NB])
        drop = sb("drop", [128, B, NB])
        rcol = sb("rcol", [128, B, NB])
        after = sb("after", [128, B, NB])
        later_first = sb("later_first", [128, B, NB])
        dot = sb("dot", [128, B, NB])
        scr = sb("scr", [128, T])
        xs = sb("xs", [128, B, XW + 1])
        ssq = sb("ssq", [128, B, 2])
        ms = sb("ms", [128, B, 2])
        rs = sb("rs", [128, B, 2])
        nmx = sb("nmx", [128, B, H])
        rsum = sb("rsum", [128, B, H])
        rrec = sb("rrec", [128, B, H])

        NA = B * (MB + 1) * HALF
        posf, ang, turns, red = (sb(n, [128, NA]) for n in ("posf", "ang", "turns", "red"))
        trig = sb("trig", [128, 3, NA])
        red2 = sb("red2", [128, 2, NA])

        ARENA = 28672
        arena = sb("arena", [128, ARENA])
        taken = {"ffn": 0, "att": 0}

        def part(who, shape, dt=f32):
            n = int(np.prod(shape))
            words = n if dt == f32 else n // 2
            at = taken[who]
            taken[who] = at + words
            assert taken[who] <= ARENA, (who, taken)
            ap = arena[:, at:at + words]
            if dt != f32:
                ap = ap.bitcast(dt)
            if len(shape) == 2:
                ap = ap.rearrange("p (a b) -> p a b", a=shape[0])
            if len(shape) == 3:
                ap = ap.rearrange("p (a b c) -> p a b c", a=shape[0], b=shape[1])
            if len(shape) == 4:
                ap = ap.rearrange("p (a b c d) -> p a b c d", a=shape[0], b=shape[1], c=shape[2])
            return ap

        ktm = part("ffn", [B, H, 128])
        slots = part("ffn", [B, T])
        slots_t = part("ffn", [B, NB + 1, 128])
        cmp_at = taken["ffn"]
        cmp = part("ffn", [B, CMP_AT[NB]], bf16)
        cmp_end = taken["ffn"]
        taken["ffn"] = cmp_at
        sc = part("ffn", [B, H, 128])
        taken["ffn"] = max(taken["ffn"], cmp_end)
        umask = part("ffn", [B, MB + 1, 128])
        prob = part("ffn", [B, H, 128])
        ra = part("ffn", [B, 2 * H, 2, HALF])
        rbuf = part("ffn", [B, 2 * H, 2, HALF])
        qk = part("ffn", [B, 2 * D])
        qt = part("ffn", [B, D])
        msel = part("ffn", [B, D])
        x1 = part("ffn", [B, D])
        x1w = part("ffn", [B, D])
        proc = part("ffn", [B, D])
        junk_a = part("ffn", [2 * B, D])
        rows_at = taken["ffn"]
        wrow = part("ffn", [B, T])
        taken["ffn"] = rows_at
        ot = part("ffn", [B, GB * 128])
        usq = part("ffn", [B, F])
        th = part("ffn", [B, F])
        gel = part("ffn", [B, F])
        hn = part("ffn", [B, D])
        ht = part("ffn", [B, D])

        q_set = part("att", [SETS, HG, T], bf16)
        k_set = part("att", [SETS, HG, T], bf16)
        v_all = part("att", [G, NB * HG * HD])
        v_set = part("att", [SETS, NB, HG, VW])
        p_at = taken["att"]
        p_buf = part("att", [3, HG, 512])
        p_end = taken["att"]
        taken["att"] = p_at
        xnt = part("att", [B, T])
        p0 = part("att", [PARTS, T], bf16)
        rq = part("att", [2, T])
        assert taken["att"] <= p_end
        taken["att"] = p_end
        o_all = part("att", [G, NB * HG * HD])
        z_buf = part("att", [2, 512])
        zrec = part("att", [2, 16])
        mx = part("att", [1, TILES])[:, 0]
        shift = part("att", [PARTS, 128], bf16)
        srem = part("att", [1, 128])[:, 0]
        junk_v = part("att", [3, T], bf16)
        o_tok = q_set[:, 2].rearrange("p j t -> p (j t)").bitcast(f32).rearrange("p (b n d) -> p b n d", b=B, n=NB)
        o_turned = k_set[:, 2].rearrange("p j t -> p (j t)").bitcast(f32).rearrange("p (b t) -> p b t", b=B)
        parts = [[p0[:, p] for p in range(PARTS)],
                 [z_buf[:, 0].bitcast(bf16), z_buf[:, 1].bitcast(bf16), scr[:, 0:T // 2].bitcast(bf16)]]
        rt = xa[:, 0:2 * NB].rearrange("p n d -> p (n d)").rearrange("p (two t) -> p two t", two=2)

        qk_scr = [nc.dram_tensor(f"{n}_parts", (G, PARTS * HD, HG * T), bf16, kind="Internal").ap() for n in ("q", "k")]

        loaded_x, loaded_r = [sem(f"loaded_x{b}") for b in range(B)], sem("loaded_r")
        loaded_p = sem("loaded_p")
        loaded_f, loaded_m, loaded_a = sem("loaded_f"), sem("loaded_m"), sem("loaded_a")
        pool_step, vec_step, act_step = sem("pool_step"), sem("vec_step"), sem("act_step")
        ident_ready, consts_ready = sem("ident_ready"), sem("consts_ready")
        angles_ready, trig_ready, aux_trig = sem("angles_ready"), sem("trig_ready"), sem("aux_trig")
        mask_wide = sem("mask_wide")
        xn_att_ready = sem("xn_att_ready")
        veps_ready, rstd_ready, xn_ready = sem("veps_ready"), sem("rstd_ready"), sem("xn_ready")
        vs_clear, half_done = sem("vs_clear"), sem("half_done")
        rrec_ready, norm_ready, last_norm_ready = sem("rrec_ready"), sem("norm_ready"), sem("last_norm_ready")
        nmean_ready = sem("nmean_ready")
        wcol_ready, aux_w, wrow_ps = sem("wcol_ready"), sem("aux_w"), sem("wrow_ps")
        wrow_ready, dot_ready = sem("wrow_ready"), sem("dot_ready")
        cmp_ready, rank_ps = sem("cmp_ready"), sem("rank_ps")
        before_ready, thr_part_ready, past_ready = sem("before_ready"), sem("thr_part_ready"), sem("past_ready")
        slots_ps = sem("slots_ps")
        drop_ready, slots_ready = sem("drop_ready"), sem("slots_ready")
        slots_t_ready, clamp_ready, gather_ps = sem("slots_t_ready"), sem("clamp_ready"), sem("gather_ps")
        xs_ready, ssq_ready, rs_ready = sem("xs_ready"), sem("ssq_ready"), sem("rs_ready")
        hn_ready, ht_ps, ht_ready = sem("hn_ready"), sem("ht_ps"), sem("ht_ready")
        u_ps, u_ready, msel_ps, msel_ready = sem("u_ps"), sem("u_ready"), sem("msel_ps"), sem("msel_ready")
        qkv_ps, qk_ready, vs_ready = sem("qkv_ps"), sem("qk_ready"), sem("vs_ready")
        u_ready_v, msel_ready_v, k_again_ps = sem("u_ready_v"), sem("msel_ready_v"), sem("k_again_ps")
        qkt_ps, qkt_ready, ktm_ready_a = sem("qkt_ps"), sem("qkt_ready"), sem("ktm_ready_a")
        ktm_ready_v = sem("ktm_ready_v")
        sc_ps = sem("sc_ps")
        sc_taken, mx_ready, exp_ready = sem("sc_taken"), sem("mx_ready"), sem("exp_ready")
        pt_last_ps, pt_last_ready = sem("pt_last_ps"), sem("pt_last_ready")
        pt_ps, pt_ready_v, pt_ready_a = sem("pt_ps"), sem("pt_ready_v"), sem("pt_ready_a")
        o_ps, ot_ready = sem("o_ps"), sem("ot_ready")
        x1_ps, x1_ready, hid_ps = sem("x1_ps"), sem("x1_ready"), sem("hid_ps")
        usq_ready, arg_ready, tanh_ready, gel_ready = sem("usq_ready"), sem("arg_ready"), sem("tanh_ready"), sem("gel_ready")
        x2_ps, proc_ready, base_ready = sem("x2_ps"), sem("proc_ready"), sem("base_ready")
        y_ps, y_ready, stored = sem("y_ps"), sem("y_ready"), sem("stored")
        sets_clear, ones_ready, ones_v = sem("sets_clear"), sem("ones_ready"), sem("ones_v")
        xnt_ps, xnt_ready = sem("xnt_ps"), sem("xnt_ready")
        two_taken, turned_taken = sem("two_taken"), sem("turned_taken")
        proj_ps, rot_ready, hi_ready, rem_ready, mid_ready = (
            sem("proj_ps"), sem("rot_ready"), sem("hi_ready"), sem("rem_ready"), sem("mid_ready"))
        low_ready, v_ps, v_ready = sem("low_ready"), sem("v_ps"), sem("v_ready")
        parts_stored = [sem("parts_stored0"), sem("parts_stored1")]
        set_loaded = [sem(f"set_loaded{i}") for i in range(SETS)]
        shift_loaded = [sem(f"shift_loaded{i}") for i in range(SETS)]
        v_set_ready = sem("v_set_ready")
        tile_ps, tile_taken = sem("tile_ps"), sem("tile_taken")
        tiles_seen, diags_seen = sem("tiles_seen"), sem("diags_seen")
        shift_step, shift_ready = sem("shift_step"), sem("shift_ready")
        st_ps, exp_done, diag_done = sem("st_ps"), sem("exp_done"), sem("diag_done")
        prob_free = sem("prob_free")
        z_ready, zt_ps, zrec_ready = sem("z_ready"), sem("zt_ps"), sem("zrec_ready")
        pv_free = [sem("pv_free0"), sem("pv_free1")]
        o_tok_ready, att_t_ps, att_t_ready, att_ps, att_base = sem("o_tok_ready"), sem("att_t_ps"), sem("att_t_ready"), sem("att_ps"), sem("att_base")

        class Step:

            def __init__(self, eng, s):
                self.eng, self.s, self.n = eng, s, 0

            def __call__(self, ins):
                self.n += 1
                ins.then_inc(self.s, 1)
                self.eng.wait_ge(self.s, self.n)

        def blocks(t, b):
            return t[:, b * NB:(b + 1) * NB]

        ffn_tokens = {0: (xa, xb), 1: (xa, xb)}
        block = ctx.enter_context(nc.Block())

        @block.sync
        def _(sp):
            for b in range(B):
                sp.dma_start(blocks(xa, b), x_d[b].rearrange("(n p) d -> p n d", p=128)).then_inc(loaded_x[b], 16)

            def load(done, *pairs):
                for dst, src in pairs:
                    sp.dma_start(dst, src).then_inc(done, 16)

            load(loaded_r, (rw[:], rw_d.rearrange("d o -> o d").partition_broadcast(128).rearrange("p o d -> p (o d)")),
                 (rb[:], rb_d.partition_broadcast(128)))
            load(loaded_p, (invf[:], invf_d.partition_broadcast(128)), (pos_i[:], pos_d))
            load(loaded_f, (ln1[:], ln1_d.rearrange("(p o) -> p o", o=1)), (ln2[:], ln2_d.rearrange("(p o) -> p o", o=1)),
                 (fqkv[:, 0:D], fwq_d), (fqkv[:, D:2 * D], fwk_d), (fqkv[:, 2 * D:], fwv_d), (fwo[:], fwo_d),
                 (fw1[:], fw1_d), (fw2[:], fw2_d.rearrange("(n p) d -> p n d", p=128)))
            for b in range(B):
                load(loaded_m, (masks[:, b, 0:MB, 0:S_MASK], masks_d[b, 0].rearrange("(n p) c -> p n c", p=128)),
                     (masks[:, b, MB, 0:S_MASK], masks_d[b, 0, S_MASK - 1].partition_broadcast(128)))
            load(loaded_a, (bv[:], bv_d.partition_broadcast(128)), (bo[:], bo_d.partition_broadcast(128)),
                 (wqk[:], wqk_d), (bqk[:], bqk_d), (wv[:], wv_d), (wo[:], wo_d), (rope_c[:], rope_d))

            def load_set(g, which=(0, 1)):
                s = g % SETS
                for p in range(PARTS):
                    rows = slice(p * PARTS * HD, (p + 1) * PARTS * HD)
                    src = qk_scr[0][g, p * HD:(p + 1) * HD, :]
                    if 0 in which:
                        sp.dma_start(q_set[rows, s].rearrange("p a b -> p (a b)"),
                                     src.unsqueeze(0).to_broadcast([PARTS, HD, HG * T])).then_inc(set_loaded[s], 16)
                    if 1 in which:
                        sp.dma_start(k_set[rows, s].rearrange("p a b -> p (a b)"), qk_scr[1][g]).then_inc(set_loaded[s], 16)

            for n in range(2 * B):
                b, which = divmod(n, 2)
                for p in range(PARTS):
                    sp.wait_ge((hi_ready, mid_ready, low_ready)[p], n + 1)
                    sp.dma_start(
                        qk_scr[which][b * GB:(b + 1) * GB, p * HD:(p + 1) * HD, :].rearrange("g d (j t) -> g (d j) t", j=HG),
                        parts[n % 2][p]).then_inc(parts_stored[n % 2], 16)
                if n == 1:
                    sp.wait_ge(sets_clear, 1)
                    sp.wait_ge(ones_ready, SETS - 1)
                    for which in range(2):
                        sp.wait_ge(parts_stored[which], 16 * PARTS)
                        load_set(0, (which,))
                    sp.wait_ge(sets_clear, 2)
                    for g in range(1, SETS):
                        load_set(g)
            for half in parts_stored:
                sp.wait_ge(half, 16 * PARTS * B)
            for g in range(G):
                sp.wait_ge(shift_ready, g + 1)
                for r in range(PARTS):
                    sp.dma_start(q_set[SHIFT + r:SHIFT + r + 1, g % SETS].rearrange("p j (i c) -> p (j i) c", c=128),
                                 shift[0:TILES, r, :]).then_inc(shift_loaded[g % SETS], 16)
                if 1 <= g <= G - SETS:
                    sp.wait_ge(st_ps, NC * HG * g)
                    load_set(g - 1 + SETS)
            for b in range(B):
                sp.wait_ge(y_ready, B * 2 + b + 1)
                sp.dma_start(out_d[b].rearrange("(n p) d -> p n d", p=128), blocks(xb, b)).then_inc(stored, 16)
            sp.wait_ge(stored, 16 * B)

        @block.gpsimd
        def _(gp):
            step = Step(gp, pool_step)

            def root(n, b):
                gp.wait_ge(veps_ready, B * n + b + 1)
                nc.gpsimd.tensor_tensor(rstd[:, b], veps[:, b], neghalf[:], ALU.pow).then_inc(rstd_ready, 1)

            step(nc.gpsimd.memset(neghalf[:], -0.5))
            step(nc.gpsimd.memset(ident[:], 0.0))
            nc.gpsimd.affine_select(out=ident[:], in_=ident[:], compare_op=ALU.not_equal, fill=1.0, base=0,
                                    pattern=[[1, 128]], channel_multiplier=-1).then_inc(ident_ready, 1)
            step(nc.gpsimd.memset(later[:], 1.0))
            step(nc.gpsimd.affine_select(out=later[:, 0:128], in_=later[:, 0:128], compare_op=ALU.is_gt, fill=0.0, base=0,
                                         pattern=[[1, 128]], channel_multiplier=-1))
            step(nc.gpsimd.iota(from_last[:], pattern=[[-128, NB]], base=T - 1, channel_multiplier=-1,
                                allow_small_or_imprecise_dtypes=True))
            step(nc.gpsimd.memset(diagmask[:], 0.0))
            dm = diagmask[:, T - 128:T]
            step(nc.gpsimd.affine_select(out=dm, in_=dm, compare_op=ALU.is_ge, fill=NEG, base=0,
                                         pattern=[[-1, 128]], channel_multiplier=1))
            for b in range(B):
                root(0, b)
            step(nc.gpsimd.memset(ones_col[:], 1.0))
            step(nc.gpsimd.memset(headmask[:], 1.0))
            step(nc.gpsimd.affine_select(out=headmask[:], in_=headmask[:], compare_op=ALU.is_ge, fill=0.0, base=0,
                                         pattern=[[-HD, H]], channel_multiplier=1))
            step(nc.gpsimd.affine_select(out=headmask[:], in_=headmask[:], compare_op=ALU.is_ge, fill=0.0, base=HD - 1,
                                         pattern=[[HD, H]], channel_multiplier=-1))
            step(nc.gpsimd.iota(iota_row[:], pattern=[[1, 128]], base=0, channel_multiplier=0,
                                allow_small_or_imprecise_dtypes=True))
            nc.gpsimd.memset(ones_bf[:], 1.0).then_inc(consts_ready, 1)
            nc.gpsimd.memset(vs[:].rearrange("p b h w -> p (b h w)"), 0.0).then_inc(vs_clear, 1)

            TWO_PI = 2.0 * np.pi
            C1 = 6.28125
            C2 = float(np.float32(np.round((TWO_PI - C1) * 2.0 ** 21) / 2.0 ** 21))
            C3 = float(np.float32(TWO_PI - C1 - C2))
            MAGIC = 1.5 * 2.0 ** 23
            PI_IN = 3.1415925
            NP = B * (MB + 1)

            def angles():
                ts, tt = nc.gpsimd.tensor_scalar, nc.gpsimd.tensor_tensor
                gp.wait_ge(loaded_p, 16 * 2)
                step(nc.gpsimd.tensor_copy(posf[:, 0:NP], pos_i[:].rearrange("p b n -> p (b n)")))
                step(tt(ang[:].rearrange("p (a f) -> p a f", f=HALF), posf[:, 0:NP].unsqueeze(2).to_broadcast([128, NP, HALF]),
                        invf[:].unsqueeze(1).to_broadcast([128, NP, HALF]), ALU.mult))
                for k, (turn, add) in enumerate(((0.25, np.pi / 2), (0.0, 0.0))):
                    step(ts(turns[:], ang[:], float(1.0 / TWO_PI), turn, ALU.mult, ALU.add))
                    step(ts(turns[:], turns[:], MAGIC, None, ALU.add))
                    step(ts(turns[:], turns[:], MAGIC, None, ALU.subtract))
                    src = ang
                    for part_of_turn in (C1, C2, C3):
                        step(ts(posf[:], turns[:], part_of_turn, None, ALU.mult))
                        step(tt(red[:], src[:], posf[:], ALU.subtract))
                        src = red
                    step(ts(red[:], red[:], float(add), PI_IN, ALU.add, ALU.min))
                    nc.gpsimd.tensor_scalar(red2[:, k], red[:], -PI_IN, None, ALU.max).then_inc(angles_ready, 1)
                    gp.wait_ge(angles_ready, k + 1)
                gp.wait_ge(trig_ready, 2)
                step(ts(trig[:, 1], trig[:, 2], -1.0, None, ALU.mult))
                for b in range(B):
                    src = trig[:].rearrange("p k (b n f) -> p b n k f", b=B, n=MB + 1)[:, b]
                    dst = blocks(xn, b)[:, :, AUX_COS:AUX_W].rearrange("p n (k f) -> p n k f", k=3)
                    nc.gpsimd.tensor_copy(dst[:, 0:MB], src[:, 0:MB]).then_inc(aux_trig, 1)
                    nc.gpsimd.tensor_copy(dst[:, MB:NB], src[:, MB:MB + 1].to_broadcast([128, NB - MB, 3, HALF])).then_inc(aux_trig, 1)

            def ffn(f):
                xi, _ = ffn_tokens[f]
                if f:
                    for b in range(B):
                        root(2, b)
                if f == 0:
                    angles()
                for b in range(B):
                    gp.wait_ge(wcol_ready, B * f + b + 1)
                    gp.wait_ge(xn_ready, B * f + b + 1)
                    nc.gpsimd.tensor_copy(blocks(xn, b)[:, :, AUX_W], wcol[:, b]).then_inc(aux_w, 1)

                def rms_root(k, b):
                    gp.wait_ge(ssq_ready, 2 * B * f + B * k + b + 1)
                    step(nc.gpsimd.tensor_scalar(ms[:, b, k:k + 1], ssq[:, b, k:k + 1], 1.0 / D, RMS_EPS, ALU.mult, ALU.add))
                    nc.gpsimd.tensor_tensor(rs[:, b, k:k + 1], ms[:, b, k:k + 1], neghalf[:, 0:1], ALU.pow).then_inc(rs_ready, 1)

                rms_root(0, 0)
                rms_root(0, 1)
                for b in range(B):
                    gp.wait_ge(drop_ready, B * f + b + 1)
                    step(nc.gpsimd.tensor_tensor(blocks(base, b), blocks(xn, b)[:, :, 0:D],
                                                 drop[:, b].unsqueeze(2).to_broadcast([128, NB, D]), ALU.mult))
                    nc.gpsimd.tensor_tensor(blocks(base, b), blocks(base, b), blocks(xi, b), ALU.add).then_inc(base_ready, 1)
                for n in range(2 * B - 1):
                    b, half = divmod(n, 2)
                    hs = slice(8 * half, 8 * half + 8)
                    gp.wait_ge(rrec_ready, 2 * B * f + n + 1)
                    nc.gpsimd.tensor_tensor(prob[:, b, hs, 0:KEEP], prob[:, b, hs, 0:KEEP],
                                            rrec[:, b, hs].unsqueeze(2).to_broadcast([128, 8, KEEP]), ALU.mult).then_inc(norm_ready, 1)
                for b in range(B):
                    rms_root(1, b)

            ffn(0)

            for b in range(B):
                root(1, b)
            gp.wait_ge(y_ready, B)
            step(nc.gpsimd.memset(v_set[:].rearrange("p s n j w -> p (s n j w)"), 0.0))
            nc.gpsimd.memset(v_set[:, :, :, :, HD].rearrange("p s n j -> p s (n j)"), 1.0).then_inc(ones_v, 1)
            nc.gpsimd.memset(q_set[:].rearrange("p s j t -> p (s j t)"), 0.0).then_inc(sets_clear, 1)
            for b in range(B):
                gp.wait_ge(y_ready, b + 1)
                gp.wait_ge(loaded_a, 16 * 7)
                nc.gpsimd.tensor_tensor(blocks(base, b), blocks(xb, b),
                                        bo[:].unsqueeze(1).to_broadcast([128, NB, D]), ALU.add).then_inc(att_base, 1)
                for which in range(2):
                    n = 2 * b + which
                    gp.wait_ge(mid_ready, n + 1)
                    nc.gpsimd.tensor_tensor(parts[n % 2][2], rt[:, n % 2], parts[n % 2][1], ALU.subtract).then_inc(low_ready, 1)
                if b == 0:
                    nc.gpsimd.memset(k_set[:, SETS - 1].rearrange("p j t -> p (j t)"), 1.0).then_inc(sets_clear, 1)

            def v_to_set(g, s):
                nc.gpsimd.tensor_copy(v_set[:, s, :, :, 0:HD].rearrange("p n j w -> p (n j) w"), v_all[:, g].rearrange("p (a w) -> p a w", w=HD)
                                      if isinstance(g, int) else
                                      v_all[:, bass.ds(g, 1)].rearrange("p o (a w) -> p (o a) w", w=HD)).then_inc(v_set_ready, 1)

            gp.wait_ge(ones_v, 1)
            gp.wait_ge(v_ready, B)
            v_to_set(0, 0)
            v_to_set(1, 1)

            def diagonal(g, c):
                gp.wait_ge(exp_done, g * (NC * HG) + HG * (c + 1))
                gp.sem_inc(diags_seen, 1)
                for at in DIAG[c]:
                    v = p_buf[:, c % 3, :, at:at + 128]
                    last = nc.gpsimd.affine_select(out=v, in_=v, compare_op=ALU.is_ge, fill=0.0, base=0,
                                                   pattern=[[0, HG], [1, 128]], channel_multiplier=-1)
                last.then_inc(diag_done, 1)

            diagonal(0, 0)

            def body(g, s, has_next, copies_v):
                for c in DIAG_CHUNKS[1:]:
                    diagonal(g, c)
                    if c == 3 and copies_v:
                        gp.wait_ge(prob_free, g * NC + 3)
                        v_to_set(g + 2, (s + 2) % SETS)
                if has_next:
                    diagonal(g + 1, 0)

            with gp.Fori(0, (G - 2) // SETS) as i:
                for s in range(SETS):
                    body(i * SETS + s, s, True, True)
            body(G - 2, (G - 2) % SETS, True, False)
            body(G - 1, (G - 1) % SETS, False, False)

            ffn(1)

        @block.vector
        def _(ve):
            V = nc.vector
            step = Step(ve, vec_step)

            def moments(n, b, xi):
                if n == 0:
                    ve.wait_ge(loaded_x[b], 16)
                else:
                    ve.wait_ge(y_ready, B * (n - 1) + b + 1)
                for k in range(b * NB, (b + 1) * NB):
                    V.bn_stats(stats[:, k], xi[:, k]).then_inc(vec_step, 1)
                step.n += NB
                ve.wait_ge(vec_step, step.n)
                for k in range(b * NB, (b + 1) * NB):
                    V.bn_aggr(mv[:, k], stats[:, k]).then_inc(vec_step, 1)
                step.n += NB
                ve.wait_ge(vec_step, step.n)
                V.tensor_scalar(veps[:, b], blocks(mv, b)[:, :, 1], LN_EPS, None, ALU.add).then_inc(veps_ready, 1)
                if n != 1:
                    V.tensor_scalar(nmean[:, b], blocks(mv, b)[:, :, 0], -1.0, None, ALU.mult).then_inc(nmean_ready, 1)

            def add_base(xo, b, first_bank, done, n):
                for h in range(2):
                    ve.wait_ge(done, n + h + 1)
                    ins = V.tensor_tensor(blocks(xo, b)[:, MB * h:MB * h + MB], bank(first_bank + h).rearrange("p (n d) -> p n d", d=D),
                                          blocks(base, b)[:, MB * h:MB * h + MB], ALU.add)
                ins.then_inc(y_ready, 1)

            def products(f, b, xi):
                prod = scr[:].rearrange("p (n d) -> p n d", n=NB)
                if b or f:
                    ve.wait_ge(dot_ready, B * f + b)
                for k in range(NB):
                    last = V.scalar_tensor_tensor(prod[:, k], xi[:, b * NB + k], mv[:, b * NB + k, 0:1], rw[:],
                                                  ALU.subtract, ALU.mult, accum_out=dot[:, b, k:k + 1])
                last.then_inc(dot_ready, 1)

            def ffn(f):
                xi, xo = ffn_tokens[f]

                def router(b):
                    ve.wait_ge(rstd_ready, 2 * B * f + b + 1)
                    ve.wait_ge(dot_ready, B * f + b + 1)
                    step(V.tensor_tensor(wcol[:, b], dot[:, b], rstd[:, b], ALU.mult))
                    V.tensor_scalar(wcol[:, b], wcol[:, b], rb[:, 0:1], None, ALU.add).then_inc(wcol_ready, 1)

                def compare(b, ks):
                    for k in ks:
                        V.scalar_tensor_tensor(cmp[:, b, CMP_AT[k]:CMP_AT[k + 1]], wrow[:, b, 128 * k:T], wcol[:, b, k:k + 1],
                                               later[:, 0:T - 128 * k], ALU.is_le, ALU.mult,
                                               accum_out=after[:, b, k:k + 1]).then_inc(cmp_ready, 1)

                def later_before(b):
                    ve.wait_ge(cmp_ready, NB * (B * f + b + 1))
                    V.tensor_tensor(later_first[:, b], from_last[:], after[:, b], ALU.subtract).then_inc(before_ready, 1)

                def one_hot(b):
                    n = B * f + b + 1
                    ve.wait_ge(before_ready, n)
                    ve.wait_ge(rank_ps, n)
                    step(V.tensor_tensor(rcol[:, b], bank(4 * b + 2, 0, NB), later_first[:, b], ALU.add))
                    V.tensor_tensor(slots_t[:, b, 0:NB], iota_row[:].unsqueeze(1).to_broadcast([128, NB, 128]),
                                    rcol[:, b].unsqueeze(2).to_broadcast([128, NB, 128]), ALU.is_equal).then_inc(slots_t_ready, 1)
                    V.tensor_scalar(past[:, b], rcol[:, b], float(KEEP), 0.5, ALU.is_ge, ALU.mult).then_inc(past_ready, 1)
                    ve.wait_ge(slots_t_ready, n)
                    step(V.tensor_tensor(at_rank[:, b], slots_t[:, b, 0:NB, KEEP], wcol[:, b], ALU.mult))
                    V.tensor_reduce(thr_part[:, b:b + 1], at_rank[:, b], AX.X, ALU.add).then_inc(thr_part_ready, 1)
                    V.tensor_reduce(slots_t[:, b, NB], slots_t[:, b, MB:NB].rearrange("p n s -> p s n"), AX.X,
                                    ALU.add).then_inc(clamp_ready, 1)

                def rope(b):
                    ve.wait_ge(qkv_ps, B * f + b + 1)
                    src = bank(4 * b + 2, 0, 2 * D).rearrange("p (h a c) -> p h a c", h=2 * H, a=2)

                    def row(at):
                        return xs[:, b, at:at + HALF].unsqueeze(1).to_broadcast([128, 2 * H, HALF])
                    V.tensor_tensor(ra[:, b, :, 0], src[:, :, 0], row(AUX_COS), ALU.mult)
                    V.tensor_tensor(ra[:, b, :, 1], src[:, :, 1], row(AUX_COS), ALU.mult)
                    V.tensor_tensor(rbuf[:, b, :, 0], src[:, :, 1], row(AUX_NSIN), ALU.mult)
                    step(V.tensor_tensor(rbuf[:, b, :, 1], src[:, :, 0], row(AUX_SIN), ALU.mult))
                    V.tensor_tensor(qk[:, b], ra[:, b].rearrange("p h a c -> p (h a c)"),
                                    rbuf[:, b].rearrange("p h a c -> p (h a c)"), ALU.add).then_inc(qk_ready, 1)

                def threshold(b):
                    n = B * f + b + 1
                    ve.wait_ge(xs_ready, n)
                    ve.wait_ge(past_ready, n)
                    step(V.tensor_scalar(drop[:, b], wcol[:, b], xs[:, b, XW:XW + 1], 0.5, ALU.is_le, ALU.mult))
                    V.tensor_tensor(drop[:, b], drop[:, b], past[:, b], ALU.max).then_inc(drop_ready, 1)

                def slot_rows(b):
                    ve.wait_ge(slots_ps, B * f + b + 1)
                    V.tensor_copy(slots[:, b, 0:T // 2], bank(3))
                    V.tensor_copy(slots[:, b, T // 2:T], bank(7)).then_inc(slots_ready, 1)

                if f == 0:
                    for b in range(B):
                        moments(0, b, xi)
                    ve.wait_ge(loaded_r, 16 * 2)
                    for b in range(B):
                        products(0, b, xi)
                        router(b)
                    ve.wait_ge(consts_ready, 1)
                    ve.wait_ge(wrow_ready, 1)
                    compare(0, range(NB))
                else:
                    tokens_out(1)
                    router(0)
                    turned_out(1)
                    ve.wait_ge(wrow_ready, B + 1)
                    compare(0, range(3))
                    projected(1)
                    router(1)
                    compare(0, range(3, NB))
                later_before(0)
                ve.wait_ge(wrow_ready, B * f + 2)
                compare(1, range(2))
                one_hot(0)
                compare(1, range(2, NB))
                later_before(1)
                one_hot(1)
                rope(0)

                def keys(b):
                    n = B * f + b + 1
                    ve.wait_ge(qkt_ps, n)
                    V.tensor_copy(qt[:, b], bank(4 * b + 2, 0, D))
                    V.tensor_tensor(ktm[:, b, 0:H // 2], bank(4 * b + 2, D, 2 * D).unsqueeze(1).to_broadcast([128, H // 2, 128]),
                                    headmask[:, 0:H // 2].unsqueeze(2).to_broadcast([128, H // 2, 128]), ALU.mult).then_inc(qkt_ready, 1)

                def masked(b, half):
                    m = 2 * (B * f + b) + half + 1
                    hs = slice(8 * half, 8 * half + 8)
                    ve.wait_ge((msel_ready, msel_ready_v)[b], f + 1)
                    ve.wait_ge(sc_ps, m)
                    V.scalar_tensor_tensor(sc[:, b, hs], psum[:, 4 * half:4 * half + 2].rearrange("p a (h k) -> p (a h) k", k=128),
                                           SCALE, msel[:, b].unsqueeze(1).to_broadcast([128, 8, 128]), ALU.mult,
                                           ALU.add).then_inc(sc_taken, 1)
                    ve.wait_ge(sc_taken, m)
                    V.tensor_reduce(nmx[:, b, hs], sc[:, b, hs, 0:KEEP], AX.X, ALU.max, negate=True).then_inc(mx_ready, 1)

                def over_sums(b, half):
                    hs = slice(8 * half, 8 * half + 8)
                    m = 2 * (B * f + b) + half + 1
                    ve.wait_ge(exp_ready, m)
                    V.reciprocal(rrec[:, b, hs], rsum[:, b, hs]).then_inc(rrec_ready, 1)
                    if (b, half) == (B - 1, 1):
                        ve.wait_ge(rrec_ready, m)
                        for h in (8, 12):
                            hs = slice(h, h + 4)
                            V.tensor_tensor(prob[:, b, hs, 0:KEEP], prob[:, b, hs, 0:KEEP],
                                            rrec[:, b, hs].unsqueeze(2).to_broadcast([128, 4, KEEP]), ALU.mult).then_inc(last_norm_ready, 1)

                keys(0)
                rope(1)
                threshold(0)
                threshold(1)
                masked(0, 0)
                keys(1)
                hs = slice(H // 2, H)
                V.tensor_tensor(ktm[:, 1, hs], bank(6, D, 2 * D).unsqueeze(1).to_broadcast([128, H // 2, 128]),
                                headmask[:, hs].unsqueeze(2).to_broadcast([128, H // 2, 128]), ALU.mult).then_inc(ktm_ready_v, 1)
                ve.wait_ge(u_ps, B * f + 2)
                V.tensor_copy(umask[:, 1].rearrange("p n s -> p (n s)"),
                              psum[:, 4:6].rearrange("p a c -> p (a c)")[:, 0:(MB + 1) * 128]).then_inc(u_ready_v, 1)
                masked(0, 1)
                ve.wait_ge(msel_ps, B * f + 2)
                V.tensor_copy(msel[:, 1], bank(7, 0, D)).then_inc(msel_ready_v, 1)
                over_sums(0, 0)
                masked(1, 0)
                slot_rows(0)
                over_sums(0, 1)
                masked(1, 1)
                slot_rows(1)
                over_sums(1, 0)
                for half in range(2):
                    ve.wait_ge(pt_ps, 2 * B * f + half + 1)
                    V.tensor_copy(ktm[0:KEEP, 0, 8 * half:8 * half + 8],
                                  psum[0:KEEP, 4 * half:4 * half + 2].rearrange("p a (h k) -> p (a h) k", k=128)).then_inc(pt_ready_v, 1)
                over_sums(1, 1)
                ve.wait_ge(pt_last_ps, f + 1)
                V.tensor_copy(ktm[0:KEEP, 1, H - HG:H], psum[0:KEEP, 5].rearrange("p (h k) -> p h k", k=128)).then_inc(pt_last_ready, 1)
                for b in range(B):
                    ve.wait_ge(x1_ps, B * f + b + 1)
                    V.tensor_tensor(x1[:, b], bank(4 * b + 3, 0, D), xs[:, b, 0:D], ALU.add).then_inc(x1_ready, 1)
                for b in range(B):
                    ve.wait_ge(x1_ready, B * f + b + 1)
                    step(V.tensor_scalar(x1w[:, b], x1[:, b], xs[:, b, AUX_W:AUX_W + 1], 0.5, ALU.mult, ALU.mult))
                    step(V.tensor_scalar(quarter_w[:, b:b + 1], xs[:, b, AUX_W:AUX_W + 1], 0.25, None, ALU.mult))
                for b in range(B):
                    n = B * f + b + 1
                    ve.wait_ge(usq_ready, n)
                    V.scalar_tensor_tensor(usq[:, b], usq[:, b], 1.0, bank(4 * b), ALU.add, ALU.mult).then_inc(arg_ready, 1)
                    ve.wait_ge(tanh_ready, n)
                    V.scalar_tensor_tensor(gel[:, b], th[:, b], 1.0, bank(4 * b), ALU.add, ALU.mult).then_inc(gel_ready, 1)
                for b in range(B):
                    ve.wait_ge(x2_ps, B * f + b + 1)
                    V.scalar_tensor_tensor(proc[:, b], bank(4 * b + 3, 0, D), quarter_w[:, b:b + 1], x1w[:, b],
                                           ALU.mult, ALU.add).then_inc(proc_ready, 1)
                for b in range(B):
                    ve.wait_ge(base_ready, B * f + b + 1)
                    add_base(xo, b, 4 * b, y_ps, 2 * (B * f + b))
                    if f == 0:
                        moments(1, b, xo)

            ffn(0)

            ve.wait_ge(loaded_a, 16 * 7)
            for b in range(B):
                ve.wait_ge(rstd_ready, B + b + 1)
                for k in range(NB):
                    last = V.tensor_scalar(xn[:, b * NB + k, 0:D], xb[:, b * NB + k], mv[:, b * NB + k, 0:1],
                                           rstd[:, b, k:k + 1], ALU.subtract, ALU.mult)
                last.then_inc(xn_att_ready, 1)

            def rotate(n):
                which, first = n % 2, PROJ_BANK[n]
                two = psum[:, first:first + 2].rearrange("p a c -> p (a c)")
                turned = psum[:, first + 2:first + 4].rearrange("p a c -> p (a c)")
                ve.wait_ge(proj_ps, 2 * n + 1)
                if n >= 2:
                    ve.wait_ge(hi_ready, n - 1)
                    ve.wait_ge(rem_ready, n - 1)
                V.scalar_tensor_tensor(rq[:, n % 2], two, bqk[:, 2 * which:2 * which + 1], rope_c[:, 0], ALU.add, ALU.mult).then_inc(two_taken, 1)
                ve.wait_ge(proj_ps, 2 * n + 2)
                if n >= 2:
                    ve.wait_ge(mid_ready, n - 1)
                    ve.wait_ge(low_ready, n - 1)
                V.scalar_tensor_tensor(rt[:, n % 2], turned, bqk[:, 2 * which + 1:2 * which + 2], rope_c[:, 1], ALU.add, ALU.mult).then_inc(turned_taken, 1)
                ve.wait_ge(two_taken, n + 1)
                ve.wait_ge(turned_taken, n + 1)
                V.tensor_tensor(rq[:, n % 2], rq[:, n % 2], rt[:, n % 2], ALU.add).then_inc(rot_ready, 1)

            def remainder(n):
                ve.wait_ge(rot_ready, n + 1)
                ve.wait_ge(hi_ready, n + 1)
                V.tensor_tensor(rt[:, n % 2], rq[:, n % 2], parts[n % 2][0], ALU.subtract).then_inc(rem_ready, 1)

            rotate(0)
            rotate(1)
            remainder(0)
            remainder(1)
            rotate(2)
            rotate(3)
            remainder(2)
            remainder(3)

            def tile_max(g, a, first=False):
                j, (i, first_bank, _) = head_and_tile(a, first)
                n = 128 * (i + 1)
                ve.wait_ge(tile_ps, g * USES + a + 1)
                if first and a >= 3:
                    ve.wait_ge(tile_taken, a - 2)
                ve.sem_inc(tiles_seen, 1)
                V.tensor_tensor_reduce(out=junk_v[:, a % 3, 0:n],
                                       in0=psum[:, first_bank:first_bank + (n + 511) // 512].rearrange("p a c -> p (a c)")[:, 0:n],
                                       in1=diagmask[:, T - n:T], scale=1.0, scalar=-3.0e38,
                                       op0=ALU.add, op1=ALU.max, accum_out=mx[:, j * NB + i:j * NB + i + 1]).then_inc(tile_taken, 1)

            def max_parts(g):
                ps = psum[0:TILES, MAX_BANK, 0:128]
                ve.wait_ge(tile_ps, g * USES + USES)
                V.tensor_scalar(shift[0:TILES, 0], ps, -1.0, None, ALU.mult).then_inc(shift_step, 1)
                ve.wait_ge(shift_step, g * 2 + 1)
                V.scalar_tensor_tensor(srem[0:TILES], ps, -1.0, shift[0:TILES, 0], ALU.mult, ALU.subtract).then_inc(tile_taken, 1)
                ve.wait_ge(tile_taken, g * USES + USES)
                V.tensor_copy(shift[0:TILES, 1], srem[0:TILES]).then_inc(shift_step, 1)
                ve.wait_ge(shift_step, g * 2 + 2)
                V.tensor_tensor(shift[0:TILES, 2], srem[0:TILES], shift[0:TILES, 1], ALU.subtract).then_inc(shift_ready, 1)

            def normalise(g, h):
                z = psum[:, 6 + h].rearrange("p (n j w) -> p n j w", n=4, j=HG)
                ve.wait_ge(zt_ps, g * 2 + h + 1)
                V.reciprocal(zrec[:, h].rearrange("p (n j) -> p n j", n=4), z[:, :, :, HD]).then_inc(zrec_ready, 1)
                ve.wait_ge(zrec_ready, g * 2 + h + 1)
                dst = o_all[:, g, h * 128:(h + 1) * 128] if isinstance(g, int) else \
                    o_all[:, bass.ds(g, 1), h * 128:(h + 1) * 128].rearrange("p o e -> p (o e)")
                V.tensor_tensor(dst.rearrange("p (n j w) -> p n j w", n=4, j=HG), z[:, :, :, 0:HD],
                                zrec[:, h].rearrange("p (n j) -> p n j", n=4).unsqueeze(3).to_broadcast([128, 4, HG, HD]),
                                ALU.mult).then_inc(pv_free[h], 1)

            for a in range(TILES):
                tile_max(0, a, first=True)
            max_parts(0)
            for a in range(FIRST):
                tile_max(1, a)
            V.memset(zrec[:, 0], 0.0).then_inc(pv_free[0], 1)
            V.memset(zrec[:, 1], 0.0).then_inc(pv_free[1], 1)

            def tokens_out(b):
                V.tensor_tensor(o_tok[:, b].rearrange("p n (g e) -> p n g e", g=GB),
                                o_all[:, b * GB:(b + 1) * GB].rearrange("p g (n e) -> p n g e", n=NB),
                                bv[:].rearrange("p (g e) -> p g e", g=GB).unsqueeze(1).to_broadcast([128, NB, GB, HG * HD]),
                                ALU.add).then_inc(o_tok_ready, 1)

            def turned_out(b):
                ve.wait_ge(att_t_ps, b + 1)
                V.tensor_copy(o_turned[:, b], psum[:, 4 * b:4 * b + 2].rearrange("p a c -> p (a c)")).then_inc(att_t_ready, 1)

            def projected(b):
                ve.wait_ge(att_base, b + 1)
                add_base(xa, b, 4 * b + 2, att_ps, 2 * b)
                moments(2, b, xa)
                products(1, b, xa)

            def body(g, has_next, has_second, has_first):
                for what, dg, n, *_ in body_plan(has_next, has_second, has_first):
                    if what == "tile":
                        tile_max(g + dg, n)
                    elif what == "maxt":
                        max_parts(g + dg)
                    elif what == "zt":
                        normalise(g, n)
                    elif what == "o_tok":
                        ve.wait_ge(pv_free[0], GB + 1)
                        ve.wait_ge(pv_free[1], GB + 1)
                        tokens_out(0)
                    elif what == "o_turn":
                        turned_out(0)
                    elif what == "o_proj":
                        projected(0)

            with ve.Fori(0, (G - 2) // SETS) as i:
                for s in range(SETS):
                    body(i * SETS + s, True, True, True)
            body(G - 2, True, True, False)
            body(G - 1, False, False, False)

            ve.wait_ge(pv_free[0], G + 1)
            ve.wait_ge(pv_free[1], G + 1)
            ffn(1)

        @block.scalar
        def _(ac):
            A = nc.scalar
            step = Step(ac, act_step)

            def ffn(f):
                def squares(k, b, src):
                    A.activation(junk_a[:, B * k + b], src, ACT.Square, accum_out=ssq[:, b, k:k + 1]).then_inc(ssq_ready, 1)

                def normalised(k, b, src):
                    n = 2 * B * f + B * k + b + 1
                    ac.wait_ge(rs_ready, n)
                    A.activation(hn[:, b], src, ACT.Copy, scale=rs[:, b, k:k + 1]).then_inc(hn_ready, 1)
                    ac.wait_ge(ht_ps, n)
                    A.activation(ht[:, b], bank(4 * b + 2, 0, D), ACT.Copy, scale=(ln1, ln2)[k][:, 0:1]).then_inc(ht_ready, 1)

                def weight_rows(b):
                    ac.wait_ge(wrow_ps, B * f + b + 1)
                    A.activation(wrow[:, b], psum[:, 4 * b:4 * b + 2].rearrange("p a c -> p (a c)"), ACT.Copy).then_inc(wrow_ready, 1)

                def gathered(b):
                    n = B * f + b + 1
                    ac.wait_ge(gather_ps, n)
                    A.activation(xs[:, b], bank(4 * b + 3, 0, XW + 1), ACT.Copy).then_inc(xs_ready, 1)
                    ac.wait_ge(xs_ready, n)
                    squares(0, b, xs[:, b, 0:D])

                def values(b):
                    ac.wait_ge(qk_ready, B * f + b + 1)
                    if f == 0 and b == 0:
                        ac.wait_ge(vs_clear, 1)
                    A.activation(vs[:, b, :, 0:HD], bank(4 * b + 2, 2 * D, 3 * D).rearrange("p (h c) -> p h c", h=H),
                                 ACT.Copy).then_inc(vs_ready, 1)

                def mask_rows():
                    ac.wait_ge(u_ps, B * f + 1)
                    A.activation(umask[:, 0].rearrange("p n s -> p (n s)"),
                                 psum[:, 0:2].rearrange("p a c -> p (a c)")[:, 0:(MB + 1) * 128], ACT.Copy).then_inc(u_ready, 1)

                def mask_columns():
                    ac.wait_ge(msel_ps, B * f + 1)
                    A.activation(msel[:, 0], bank(3, 0, D), ACT.Copy).then_inc(msel_ready, 1)

                def normalised_tokens(b):
                    tokens = ffn_tokens[f][0]
                    ac.wait_ge(nmean_ready, B * f + b + 1)
                    for k in range(NB):
                        A.activation(xn[:, b * NB + k, 0:D], tokens[:, b * NB + k], ACT.Identity, bias=nmean[:, b, k:k + 1]).then_inc(act_step, 1)
                    step.n += NB
                    ac.wait_ge(act_step, step.n)
                    ac.wait_ge(rstd_ready, 2 * B * f + b + 1)
                    for k in range(NB):
                        last = A.activation(xn[:, b * NB + k, 0:D], xn[:, b * NB + k, 0:D], ACT.Copy, scale=rstd[:, b, k:k + 1])
                    last.then_inc(xn_ready, 1)

                def keys():
                    ac.wait_ge(k_again_ps, f + 1)
                    for h in range(H // 2, H):
                        last = A.activation(ktm[:, 0, h], bank(3, D, 2 * D), ACT.Copy, scale=headmask[:, h:h + 1])
                    last.then_inc(ktm_ready_a, 1)

                def exps(b, half):
                    ac.wait_ge(mx_ready, 2 * (B * f + b) + half + 1)
                    for h in range(8 * half, 8 * half + 8):
                        last = A.activation(prob[:, b, h, 0:KEEP], sc[:, b, h, 0:KEEP], ACT.Exp, bias=nmx[:, b, h:h + 1],
                                            accum_out=rsum[:, b, h:h + 1])
                    last.then_inc(exp_ready, 1)

                normalised_tokens(0)
                weight_rows(0)
                weight_rows(1)
                normalised_tokens(1)
                if f == 0:
                    for k in range(2):
                        ac.wait_ge(angles_ready, k + 1)
                        A.activation(trig[:, 2 * k], red2[:, k], ACT.Sin).then_inc(trig_ready, 1)
                if f == 0:
                    ac.wait_ge(loaded_m, 16 * 2 * B)
                    for b in range(B):
                        A.activation(masks[:, b, :, S_MASK:], masks[:, b, :, S_MASK - 1:S_MASK].to_broadcast([128, MB + 1, 128]),
                                     ACT.Copy).then_inc(mask_wide, 1)
                gathered(0)
                normalised(0, 0, xs[:, 0, 0:D])
                gathered(1)
                values(0)
                normalised(0, 1, xs[:, 1, 0:D])
                mask_rows()
                mask_columns()
                values(1)
                keys()
                exps(0, 0)
                exps(0, 1)
                exps(1, 0)
                exps(1, 1)

                def outputs(b):
                    ac.wait_ge(o_ps, B * f + b + 1)
                    A.activation(ot[:, b], bank(4 * b + 2), ACT.Copy).then_inc(ot_ready, 1)

                def turned(half):
                    ac.wait_ge(pt_ps, 2 * (B * f + 1) + half + 1)
                    banks = 2 - half
                    A.activation(ktm[0:KEEP, 1, 8 * half:8 * half + 4 * banks],
                                 psum[0:KEEP, 4 * half:4 * half + banks].rearrange("p a (h k) -> p (a h) k", k=128), ACT.Copy).then_inc(pt_ready_a, 1)

                def squares_of_sum(b):
                    ac.wait_ge(x1_ready, B * f + b + 1)
                    squares(1, b, x1[:, b])

                turned(0)
                outputs(0)
                turned(1)
                squares_of_sum(0)
                outputs(1)
                normalised(1, 0, x1[:, 0])
                squares_of_sum(1)

                def hidden_squares(b):
                    ac.wait_ge(hid_ps, B * f + b + 1)
                    A.activation(usq[:, b], bank(4 * b), ACT.Square, scale=float(np.sqrt(0.044715))).then_inc(usq_ready, 1)

                hidden_squares(0)
                normalised(1, 1, x1[:, 1])

                def tanh(b):
                    ac.wait_ge(arg_ready, B * f + b + 1)
                    A.activation(th[:, b], usq[:, b], ACT.Tanh, scale=float(np.sqrt(2.0 / np.pi))).then_inc(tanh_ready, 1)

                tanh(0)
                hidden_squares(1)
                tanh(1)

            ffn(0)

            ac.wait_ge(y_ready, B)

            def ones(s):
                A.activation(k_set[:, s].rearrange("p j t -> p (j t)"), ones_bf[:, 0:1].to_broadcast([128, HG * T]),
                             ACT.Copy).then_inc(ones_ready, 1)
            ones(0)
            for b in range(B):
                ac.wait_ge(xnt_ps, b + 1)
                A.activation(xnt[:, b], psum[:, 4 + 2 * b:6 + 2 * b].rearrange("p a c -> p (a c)"), ACT.Copy).then_inc(xnt_ready, 1)
            for s in range(1, SETS - 1):
                ones(s)

            def high(n):
                ac.wait_ge(rot_ready, n + 1)
                if n >= 2:
                    ac.wait_ge(parts_stored[n % 2], 16 * PARTS)
                A.activation(parts[n % 2][0], rq[:, n % 2], ACT.Copy).then_inc(hi_ready, 1)

            def middle(n):
                ac.wait_ge(rem_ready, n + 1)
                A.activation(parts[n % 2][1], rt[:, n % 2], ACT.Copy).then_inc(mid_ready, 1)

            def values(b):
                ac.wait_ge(v_ps, b + 1)
                A.activation(v_all[:, b * GB:(b + 1) * GB].rearrange("p g (n e) -> p n g e", n=NB),
                             psum[:, V_BANK[b]:V_BANK[b] + 2].rearrange("p a (n g e) -> p (a n) g e", n=MB, g=GB),
                             ACT.Copy).then_inc(v_ready, 1)

            high(0)
            high(1)
            middle(0)
            values(0)
            middle(1)
            high(2)
            high(3)
            middle(2)
            values(1)
            middle(3)

            def exps(g, c, j):
                e = g * (NC * HG) + (HG * c + j)
                ac.wait_ge(st_ps, e + 1)
                if j == 0:
                    ac.wait_ge(prob_free, g * NC + (c + 1))
                A.activation(p_buf[:, c % 3, j], bank(4 + j % 2), ACT.Exp, scale=SCALE).then_inc(exp_done, 1)

            def evacuate(g, h):
                if h == 0:
                    ac.wait_ge(half_done, g + 1)
                else:
                    ac.wait_ge(prob_free, g * NC + NC + 3)
                A.activation(z_buf[:, h], bank(6 + h), ACT.Copy).then_inc(z_ready, 1)

            for half in parts_stored:
                ac.wait_ge(half, 16 * PARTS * B)
            for c in range(2):
                for j in range(HG):
                    exps(0, c, j)

            def body(g, has_next, has_second, has_first):
                for what, dg, n, *j in body_plan(has_next, has_second, has_first):
                    if what == "st":
                        exps(g + dg, n, j[0])
                    elif what == "evac":
                        evacuate(g, n)

            with ac.Fori(0, (G - 2) // SETS) as i:
                for s in range(SETS):
                    body(i * SETS + s, True, True, True)
            body(G - 2, True, True, False)
            body(G - 1, False, False, False)

            ffn(1)

        @block.tensor
        def _(pe):
            M = nc.tensor

            def mm(out, w, m, start=True, stop=True):
                return M.matmul(out, w, m, start=start, stop=stop)

            def ffn(f):
                def weight_rows(b):
                    pe.wait_ge(wcol_ready, B * f + b + 1)
                    for k in range(NB):
                        last = M.transpose(bank(4 * b + k // 4, 128 * (k % 4), 128 * (k % 4) + 128),
                                           wcol[:, b, k:k + 1].to_broadcast([128, 128]), ident[:])
                    last.then_inc(wrow_ps, 1)

                if f:
                    turn_out(1)
                weight_rows(0)
                if f:
                    project_out(1)
                weight_rows(1)

                def ranks(b, ks):
                    cols = bank(4 * b + 2)
                    if 0 in ks:
                        mm(cols[:, 0:NB], ones_bf[:], diagmask[:, 0:NB], stop=False)
                    for k in ks:
                        pe.wait_ge(cmp_ready, NB * (B * f + b) + k + 1)
                        for i in range(k, NB):
                            at = CMP_AT[k] + 128 * (i - k)
                            last = mm(cols[:, i:i + 1], cmp[:, b, at:at + 128], ones_bf[:, 0:1], start=False, stop=(k == NB - 1))
                        if k == NB - 1:
                            last.then_inc(rank_ps, 1)

                def gather(b):
                    n = B * f + b + 1
                    pe.wait_ge(slots_t_ready, n)
                    pe.wait_ge(aux_w, n)
                    if f == 0:
                        pe.wait_ge(aux_trig, 2 * B)
                    for k in range(NB):
                        mm(bank(4 * b + 3, 0, XW), slots_t[:, b, k], xn[:, b * NB + k, :], start=(k == 0), stop=(k == NB - 1))
                    pe.wait_ge(thr_part_ready, n)
                    mm(bank(4 * b + 3, XW, XW + 1), thr_part[:, b:b + 1].to_broadcast([128, 128]), ones_col[:]).then_inc(gather_ps, 1)

                def normed_t(k, b):
                    pe.wait_ge(hn_ready, 2 * B * f + B * k + b + 1)
                    M.transpose(bank(4 * b + 2, 0, D), hn[:, b], ident[:]).then_inc(ht_ps, 1)

                def qkv(b):
                    pe.wait_ge(ht_ready, 2 * B * f + b + 1)
                    mm(bank(4 * b + 2, 0, 3 * D), ht[:, b], fqkv[:]).then_inc(qkv_ps, 1)

                def mask_rows(b, cs):
                    n = B * f + b + 1
                    pe.wait_ge(clamp_ready, n)
                    for c in cs:
                        for k in range(MB + 1):
                            last = mm(bank(4 * b + c // 4, 128 * (c % 4), 128 * (c % 4) + 128),
                                      masks[:, b, k, 128 * c:128 * c + 128], slots_t[:, b, k if k < MB else NB],
                                      start=(k == 0), stop=(k == MB))
                    if MB in cs:
                        last.then_inc(u_ps, 1)

                if f == 0:
                    pe.wait_ge(consts_ready, 1)
                def slots_turned(b):
                    if b:
                        pe.wait_ge(slots_ready, B * f + b)
                    else:
                        pe.wait_ge(ktm_ready_a, f + 1)
                        pe.wait_ge(msel_ready_v, f + 1)
                    for k in range(NB):
                        last = M.transpose(bank(3 + k // 4 * 4, 128 * (k % 4), 128 * (k % 4) + 128), slots_t[:, b, k], ident[:])
                    last.then_inc(slots_ps, 1)

                ranks(0, range(NB))
                ranks(1, range(2))
                if f == 0:
                    pe.wait_ge(loaded_f, 16 * 8)
                gather(0)
                if f == 0:
                    pe.wait_ge(mask_wide, B)
                mask_rows(0, range(1))
                ranks(1, range(2, NB))
                mask_rows(0, range(1, 3))
                normed_t(0, 0)
                gather(1)
                qkv(0)
                mask_rows(0, range(3, MB + 1))
                def mask_columns(b):
                    n = B * f + b + 1
                    pe.wait_ge((u_ready, u_ready_v)[b], f + 1)
                    pe.wait_ge(xs_ready, n)
                    for k in range(MB + 1):
                        last = mm(bank(4 * b + 3, 0, D), umask[:, b, k], slots_t[:, b, k if k < MB else NB],
                                  start=(k == 0), stop=(k == MB))
                    last.then_inc(msel_ps, 1)

                def turned(b):
                    n = B * f + b + 1
                    pe.wait_ge(qk_ready, n)
                    pe.wait_ge(vs_ready, n)
                    M.transpose(bank(4 * b + 2, 0, D), qk[:, b, 0:D], ident[:])
                    M.transpose(bank(4 * b + 2, D, 2 * D), qk[:, b, D:2 * D], ident[:]).then_inc(qkt_ps, 1)

                def k_again():
                    pe.wait_ge(msel_ready, f + 1)
                    M.transpose(bank(3, D, 2 * D), qk[:, 0, D:2 * D], ident[:]).then_inc(k_again_ps, 1)

                def scores(b, half):
                    if half == 0:
                        pe.wait_ge(qkt_ready, B * f + b + 1)
                        pe.wait_ge(u_ready, f + 1)
                    else:
                        pe.wait_ge((ktm_ready_a, ktm_ready_v)[b], f + 1)
                        pe.wait_ge(u_ready_v, f + 1)
                    if b:
                        pe.wait_ge(sc_taken, 2 * B * f + half + 1)
                    for q in range(2):
                        h = 8 * half + 4 * q
                        last = mm(bank(4 * half + q), qt[:, b], ktm[:, b, h:h + 4].rearrange("p h k -> p (h k)"))
                    last.then_inc(sc_ps, 1)

                normed_t(0, 1)
                turned(0)
                mask_rows(1, range(1))
                qkv(1)
                mask_columns(0)
                scores(0, 0)
                k_again()
                mask_rows(1, range(1, 2))
                turned(1)
                mask_rows(1, range(2, MB + 1))
                scores(0, 1)
                mask_columns(1)
                scores(1, 0)
                scores(1, 1)
                slots_turned(0)
                slots_turned(1)

                def prob_turned(b, half):
                    if (b, half) == (B - 1, 1):
                        pe.wait_ge(last_norm_ready, 2 * f + 1)
                    else:
                        pe.wait_ge(norm_ready, (2 * B - 1) * f + 2 * b + half + 1)
                    if b:
                        pe.wait_ge(pt_ready_v, 2 * f + half + 1)
                    else:
                        pe.wait_ge(sc_taken, 2 * (B * f + 1) + half + 1)
                    for q in range(8):
                        if (b, half, q) == (B - 1, 1, 4):
                            pe.wait_ge(last_norm_ready, 2 * f + 2)
                        last = M.transpose(psum[0:KEEP, 4 * half + q // 4, 128 * (q % 4):128 * (q % 4) + 128],
                                           prob[:, b, 8 * half + q, 0:KEEP], ident[:])
                        if (b, half, q) == (B - 1, 1, 3):
                            last.then_inc(pt_ps, 1)
                    last.then_inc(pt_last_ps if (b, half) == (B - 1, 1) else pt_ps, 1)

                def outputs(b):
                    pe.wait_ge((pt_ready_v, pt_ready_a)[b], 2 * (f + 1))
                    for h in range(H):
                        j = h % HG
                        if (b, h) == (B - 1, H - HG):
                            pe.wait_ge(pt_last_ready, f + 1)
                        last = mm(psum[32 * j:32 * j + 32, 4 * b + 2, 128 * (h // HG):128 * (h // HG) + 128],
                                  vs[0:KEEP, b, h], ktm[0:KEEP, b, h])
                    last.then_inc(o_ps, 1)

                def project(b):
                    pe.wait_ge(ot_ready, B * f + b + 1)
                    pe.wait_ge(slots_ready, B * (f + 1))
                    for g in range(GB):
                        last = mm(bank(4 * b + 3, 0, D), ot[:, b, 128 * g:128 * g + 128], fwo[:, g], start=(g == 0), stop=(g == GB - 1))
                    last.then_inc(x1_ps, 1)

                def hidden(b):
                    pe.wait_ge(ht_ready, 2 * B * f + B + b + 1)
                    for k in range(FB):
                        last = mm(bank(4 * b, 128 * k, 128 * k + 128), fw1[:, 128 * k:128 * k + 128], ht[:, b])
                    last.then_inc(hid_ps, 1)

                prob_turned(0, 0)
                prob_turned(0, 1)
                prob_turned(1, 0)
                outputs(0)
                prob_turned(1, 1)
                project(0)
                outputs(1)
                normed_t(1, 0)
                project(1)
                hidden(0)
                normed_t(1, 1)
                hidden(1)
                for b in range(B):
                    pe.wait_ge(gel_ready, B * f + b + 1)
                    for k in range(FB):
                        last = mm(bank(4 * b + 3, 0, D), gel[:, b, 128 * k:128 * k + 128], fw2[:, k], start=(k == 0), stop=(k == FB - 1))
                    last.then_inc(x2_ps, 1)
                for b in range(B):
                    n = B * f + b + 1
                    pe.wait_ge(proc_ready, n)
                    pe.wait_ge(slots_ready, n)
                    for k in range(NB):
                        last = mm(bank(4 * b + k // 4, 128 * (k % 4), 128 * (k % 4) + 128),
                                  slots[0:KEEP, b, 128 * k:128 * k + 128], proc[0:KEEP, b])
                        if k % 4 == 3:
                            last.then_inc(y_ps, 1)

            pe.wait_ge(ident_ready, 1)
            ffn(0)
            pe.wait_ge(loaded_a, 16 * 7)

            for b in range(B):
                pe.wait_ge(xn_att_ready, b + 1)
                if b == 0:
                    pe.wait_ge(y_ready, B)
                for k in range(NB):
                    last = M.transpose(bank(4 + 2 * b + k // 4, 128 * (k % 4), 128 * (k % 4) + 128), xn[:, b * NB + k, 0:D], ident[:])
                last.then_inc(xnt_ps, 1)

            def project(n):
                b, which = divmod(n, 2)
                for w in range(2):
                    if n == 2:
                        pe.wait_ge((two_taken, turned_taken)[w], n)
                    elif n == 3:
                        pe.wait_ge(v_ready, 1)
                    for h in range(2):
                        last = mm(bank(PROJ_BANK[n] + 2 * w + h), wqk[:, 2 * which + w], xnt[:, b, 512 * h:512 * h + 512])
                    last.then_inc(proj_ps, 1)

            def project_v(b):
                for k in range(NB):
                    last = mm(bank(V_BANK[b] + k // 4, 128 * (k % 4), 128 * (k % 4) + 128), xnt[:, b, 128 * k:128 * k + 128], wv[:])
                last.then_inc(v_ps, 1)

            pe.wait_ge(xnt_ready, 1)
            project(0)
            pe.wait_ge(xnt_ready, 2)
            project(1)
            pe.wait_ge(two_taken, 1)
            project_v(0)
            project(2)
            project(3)
            pe.wait_ge(two_taken, 3)
            project_v(1)

            def score_tile(g, s, a, first=False):
                j, (i, first_bank, lag) = head_and_tile(a, first)
                if a == 0:
                    pe.wait_ge(set_loaded[s], (g // SETS + 1) * LOADS if isinstance(g, int) else turn(g, s) * LOADS)
                before = max(a - lag + 1, 0)
                if a == 0 and not first:
                    pe.wait_ge(tile_taken, g * USES - 2)
                elif not (first and before == 0):
                    pe.wait_ge(tile_taken, g * USES + before)
                n = 128 * (i + 1)
                for lo in range(0, n, 512):
                    hi = min(n, lo + 512)
                    last = mm(bank(first_bank + lo // 512, 0, hi - lo), q_set[0:SHIFT, s, j, 128 * i:128 * i + 128],
                              k_set[0:SHIFT, s, j, lo:hi])
                last.then_inc(tile_ps, 1)

            def transpose_max(g):
                pe.wait_ge(tile_taken, g * USES + TILES)
                M.transpose(psum[0:TILES, MAX_BANK, 0:128], mx[:, 0:TILES], ident[:]).then_inc(tile_ps, 1)

            def score_chunk(g, s, c, j, first=False):
                if c == 0 and j == 0:
                    pe.wait_ge(shift_loaded[s], (g // SETS + 1) * SHIFTS if isinstance(g, int) else turn(g, s) * SHIFTS)
                if not (first and c == 0 and j < 2):
                    pe.wait_ge(exp_done, g * (NC * HG) + (HG * c + j - 1))
                at = 0
                for kb, q0, w in CHUNKS[c]:
                    last = mm(bank(4 + j % 2, at, at + w), k_set[:, s, j, 128 * kb:128 * kb + 128], q_set[:, s, j, q0:q0 + w])
                    at += w
                last.then_inc(st_ps, 1)

            def values(g, s, c, part_of):
                if part_of == 0:
                    if c == 0:
                        pe.wait_ge(v_set_ready, g + 1)
                    if c < 2:
                        pe.wait_ge(pv_free[c], g + 1)
                    if DIAG[c]:
                        pe.wait_ge(diag_done, g * len(DIAG_CHUNKS) + (DIAG_CHUNKS.index(c) + 1))
                    else:
                        pe.wait_ge(exp_done, g * (NC * HG) + HG * (c + 1))
                at = 0
                for n, (kb, q0, w) in enumerate(CHUNKS[c]):
                    h = q0 // 512
                    lo, hi = max(at, 256 * part_of), min(at + w, 256 * part_of + 256)
                    if lo < hi:
                        q = q0 % 512 + lo - at
                        ends = c == HALF_END[h] and (hi == 512 or CHUNKS[c][n][1] // 512 != CHUNKS[c][-1][1] // 512)
                        for j in range(HG):
                            last = M.matmul(psum[32 * j:32 * j + 32, 6 + h, q:q + hi - lo], v_set[:, s, kb, j],
                                            p_buf[:, c % 3, j, lo:hi], start=(c == h and part_of == 0), stop=ends)
                        if ends and h == 0:
                            last.then_inc(half_done, 1)
                    at += w
                if part_of == 1:
                    last.then_inc(prob_free, 1)

            def outputs_t(g, h):
                pe.wait_ge(z_ready, g * 2 + h + 1)
                for k in range(4):
                    last = M.transpose(bank(6 + h, 128 * k, 128 * k + 128), z_buf[:, h, 128 * k:128 * k + 128], ident[:])
                last.then_inc(zt_ps, 1)

            pe.wait_ge(two_taken, 2 * B)
            pe.wait_ge(turned_taken, 2 * B)
            for a in range(TILES):
                if a == 1:
                    pe.wait_ge(v_ready, B)
                score_tile(0, 0, a, first=True)
            transpose_max(0)
            M.transpose(psum[0:TILES, 7, 0:128], ident[:, 0:TILES], ident[:]).then_inc(prob_free, 3)
            ahead = FIRST - 2 * HG
            for a in range(ahead):
                score_tile(1, 1, a)
            for n in range(2 * HG):
                score_tile(1, 1, ahead + n)
                score_chunk(0, 0, n // HG, n % HG, first=True)
            values(0, 0, 0, 0)

            def turn_out(b):
                pe.wait_ge(o_tok_ready, b + 1)
                for k in range(NB):
                    last = M.transpose(bank(4 * b + k // 4, 128 * (k % 4), 128 * (k % 4) + 128), o_tok[:, b, k], ident[:])
                last.then_inc(att_t_ps, 1)

            def project_out(b):
                pe.wait_ge(att_t_ready, b + 1)
                for k in range(NB):
                    last = mm(bank(4 * b + 2 + k // 4, 128 * (k % 4), 128 * (k % 4) + 128), o_turned[:, b, 128 * k:128 * k + 128], wo[:])
                    if k % 4 == 3:
                        last.then_inc(att_ps, 1)

            def body(g, s, has_next, has_second, has_first):
                for what, dg, n, *j in body_plan(has_next, has_second, has_first):
                    if what == "o_turn":
                        turn_out(0)
                    elif what == "o_proj":
                        project_out(0)
                    elif what == "tile":
                        score_tile(g + dg, (s + dg) % SETS, n)
                    elif what == "maxt":
                        transpose_max(g + dg)
                    elif what == "st":
                        score_chunk(g + dg, (s + dg) % SETS, n, j[0])
                    elif what == "pv":
                        values(g + dg, (s + dg) % SETS, n, j[0])
                    elif what == "zt":
                        outputs_t(g, n)

            turn = None
            with pe.Fori(0, (G - 2) // SETS) as i:
                for s in range(SETS):
                    def turn(gg, t, s=s, i=i):
                        return i + (1 if t >= s else 2)
                    body(i * SETS + s, s, True, True, True)
            body(G - 2, (G - 2) % SETS, True, True, False)
            body(G - 1, (G - 1) % SETS, False, False, False)

            ffn(1)


LOADS = 16 * 2 * PARTS
SHIFTS = 16 * PARTS


def kernel(**inputs):
    import concourse.bacc as bacc
    from concourse.bass_utils import run_bass_kernel_spmd

    a = {k: np.asarray(v) for k, v in inputs.items()}
    f32 = np.float32

    def turned(w, rotated):
        w = w.reshape(GB, HG, HD, -1)
        if rotated:
            w = np.roll(w, -HALF, axis=2)
        return w.transpose(0, 2, 1, 3).reshape(D, -1)

    wqk = np.stack([turned(a["L0_attn_" + n], r).T for n in ("Wq", "Wk") for r in (False, True)], axis=1)
    bqk = np.concatenate([turned(a["L0_attn_" + n], r) for n in ("bq", "bk") for r in (False, True)], axis=1)
    inv = (1.0 / (np.float32(10000.0) ** (np.arange(0, HD, 2, dtype=f32) / f32(HD)))).astype(f32)
    ang = (np.arange(T, dtype=f32)[:, None] * inv[None, :]).astype(f32)
    ang = np.concatenate([ang, ang], axis=1).astype(np.float64)
    sign = np.where(np.arange(HD) < HALF, -1.0, 1.0)
    rope = np.stack([np.cos(ang).T, (np.sin(ang) * sign).T]).astype(f32)
    rope = np.tile(np.repeat(rope, HG, axis=1), (1, GB, 1)).transpose(1, 0, 2)
    p = "L0_ffn_"
    fwo = np.zeros((HG, VW, GB, D), f32)
    fwo[:, :HD] = a[p + "wo"].reshape(GB, HG, HD, D).transpose(1, 2, 0, 3)
    fwo = fwo.reshape(HG * VW, GB, D)
    pos = a[p + "position_ids"][:B]
    pos = np.concatenate([pos.reshape(B, MB, 128), np.broadcast_to(pos[:, -1:, None], (B, 1, 128))], axis=1).transpose(2, 0, 1)
    sent = [
        ("x", a["L0_attn_x"]), ("masks", a[p + "attention_mask"]), ("pos", pos),
        ("rw", a[p + "router_w"]), ("rb", a[p + "router_b"]), ("fwq", a[p + "wq"]), ("fwk", a[p + "wk"]),
        ("fwv", a[p + "wv"]), ("fwo", fwo), ("fw1", a[p + "w1"]), ("fw2", a[p + "w2"]),
        ("ln1", a[p + "ln1"]), ("ln2", a[p + "ln2"]), ("wqk", wqk), ("bqk", bqk), ("wv", a["L0_attn_Wv"].T),
        ("bv", a["L0_attn_bv"]), ("wo", a["L0_attn_Wo"].T), ("bo", a["L0_attn_bo"]), ("rope", rope), ("invf", inv),
    ]
    nc = bacc.Bacc("TRN2", target_bir_lowering=False, num_devices=1)
    arrays, args = {}, []
    for name, value in sent:
        v = np.ascontiguousarray(value)
        arrays[f"in_{name}"] = v
        args.append(nc.dram_tensor(f"in_{name}", v.shape, mybir.dt.from_np(v.dtype), kind="ExternalInput").ap())
    args.append(nc.dram_tensor("out", (B, T, D), mybir.dt.float32, kind="ExternalOutput").ap())
    build(nc, *args)
    r = run_bass_kernel_spmd(nc, [arrays], core_ids=[0])
    return r.results[0]["out"]
```
